# Optimizing a Trainium2 kernel written in Bass

```python
import numpy as np
import jax
import jax.numpy as jnp

def _softmax(x, axis=-1):
    return jax.nn.softmax(x, axis=axis)

def _gelu(x):
    return jax.nn.gelu(x, approximate=True)

def _silu(x):
    return jax.nn.silu(x)

def _sigmoid(x):
    return jax.nn.sigmoid(x)

def _layernorm(x, axis=-1, eps=1e-05):
    m = jnp.mean(x, axis=axis, keepdims=True)
    v = jnp.var(x, axis=axis, keepdims=True)
    return (x - m) / jnp.sqrt(v + eps)

def _scatter_add(tgt, idx, src, axis=0):
    return tgt.at[idx].add(src)

def _segment_sum(src, seg, n):
    return jax.ops.segment_sum(src, seg, n)
kernel_name = 'mk_gnn_ffn_d2_gnn_r8_84eec6'

def setup_inputs(seed: int=0):
    np.random.seed(seed)
    _w = jnp.asarray

    def _rec_inputs():
        import jax
        import jax.numpy as jnp
        _gk = jax.random.key(seed)
        x = -0.0003713 + 1 * jax.random.normal(jax.random.fold_in(_gk, 1), (6250, 256), jnp.float32)
        src = jax.random.randint(jax.random.fold_in(_gk, 2), (100000,), 0, 6250, jnp.int32)
        dst = jnp.minimum((6250 * jax.random.uniform(jax.random.fold_in(_gk, 3), (100000,)) ** 2.0).astype(jnp.int32), 49999)
        _o = jnp.argsort(dst, stable=True)
        src = src[_o]
        dst = dst[_o]
        edge_attr_64 = -9.77346e-05 + 0.999888 * jax.random.normal(jax.random.fold_in(_gk, 12), (100000, 64), jnp.float32)
        return (x, src, dst, edge_attr_64)
    x, src, dst, edge_attr_64 = _rec_inputs()

    def _L0_gnn_setup():
        import jax, jax.numpy as jnp
        import numpy as np
        N = 6250
        E = 100000
        F = 256
        H = 256
        EPS = 1e-05

        def _gcn_norm(edge_index):
            loop = jnp.arange(N, dtype=edge_index.dtype)
            src = jnp.concatenate([edge_index[0], loop])
            dst = jnp.concatenate([edge_index[1], loop])
            deg = jax.ops.segment_sum(jnp.ones_like(dst, dtype=jnp.float32), dst, num_segments=N)
            dinv = deg ** (-0.5)
            norm = dinv[src] * dinv[dst]
            return (src, dst, norm)

        def _gcn_conv(h, W, b, src, dst, norm):
            h = h @ W
            msg = h[src] * norm[:, None]
            out = jax.ops.segment_sum(msg, dst, num_segments=N)
            return out + b

        def _bn(h, gamma, beta):
            m = jnp.mean(h, axis=0)
            v = jnp.var(h, axis=0)
            return (h - m) * jax.lax.rsqrt(v + EPS) * gamma + beta
        key = jax.random.key(seed)
        ks = jax.random.split(key, 16)
        x = jax.random.normal(ks[0], (N, F), dtype=jnp.float32)
        edge_index = jax.random.randint(ks[1], (2, E), 0, N, dtype=jnp.int32)

        def glorot(k, fan_in, fan_out):
            lim = float(np.sqrt(6.0 / (fan_in + fan_out)))
            return jax.random.uniform(k, (fan_in, fan_out), jnp.float32, -lim, lim)
        inp = {'x': x, 'edge_index': edge_index, 'W1': glorot(ks[2], F, H), 'b1': jnp.zeros((H,), jnp.float32), 'g1': jnp.ones((H,), jnp.float32), 'be1': jnp.zeros((H,), jnp.float32), 'W2': glorot(ks[3], H, H), 'b2': jnp.zeros((H,), jnp.float32), 'g2': jnp.ones((H,), jnp.float32), 'be2': jnp.zeros((H,), jnp.float32), 'W3': glorot(ks[4], H, H), 'b3': jnp.zeros((H,), jnp.float32), 'g3': jnp.ones((H,), jnp.float32), 'be3': jnp.zeros((H,), jnp.float32)}
        return inp
    _L0_gnn_all = _L0_gnn_setup()
    _L0_gnn_in = {k: v for k, v in _L0_gnn_all.items() if k in ('W1', 'b1', 'g1', 'be1', 'W2', 'b2', 'g2', 'be2', 'W3', 'b3', 'g3', 'be3')}
    del _L0_gnn_all

    def _L0_ffn_setup():
        import jax, jax.numpy as jnp
        import numpy as np
        TOP_K = 2
        LN_EPS = 1e-05
        key = jax.random.key(seed)
        ks = jax.random.split(key, 8)
        B, S, D, E, H = (16, 1024, 256, 8, 1024)
        x = jax.random.normal(ks[0], (B, S, D), dtype=jnp.float32)
        Wr = jax.random.normal(ks[1], (D, E), dtype=jnp.float32) * 0.1
        br = jnp.zeros((E,), dtype=jnp.float32)
        ln_g = jnp.ones((E, D), dtype=jnp.float32)
        ln_b = jnp.zeros((E, D), dtype=jnp.float32)
        W1 = jax.random.normal(ks[2], (E, D, H), dtype=jnp.float32) * (1.0 / np.sqrt(D))
        b1 = jnp.zeros((E, H), dtype=jnp.float32)
        W2 = jax.random.normal(ks[3], (E, H, D), dtype=jnp.float32) * (1.0 / np.sqrt(H))
        b2 = jnp.zeros((E, D), dtype=jnp.float32)
        return {'x': x, 'Wr': Wr, 'br': br, 'ln_g': ln_g, 'ln_b': ln_b, 'W1': W1, 'b1': b1, 'W2': W2, 'b2': b2}
    _L0_ffn_all = _L0_ffn_setup()
    _L0_ffn_in = {k: v for k, v in _L0_ffn_all.items() if k in ('Wr', 'br', 'ln_g', 'ln_b', 'W1', 'b1', 'W2', 'b2')}
    del _L0_ffn_all

    def _L1_gnn_setup():
        import jax, jax.numpy as jnp
        import numpy as np
        N_NODES = 6250
        N_EDGES = 100000
        IN_DIM = 256
        E_DIM = 64
        N_HEADS = 8
        OUT_DIM = 32
        NEG_SLOPE = 0.2
        key = jax.random.key(seed)
        ks = jax.random.split(key, 10)
        return {'feat': jax.random.normal(ks[0], (N_NODES, IN_DIM), dtype=jnp.float32), 'edge_attr': jax.random.normal(ks[1], (N_EDGES, E_DIM), dtype=jnp.float32), 'src': jax.random.randint(ks[2], (N_EDGES,), 0, N_NODES, dtype=jnp.int32), 'dst': jax.random.randint(ks[3], (N_EDGES,), 0, N_NODES, dtype=jnp.int32), 'W_fc': jax.random.normal(ks[4], (IN_DIM, N_HEADS * OUT_DIM), dtype=jnp.float32) * (1.0 / np.sqrt(IN_DIM)), 'W_e': jax.random.normal(ks[5], (E_DIM, N_HEADS * OUT_DIM), dtype=jnp.float32) * (1.0 / np.sqrt(E_DIM)), 'attn_h': jax.random.normal(ks[6], (N_HEADS, OUT_DIM), dtype=jnp.float32) * 0.1, 'attn_e': jax.random.normal(ks[7], (N_HEADS, OUT_DIM), dtype=jnp.float32) * 0.1, 'attn_t': jax.random.normal(ks[8], (N_HEADS, OUT_DIM), dtype=jnp.float32) * 0.1, 'bias': jnp.zeros((N_HEADS, OUT_DIM), dtype=jnp.float32)}
    _L1_gnn_all = _L1_gnn_setup()
    _L1_gnn_in = {k: v for k, v in _L1_gnn_all.items() if k in ('W_fc', 'W_e', 'attn_h', 'attn_e', 'attn_t', 'bias')}
    del _L1_gnn_all

    def _L1_ffn_setup():
        import jax, jax.numpy as jnp
        import numpy as np
        B, S, D = (8, 512, 256)
        H = 4 * D
        CAPACITY = 0.5
        key = jax.random.key(seed)
        ks = jax.random.split(key, 6)
        x = jax.random.normal(ks[0], (B, S, D), dtype=jnp.float32)
        attention_mask = jnp.zeros((B, 1, 1, S), dtype=jnp.float32)
        wr = jax.random.normal(ks[1], (D, 1), dtype=jnp.float32) * 0.02
        br = jnp.zeros((1,), dtype=jnp.float32)
        w1 = jax.random.normal(ks[2], (D, H), dtype=jnp.float32) * 0.02
        b1 = jnp.zeros((H,), dtype=jnp.float32)
        w2 = jax.random.normal(ks[3], (H, D), dtype=jnp.float32) * 0.02
        b2 = jnp.zeros((D,), dtype=jnp.float32)
        return {'x': x, 'attention_mask': attention_mask, 'wr': wr, 'br': br, 'w1': w1, 'b1': b1, 'w2': w2, 'b2': b2}
    _L1_ffn_all = _L1_ffn_setup()
    _L1_ffn_in = {k: v for k, v in _L1_ffn_all.items() if k in ('attention_mask', 'wr', 'br', 'w1', 'b1', 'w2', 'b2')}
    del _L1_ffn_all
    return {'x': x, 'src': src, 'dst': dst, 'edge_attr_64': edge_attr_64, 'L0_gnn_W1': _L0_gnn_in['W1'], 'L0_gnn_b1': _L0_gnn_in['b1'], 'L0_gnn_g1': _L0_gnn_in['g1'], 'L0_gnn_be1': _L0_gnn_in['be1'], 'L0_gnn_W2': _L0_gnn_in['W2'], 'L0_gnn_b2': _L0_gnn_in['b2'], 'L0_gnn_g2': _L0_gnn_in['g2'], 'L0_gnn_be2': _L0_gnn_in['be2'], 'L0_gnn_W3': _L0_gnn_in['W3'], 'L0_gnn_b3': _L0_gnn_in['b3'], 'L0_gnn_g3': _L0_gnn_in['g3'], 'L0_gnn_be3': _L0_gnn_in['be3'], 'L0_ffn_Wr': _L0_ffn_in['Wr'], 'L0_ffn_br': _L0_ffn_in['br'], 'L0_ffn_ln_g': _L0_ffn_in['ln_g'], 'L0_ffn_ln_b': _L0_ffn_in['ln_b'], 'L0_ffn_W1': _L0_ffn_in['W1'], 'L0_ffn_b1': _L0_ffn_in['b1'], 'L0_ffn_W2': _L0_ffn_in['W2'], 'L0_ffn_b2': _L0_ffn_in['b2'], 'L1_gnn_W_fc': _L1_gnn_in['W_fc'], 'L1_gnn_W_e': _L1_gnn_in['W_e'], 'L1_gnn_attn_h': _L1_gnn_in['attn_h'], 'L1_gnn_attn_e': _L1_gnn_in['attn_e'], 'L1_gnn_attn_t': _L1_gnn_in['attn_t'], 'L1_gnn_bias': _L1_gnn_in['bias'], 'L1_ffn_attention_mask': _L1_ffn_in['attention_mask'], 'L1_ffn_wr': _L1_ffn_in['wr'], 'L1_ffn_br': _L1_ffn_in['br'], 'L1_ffn_w1': _L1_ffn_in['w1'], 'L1_ffn_b1': _L1_ffn_in['b1'], 'L1_ffn_w2': _L1_ffn_in['w2'], 'L1_ffn_b2': _L1_ffn_in['b2']}

def reference(x, src, dst, edge_attr_64, L0_gnn_W1, L0_gnn_b1, L0_gnn_g1, L0_gnn_be1, L0_gnn_W2, L0_gnn_b2, L0_gnn_g2, L0_gnn_be2, L0_gnn_W3, L0_gnn_b3, L0_gnn_g3, L0_gnn_be3, L0_ffn_Wr, L0_ffn_br, L0_ffn_ln_g, L0_ffn_ln_b, L0_ffn_W1, L0_ffn_b1, L0_ffn_W2, L0_ffn_b2, L1_gnn_W_fc, L1_gnn_W_e, L1_gnn_attn_h, L1_gnn_attn_e, L1_gnn_attn_t, L1_gnn_bias, L1_ffn_attention_mask, L1_ffn_wr, L1_ffn_br, L1_ffn_w1, L1_ffn_b1, L1_ffn_w2, L1_ffn_b2):
    import jax
    import jax.numpy as jnp

    def _L0_gnn_ref(x, edge_index, W1, b1, g1, be1, W2, b2, g2, be2, W3, b3, g3, be3):
        import jax, jax.numpy as jnp
        import numpy as np
        N = 6250
        E = 100000
        F = 256
        H = 256
        EPS = 1e-05

        def _gcn_norm(edge_index):
            loop = jnp.arange(N, dtype=edge_index.dtype)
            src = jnp.concatenate([edge_index[0], loop])
            dst = jnp.concatenate([edge_index[1], loop])
            deg = jax.ops.segment_sum(jnp.ones_like(dst, dtype=jnp.float32), dst, num_segments=N)
            dinv = deg ** (-0.5)
            norm = dinv[src] * dinv[dst]
            return (src, dst, norm)

        def _gcn_conv(h, W, b, src, dst, norm):
            h = h @ W
            msg = h[src] * norm[:, None]
            out = jax.ops.segment_sum(msg, dst, num_segments=N)
            return out + b

        def _bn(h, gamma, beta):
            m = jnp.mean(h, axis=0)
            v = jnp.var(h, axis=0)
            return (h - m) * jax.lax.rsqrt(v + EPS) * gamma + beta
        src, dst, norm = _gcn_norm(edge_index)
        h = _bn(_gcn_conv(x, W1, b1, src, dst, norm), g1, be1)
        h = _bn(_gcn_conv(h, W2, b2, src, dst, norm), g2, be2)
        h = _bn(_gcn_conv(h, W3, b3, src, dst, norm), g3, be3)
        return h

    def _L0_ffn_ref(x, Wr, br, ln_g, ln_b, W1, b1, W2, b2):
        import jax, jax.numpy as jnp
        import numpy as np
        TOP_K = 2
        LN_EPS = 1e-05
        B, S, D = x.shape
        N = B * S
        xt = x.reshape(N, D)
        logits = xt @ Wr + br
        probs = jax.nn.softmax(logits, axis=-1)
        top_p, top_idx = jax.lax.top_k(probs, TOP_K)
        weights = top_p / top_p.sum(axis=-1, keepdims=True)
        mu = xt.mean(axis=-1, keepdims=True)
        var = ((xt - mu) ** 2).mean(axis=-1, keepdims=True)
        xn = (xt - mu) * jax.lax.rsqrt(var + LN_EPS)
        xe = xn[None, :, :] * ln_g[:, None, :] + ln_b[:, None, :]
        h = jax.nn.gelu(jnp.einsum('end,edh->enh', xe, W1) + b1[:, None, :], approximate=False)
        y = jnp.einsum('enh,ehd->end', h, W2) + b2[:, None, :]
        y_tok = jnp.transpose(y, (1, 0, 2))
        sel = jnp.take_along_axis(y_tok, top_idx[:, :, None], axis=1)
        out = (weights[:, :, None] * sel).sum(axis=1)
        return out.reshape(B, S, D)

    def _L1_gnn_ref(feat, edge_attr, src, dst, W_fc, W_e, attn_h, attn_e, attn_t, bias):
        import jax, jax.numpy as jnp
        import numpy as np
        N_NODES = 6250
        N_EDGES = 100000
        IN_DIM = 256
        E_DIM = 64
        N_HEADS = 8
        OUT_DIM = 32
        NEG_SLOPE = 0.2
        N = feat.shape[0]
        H, D = attn_h.shape
        ft = (feat @ W_fc).reshape(N, H, D)
        eh = jnp.einsum('nhd,hd->nh', ft, attn_h)
        et = jnp.einsum('nhd,hd->nh', ft, attn_t)
        fe = (edge_attr @ W_e).reshape(-1, H, D)
        ee = jnp.einsum('ehd,hd->eh', fe, attn_e)
        e = jax.nn.leaky_relu(eh[src] + ee + et[dst], negative_slope=NEG_SLOPE)
        e_max = jax.ops.segment_max(e, dst, num_segments=N)
        e_max = jax.lax.stop_gradient(jnp.where(jnp.isfinite(e_max), e_max, 0.0))
        ex = jnp.exp(e - e_max[dst])
        denom = jax.ops.segment_sum(ex, dst, num_segments=N)
        a = ex / denom[dst]
        msg = ft[src] * a[:, :, None]
        rst = jax.ops.segment_sum(msg, dst, num_segments=N)
        rst = rst + bias[None, :, :]
        return rst.reshape(N, H * D)

    def _L1_ffn_ref(x, attention_mask, wr, br, w1, b1, w2, b2):
        import jax, jax.numpy as jnp
        import numpy as np
        B, S, D = (8, 512, 256)
        H = 4 * D
        CAPACITY = 0.5
        b, s, d = x.shape
        weights = (jnp.einsum('bsd,do->bso', x, wr) + br)[..., 0]
        k = max(1, int(CAPACITY * s))
        kk = k - 1 if k > 1 else 1
        _, idx = jax.lax.top_k(weights, k)
        sel_idx = idx[:, :kk]
        sel = jnp.take_along_axis(x, sel_idx[:, :, None], axis=1)
        h = jax.nn.gelu(jnp.einsum('bkd,dh->bkh', sel, w1) + b1)
        y = jnp.einsum('bkh,hd->bkd', h, w2) + b2
        w_sel = jnp.take_along_axis(weights, sel_idx, axis=1)
        y = y * w_sel[..., None]
        batch_idx = jnp.arange(b)[:, None]
        processed = jnp.zeros_like(x).at[batch_idx, sel_idx].set(y)
        return processed + x
    edge_index = jnp.stack([src, dst])
    x = x + _L0_gnn_ref(_layernorm(x, axis=-1), edge_index, L0_gnn_W1, L0_gnn_b1, L0_gnn_g1, L0_gnn_be1, L0_gnn_W2, L0_gnn_b2, L0_gnn_g2, L0_gnn_be2, L0_gnn_W3, L0_gnn_b3, L0_gnn_g3, L0_gnn_be3)
    x = x + _L0_ffn_ref(_layernorm(x, axis=-1)[None], L0_ffn_Wr, L0_ffn_br, L0_ffn_ln_g, L0_ffn_ln_b, L0_ffn_W1, L0_ffn_b1, L0_ffn_W2, L0_ffn_b2)[0]
    x = x + _L1_gnn_ref(_layernorm(x, axis=-1), edge_attr_64, src, dst, L1_gnn_W_fc, L1_gnn_W_e, L1_gnn_attn_h, L1_gnn_attn_e, L1_gnn_attn_t, L1_gnn_bias)
    x = x + _L1_ffn_ref(_layernorm(x, axis=-1)[None], L1_ffn_attention_mask, L1_ffn_wr, L1_ffn_br, L1_ffn_w1, L1_ffn_b1, L1_ffn_w2, L1_ffn_b2)[0]
    return x

_drawn_inputs = setup_inputs


def setup_inputs(seed=0):
    import zlib

    import numpy as np

    out = dict(_drawn_inputs(seed))
    spreads = {'L0_gnn_b1': (0.0, 0.8),
     'L0_gnn_g1': (1.0, 0.2),
     'L0_gnn_be1': (0.0, 0.1),
     'L0_gnn_b2': (0.0, 0.8),
     'L0_gnn_g2': (1.0, 0.2),
     'L0_gnn_be2': (0.0, 0.1),
     'L0_gnn_b3': (0.0, 0.8),
     'L0_gnn_g3': (1.0, 0.2),
     'L0_gnn_be3': (0.0, 0.1),
     'L0_ffn_br': (0.0, 0.1),
     'L0_ffn_ln_g': (1.0, 0.2),
     'L0_ffn_ln_b': (0.0, 0.1),
     'L0_ffn_b1': (0.0, 0.1),
     'L0_ffn_b2': (0.0, 0.1),
     'L1_gnn_bias': (0.0, 0.1),
     'L1_ffn_b1': (0.0, 0.8),
     'L1_ffn_b2': (0.0, 0.8)}
    factors = {'L1_ffn_wr': 4.736, 'L1_ffn_w1': 6.069, 'L1_ffn_w2': 5.614}
    for name, (base, spread) in spreads.items():
        noise = np.random.default_rng([zlib.crc32(name.encode()), seed]).standard_normal(out[name].shape)
        drawn = base * np.exp(spread * noise) if base else spread * noise
        out[name] = jnp.asarray(drawn.astype(out[name].dtype))
    for name, factor in factors.items():
        out[name] = (out[name] * factor).astype(out[name].dtype)
    return out
```

```python
from contextlib import ExitStack

import concourse.bass as bass
from concourse import mybir
import numpy as np

F32 = mybir.dt.float32
BF16 = mybir.dt.bfloat16
I32 = mybir.dt.int32
ALU = mybir.AluOpType
ACT = mybir.ActivationFunctionType
AX = mybir.AxisListType

P = 128
N = 6250
E = 100000
F = 256
FC = F // P
NT = -(-N // P)
NPAD = NT * P
NLAST = N - (NT - 1) * P
ET = -(-E // P)
ETB = -(-ET // P)
G = 8
ITERS = -(-(ET + NT - 1) // (2 * G))
NPAIR = ITERS * 2 * G
PCOL = ETB * P
NODST = 1 << 20
BIG = 1.0e30
EPS = 1e-5
HEADS = 8
HD = F // HEADS
EDIM = 64
EXPERTS = 8
HID = 1024
HC = HID // P
SLOPE = 0.2


class Sem:

    def __init__(self, handle):
        self.h, self.base = handle, 0

    def next(self):
        self.base += 1
        return self.base


def node_tiles(eng):
    with eng.Fori(0, NT // 2) as i:
        yield 2 * i, 0
        yield 2 * i + 1, 1
    for d in range(NT // 2 * 2, NT):
        yield d, d % 2


def two_ahead(eng, early, late):
    early(0, 0)
    early(1, 1)
    loops = (NT - 2) // 2
    for k in range(2):
        early(2 + k, k)
        late(k, k)
    with eng.Fori(1, loops) as i:
        for k in range(2):
            early(2 * i + 2 + k, k)
            late(2 * i + k, k)
    for d in range(2 * loops, NT):
        if d + 2 < NT:
            early(d + 2, d % 2)
        late(d, d % 2)


def node_tiles_apart(eng):
    yield 0, 0
    yield 1, 1
    with eng.Fori(1, NT // 2) as i:
        yield 2 * i, 0
        yield 2 * i + 1, 1
    for d in range(NT // 2 * 2, NT):
        yield d, d % 2


def wait_earlier(eng, sem, d, k, each):
    if not isinstance(d, int):
        eng.wait_ge(sem.h, sem.base + (d - k) * (each // 2))
    elif d >= 2:
        eng.wait_ge(sem.h, sem.base + d // 2 * each)


def build(nc, t, out):
    with ExitStack() as top:
        _build(nc, t, out, top)


def _build(nc, t, out, top):
    uses = {}

    def sb(name, shape, dt=F32, ctx=top):
        uses[name] = uses.get(name, 0) + 1
        return ctx.enter_context(nc.sbuf_tensor(f"{name}_{uses[name]}", shape, dt))

    def sem(name):
        return Sem(top.enter_context(nc.semaphore(name)))

    def dram(name, shape, dt=F32):
        return nc.dram_tensor(name, shape, dt, kind="Internal").ap()

    ps = [top.enter_context(nc.psum_tensor(f"ps{i}", [P, 512], F32)) for i in range(8)]

    ident = sb("ident", [P, P])
    iota_f = sb("iota_f", [P, P])
    ones = sb("ones", [P, P])
    excl = sb("excl", [P, P])
    psrc = sb("psrc", [P, PCOL], I32)
    pdl = sb("pdl", [P, PCOL])
    plast = sb("plast", [P, PCOL])
    first = sb("first", [P, ETB, P])
    prow = sb("prow", [2, PCOL], I32)
    dinv = sb("dinv", [P, NT])
    idx = sb("idx", [P, 2, G], I32)
    carrier = sb("carrier", [P, 1], I32)

    MT = -(-(2 * N) // P) + EXPERTS
    MT += MT % 2
    CAP = MT * P
    slot_rows = dram("slot_rows", [CAP + 2 * P, F])
    slot_out = dram("slot_out", [CAP + 2 * P, F])
    resid = dram("resid", [NPAD, F])
    slots = sb("slots", [P, 2, NT], I32)
    gate = sb("gate", [P, 2, NT], F32)
    tile_expert = sb("tile_expert", [P, MT], F32)
    tile_expert_i = sb("tile_expert_i", [1, MT], I32)

    edge_table = dram("edge_table", [PCOL, 2 * P + 1])
    node_table = dram("node_table", [NPAD, F])

    v_step = sem("v_step")
    row_sem = [sem(f"row_landed{s}") for s in range(2 * G)]
    idx_ready = sem("idx_ready")
    onehot_ready, aggregated, added = sem("onehot_ready"), sem("aggregated"), sem("added")
    loaded, stored, x_loaded = sem("loaded"), sem("stored"), sem("x_loaded")
    turned, turned_out = sem("turned"), sem("turned_out")
    projected, projected_out = sem("projected"), sem("projected_out")
    credit = {aggregated: 2 * G, added: G, turned: 2, turned_out: 2, projected: 2, projected_out: 2}

    root_ready, root_done = sem("root_ready"), sem("root_done")
    roots = [0]

    class Rsqrt:

        def __init__(self, var, res, tmp):
            self.var, self.res, self.tmp, self.n = var, res, tmp, roots[0] + 1
            roots[0] += 1

        def scalar(self, a):
            a.wait_ge(root_ready.h, self.n)
            a.activation(self.res, self.var, ACT.Sqrt).then_inc(root_done.h, 1)

        def vector(self, v):
            var, res, tmp = self.var, self.res, self.tmp
            v.nop().then_inc(root_ready.h, 1)
            v.wait_ge(root_done.h, self.n)
            v.reciprocal(tmp, res).then_inc(v_step.h, 1)
            v.wait_ge(v_step.h, v_step.next())
            v.tensor_tensor(res, tmp, tmp, ALU.mult).then_inc(v_step.h, 1)
            v.wait_ge(v_step.h, v_step.next())
            v.tensor_tensor(res, res, var, ALU.mult).then_inc(v_step.h, 1)
            v.wait_ge(v_step.h, v_step.next())
            v.tensor_scalar(res, res, -0.5, 1.5, ALU.mult, ALU.add).then_inc(v_step.h, 1)
            v.wait_ge(v_step.h, v_step.next())
            v.tensor_tensor(res, res, tmp, ALU.mult).then_inc(v_step.h, 1)
            v.wait_ge(v_step.h, v_step.next())

    def rows_of(big, d):
        return big[:, bass.ds(d, 1), :].rearrange("p a f -> p (a f)")

    def edge_tables():
        with ExitStack() as ctx:
            iota_i = sb("iota_i", [P, P], I32, ctx)
            col_i = sb("col_i", [P, 1], I32, ctx)
            pv_i = sb("pv_i", [P, ETB], I32, ctx)
            col_f = sb("col_f", [P, 1], F32, ctx)
            pv = sb("pv", [P, ETB], F32, ctx)
            incl = sb("incl", [P, P], F32, ctx)
            edges_i = sb("edges_i", [P, ETB, 2, P], I32, ctx)
            edges_f = sb("edges_f", [P, ETB, 2 * P + 1], F32, ctx)
            tmp = sb("tmp", [P, ETB, P], F32, ctx)
            mm = sb("mm", [P, 2, ETB], F32, ctx)
            mm_i = sb("mm_i", [P, 2, ETB], I32, ctx)
            small = sb("small", [P, 8, ETB], F32, ctx)
            cumrow = sb("cumrow", [P, PCOL], F32, ctx)
            junk = sb("junk", [P, PCOL], F32, ctx)
            tile_of = sb("tile_of", [P, ETB], F32, ctx)
            tile_i = sb("tile_i", [P, ETB], I32, ctx)
            pair_edges = sb("pair_edges", [P, ETB, 2 * P + 1], F32, ctx)
            pair_dst = sb("pair_dst", [P, ETB, P], F32, ctx)
            lastf = sb("lastf", [P, ETB, P], F32, ctx)
            drow = sb("drow", [P, ETB, 2], F32, ctx)
            consts, padded, edges_in = sem("consts"), sem("padded"), sem("edges_in")
            counted, scanned, spread, spread_done = sem("counted"), sem("scanned"), sem("spread"), sem("spread_done")
            table_ready, tiles_found, pairs_in = sem("table_ready"), sem("tiles_found"), sem("pairs_in")
            pairs_ready, pairs_turned = sem("pairs_ready"), sem("pairs_turned")
            full = (ETB - 1) * P * P
            lastb = ETB - 1
            rows = (E - full) // P
            rest = E - full - rows * P

            block = nc.Block()
            with block as block:
                @block.gpsimd
                def _(g):
                    g.iota(iota_i[:], [[1, P]], base=0, channel_multiplier=0).then_inc(consts.h, 1)
                    g.iota(col_i[:], [[0, 1]], base=0, channel_multiplier=1).then_inc(consts.h, 1)
                    g.iota(pv_i[:], [[P, ETB]], base=0, channel_multiplier=1).then_inc(consts.h, 1)
                    g.memset(edges_i[:, lastb, 0, :], 0).then_inc(padded.h, 1)
                    g.memset(edges_i[:, lastb, 1, :], NODST).then_inc(padded.h, 1)
                    g.memset(ones[:], 1.0).then_inc(consts.h, 1)
                    g.wait_ge(tiles_found.h, 1)
                    g.wait_ge(stored.h, stored.base + 16)
                    for b in range(ETB):
                        g.indirect_dma_start(pair_edges[:, b, :], None, edge_table,
                                             bass.IndirectOffsetOnAxis(ap=tile_i[:, b:b + 1], axis=0)).then_inc(pairs_in.h, 16)

                @block.sync
                def _(sp):
                    sp.wait_ge(padded.h, 2)
                    for k, a in enumerate((t["src"], t["dst"])):
                        sp.dma_start(edges_i[:, 0:lastb, k, :], a[0:full].rearrange("(b p l) -> p b l", p=P, l=P)).then_inc(edges_in.h, 16)
                        sp.dma_start(edges_i[0:rows, lastb, k, :], a[full:full + rows * P].rearrange("(p l) -> p l", l=P)).then_inc(edges_in.h, 16)
                        sp.dma_start(edges_i[rows:rows + 1, lastb, k, P - rest:P], a[E - rest:E].rearrange("(p l) -> p l", p=1)).then_inc(edges_in.h, 16)
                    sp.wait_ge(table_ready.h, 1)
                    sp.dma_start(edge_table.rearrange("(b p) c -> p b c", p=P), edges_f[:]).then_inc(stored.h, 16)

                @block.vector
                def _(v):
                    for s, n in credit.items():
                        v.sem_inc(s.h, n)
                    v.wait_ge(consts.h, 4)
                    v.tensor_copy(iota_f[:], iota_i[:]).then_inc(v_step.h, 1)
                    v.wait_ge(v_step.h, v_step.next())
                    v.tensor_copy(col_f[:], col_i[:]).then_inc(v_step.h, 1)
                    v.wait_ge(v_step.h, v_step.next())
                    v.tensor_copy(pv[:], pv_i[:]).then_inc(v_step.h, 1)
                    v.wait_ge(v_step.h, v_step.next())
                    v.tensor_scalar(ident[:], iota_f[:], col_f[:], None, ALU.is_equal).then_inc(v_step.h, 1)
                    v.wait_ge(v_step.h, v_step.next())
                    v.tensor_scalar(excl[:], iota_f[:], col_f[:], None, ALU.is_gt).then_inc(v_step.h, 1)
                    v.wait_ge(v_step.h, v_step.next())
                    v.tensor_scalar(incl[:], iota_f[:], col_f[:], None, ALU.is_ge).then_inc(v_step.h, 1)
                    v.wait_ge(v_step.h, v_step.next())
                    v.wait_ge(edges_in.h, 6 * 16)
                    v.tensor_copy(edges_f[:, :, 0:2 * P], edges_i[:].rearrange("p b k l -> p b (k l)")).then_inc(v_step.h, 1)
                    v.wait_ge(v_step.h, v_step.next())
                    dst = edges_f[:, :, P:2 * P]
                    v.scalar_tensor_tensor(tmp[:], dst, float(NODST // 2), dst, ALU.is_lt, ALU.mult).then_inc(v_step.h, 1)
                    v.wait_ge(v_step.h, v_step.next())
                    v.tensor_reduce(mm[:, 0, :], dst, AX.X, ALU.min).then_inc(v_step.h, 1)
                    v.wait_ge(v_step.h, v_step.next())
                    v.tensor_reduce(mm[:, 1, :], tmp[:], AX.X, ALU.max).then_inc(v_step.h, 1)
                    v.wait_ge(v_step.h, v_step.next())
                    valid, cnt, tot, cum, off = (small[:, k, :] for k in range(5))
                    v.tensor_scalar(valid, mm[:, 0, :], float(NODST // 2), None, ALU.is_lt).then_inc(v_step.h, 1)
                    v.wait_ge(v_step.h, v_step.next())
                    v.tensor_copy(mm_i[:], mm[:]).then_inc(v_step.h, 1)
                    v.wait_ge(v_step.h, v_step.next())
                    v.tensor_scalar(mm_i[:], mm_i[:], 7, None, ALU.arith_shift_right).then_inc(v_step.h, 1)
                    v.wait_ge(v_step.h, v_step.next())
                    v.tensor_copy(mm[:], mm_i[:]).then_inc(v_step.h, 1)
                    v.wait_ge(v_step.h, v_step.next())
                    v.tensor_tensor(cnt, mm[:, 1, :], mm[:, 0, :], ALU.subtract).then_inc(v_step.h, 1)
                    v.wait_ge(v_step.h, v_step.next())
                    v.scalar_tensor_tensor(cnt, cnt, 1.0, valid, ALU.add, ALU.mult).then_inc(v_step.h, 1)
                    v.wait_ge(v_step.h, v_step.next())
                    v.nop().then_inc(counted.h, 1)
                    v.wait_ge(scanned.h, 1)
                    v.tensor_copy(tot, ps[0][:, 16:16 + ETB]).then_inc(v_step.h, 1)
                    v.wait_ge(v_step.h, v_step.next())
                    v.tensor_tensor_scan(cum, ones[:, 0:ETB], tot, 0.0, ALU.mult, ALU.add).then_inc(v_step.h, 1)
                    v.wait_ge(v_step.h, v_step.next())
                    v.tensor_tensor(cum, cum, ps[0][:, 0:ETB], ALU.add).then_inc(v_step.h, 1)
                    v.wait_ge(v_step.h, v_step.next())
                    v.tensor_tensor(cum, cum, tot, ALU.subtract).then_inc(v_step.h, 1)
                    v.wait_ge(v_step.h, v_step.next())
                    v.tensor_tensor(off, cum, cnt, ALU.subtract).then_inc(v_step.h, 1)
                    v.wait_ge(v_step.h, v_step.next())
                    v.tensor_tensor(off, mm[:, 0, :], off, ALU.subtract).then_inc(v_step.h, 1)
                    v.wait_ge(v_step.h, v_step.next())
                    v.tensor_tensor(edges_f[:, :, 2 * P], off, valid, ALU.mult).then_inc(v_step.h, 1)
                    v.wait_ge(v_step.h, v_step.next())
                    v.nop().then_inc(table_ready.h, 1)
                    v.tensor_tensor(tmp[:], ident[:].rearrange("p (b l) -> p b l", b=1).to_broadcast([P, ETB, P]),
                                    cum.rearrange("p (b l) -> p b l", l=1).to_broadcast([P, ETB, P]), ALU.mult).then_inc(v_step.h, 1)
                    v.wait_ge(v_step.h, v_step.next())
                    v.nop().then_inc(spread.h, 1)
                    v.wait_ge(spread_done.h, 1)
                    v.tensor_copy(cumrow[:, 0:512], ps[1][:]).then_inc(v_step.h, 1)
                    v.wait_ge(v_step.h, v_step.next())
                    v.tensor_copy(cumrow[:, 512:PCOL], ps[2][:, 0:PCOL - 512]).then_inc(v_step.h, 1)
                    v.wait_ge(v_step.h, v_step.next())
                    for b in range(ETB):
                        v.tensor_scalar(junk[:], cumrow[:], pv[:, b:b + 1], 0.0, ALU.is_le, ALU.add, accum_out=tile_of[:, b:b + 1]).then_inc(v_step.h, 1)
                        v.wait_ge(v_step.h, v_step.next())
                    v.tensor_scalar(tile_of[:], tile_of[:], float(PCOL - 1), None, ALU.min).then_inc(v_step.h, 1)
                    v.wait_ge(v_step.h, v_step.next())
                    v.tensor_copy(tile_i[:], tile_of[:]).then_inc(v_step.h, 1)
                    v.wait_ge(v_step.h, v_step.next())
                    v.nop().then_inc(tiles_found.h, 1)
                    v.wait_ge(pairs_in.h, 16 * ETB)
                    dp = drow[:, :, 0]
                    v.tensor_tensor(dp, pv[:], pair_edges[:, :, 2 * P], ALU.add).then_inc(v_step.h, 1)
                    v.wait_ge(v_step.h, v_step.next())
                    v.tensor_scalar(dp, dp, float(NT - 1), 0.0, ALU.min, ALU.max).then_inc(v_step.h, 1)
                    v.wait_ge(v_step.h, v_step.next())
                    v.tensor_scalar(small[:, 5, :], dp, float(P), None, ALU.mult).then_inc(v_step.h, 1)
                    v.wait_ge(v_step.h, v_step.next())
                    v.tensor_scalar(drow[:, :, 1], tile_of[:], float(P), float(E - P), ALU.mult, ALU.min).then_inc(v_step.h, 1)
                    v.wait_ge(v_step.h, v_step.next())
                    v.tensor_tensor(pair_dst[:], pair_edges[:, :, P:2 * P],
                                    small[:, 5, :].rearrange("p (b l) -> p b l", l=1).to_broadcast([P, ETB, P]), ALU.subtract).then_inc(v_step.h, 1)
                    v.wait_ge(v_step.h, v_step.next())
                    v.memset(lastf[:], 1.0).then_inc(v_step.h, 1)
                    v.wait_ge(v_step.h, v_step.next())
                    v.memset(first[:], -BIG).then_inc(v_step.h, 1)
                    v.wait_ge(v_step.h, v_step.next())
                    v.tensor_tensor(lastf[:, :, 0:P - 1], pair_dst[:, :, 0:P - 1], pair_dst[:, :, 1:P], ALU.not_equal).then_inc(v_step.h, 1)
                    v.wait_ge(v_step.h, v_step.next())
                    v.tensor_scalar(first[:, :, 1:P], lastf[:, :, 0:P - 1], -BIG, None, ALU.mult).then_inc(v_step.h, 1)
                    v.wait_ge(v_step.h, v_step.next())
                    v.nop().then_inc(pairs_ready.h, 1)
                    for b in range(ETB):
                        v.wait_ge(pairs_turned.h, b + 1)
                        c = slice(b * P, (b + 1) * P)
                        v.tensor_copy(psrc[:, c], ps[b][:, 0:P]).then_inc(v_step.h, 1)
                        v.wait_ge(v_step.h, v_step.next())
                        v.tensor_copy(pdl[:, c], ps[b][:, P:2 * P]).then_inc(v_step.h, 1)
                        v.wait_ge(v_step.h, v_step.next())
                        v.tensor_copy(plast[:, c], ps[b][:, 2 * P:3 * P]).then_inc(v_step.h, 1)
                        v.wait_ge(v_step.h, v_step.next())
                        v.tensor_copy(prow[:, c], ps[b][0:2, 3 * P:4 * P]).then_inc(v_step.h, 1)
                        v.wait_ge(v_step.h, v_step.next())

                @block.tensor
                def _(pe):
                    pe.wait_ge(counted.h, 1)
                    pe.matmul(ps[0][:, 0:ETB], incl[:], small[:, 1, :], start=True, stop=True)
                    pe.matmul(ps[0][:, 16:16 + ETB], ones[:], small[:, 1, :], start=True, stop=True).then_inc(scanned.h, 1)
                    pe.wait_ge(spread.h, 1)
                    diag = tmp[:].rearrange("p b l -> p (b l)")
                    pe.matmul(ps[1][:], ones[:], diag[:, 0:512], start=True, stop=True)
                    pe.matmul(ps[2][:, 0:PCOL - 512], ones[:], diag[:, 512:PCOL], start=True, stop=True).then_inc(spread_done.h, 1)
                    pe.wait_ge(pairs_ready.h, 1)
                    for b in range(ETB):
                        pe.transpose(ps[b][:, 0:P], pair_edges[:, b, 0:P], ident[:])
                        pe.transpose(ps[b][:, P:2 * P], pair_dst[:, b, :], ident[:])
                        pe.transpose(ps[b][:, 2 * P:3 * P], lastf[:, b, :], ident[:])
                        pe.matmul(ps[b][0:2, 3 * P:4 * P], drow[:, b, :], ident[:], start=True, stop=True).then_inc(pairs_turned.h, 1)
            stored.base += 16

    edge_tables()

    def degrees():
        with ExitStack() as ctx:
            hot = sb("hot", [P, 2, 2 * G, P], BF16, ctx)
            ones_b = sb("ones_b", [P, 1], BF16, ctx)
            cnt = sb("cnt", [P, PCOL], F32, ctx)
            cnt_t = sb("cnt_t", [P, ETB, P], F32, ctx)
            hit = sb("hit", [P, ETB, NT], F32, ctx)
            drow_f = sb("drow_f", [1, PCOL], F32, ctx)
            dcol = sb("dcol", [P, ETB], F32, ctx)
            deg = sb("deg", [P, NT], F32, ctx)
            tmp = sb("deg_tmp", [P, NT], F32, ctx)
            hot_ready, hot_used, count_out = sem("hot_ready"), sem("hot_used"), sem("count_out")
            row_ready, col_ready = sem("row_ready"), sem("col_ready")
            cnt_ready, cnt_turned, cnt_back, deg_ready = sem("cnt_ready"), sem("cnt_turned"), sem("cnt_back"), sem("deg_ready")
            root = Rsqrt(deg[:], dinv[:], tmp[:])
            with nc.Block() as block:
                @block.vector
                def _(v):
                    v.memset(ones_b[:], 1.0).then_inc(v_step.h, 1)
                    v.wait_ge(v_step.h, v_step.next())
                    v.memset(cnt[:], 0.0).then_inc(v_step.h, 1)
                    v.wait_ge(v_step.h, v_step.next())
                    v.tensor_copy(drow_f[:], prow[0:1, :]).then_inc(v_step.h, 1)
                    v.wait_ge(v_step.h, v_step.next())
                    v.nop().then_inc(row_ready.h, 1)

                    def mark(i, k):
                        v.tensor_tensor(hot[:, k], iota_f[:].rearrange("p (j n) -> p j n", j=1).to_broadcast([P, 2 * G, P]),
                                        pdl[:, bass.ds(i * 2 * G, 2 * G)].rearrange("p (j n) -> p j n", n=1).to_broadcast([P, 2 * G, P]),
                                        ALU.is_equal).then_inc(hot_ready.h, 1)

                    def keep(i, k):
                        v.wait_ge(hot_used.h, i + 1)
                        v.tensor_copy(cnt[:, bass.ds(i * 2 * G, 2 * G)], ps[k][:, 0:2 * G]).then_inc(count_out.h, 1)

                    mark(0, 0)
                    with v.Fori(0, ITERS // 2) as j:
                        mark(2 * j + 1, 1)
                        keep(2 * j, 0)
                        mark(2 * j + 2, 0)
                        keep(2 * j + 1, 1)
                    v.wait_ge(count_out.h, ITERS)
                    v.nop().then_inc(cnt_ready.h, 1)
                    v.wait_ge(col_ready.h, 1)
                    v.tensor_copy(dcol[:], ps[7][:, 0:ETB]).then_inc(v_step.h, 1)
                    v.wait_ge(v_step.h, v_step.next())
                    for b in range(ETB):
                        v.tensor_scalar(hit[:, b, :], iota_f[:, 0:NT], dcol[:, b:b + 1], None, ALU.is_equal).then_inc(v_step.h, 1)
                        v.wait_ge(v_step.h, v_step.next())
                    v.wait_ge(cnt_turned.h, 1)
                    v.tensor_copy(cnt_t[:, 0:4, :], ps[2][:].rearrange("p (b l) -> p b l", l=P)).then_inc(v_step.h, 1)
                    v.wait_ge(v_step.h, v_step.next())
                    v.tensor_copy(cnt_t[:, 4:ETB, :], ps[3][:, 0:(ETB - 4) * P].rearrange("p (b l) -> p b l", l=P)).then_inc(v_step.h, 1)
                    v.wait_ge(v_step.h, v_step.next())
                    v.nop().then_inc(cnt_back.h, 1)
                    v.wait_ge(deg_ready.h, 1)
                    v.tensor_scalar(deg[:], ps[4][:, 0:NT], 1.0, None, ALU.add).then_inc(v_step.h, 1)
                    v.wait_ge(v_step.h, v_step.next())
                    root.vector(v)

                @block.scalar
                def _(a):
                    root.scalar(a)

                @block.tensor
                def _(pe):
                    pe.wait_ge(row_ready.h, 1)
                    for b in range(ETB):
                        mm = pe.matmul(ps[7][:, b:b + 1], drow_f[0:1, b * P:(b + 1) * P], ones[0:1, 0:1], start=True, stop=True)
                    mm.then_inc(col_ready.h, 1)
                    with pe.Fori(0, ITERS // 2) as j:
                        for k in range(2):
                            pe.wait_ge(hot_ready.h, 2 * j + k + 1)
                            for b in range(2 * G):
                                mm = pe.matmul(ps[k][:, b:b + 1], hot[:, k, b, :], ones_b[:], start=True, stop=True)
                            mm.then_inc(hot_used.h, 1)
                    pe.wait_ge(cnt_ready.h, 1)
                    for b in range(ETB):
                        mm = pe.transpose(ps[2 + b // 4][:, b % 4 * P:(b % 4 + 1) * P], cnt[:, b * P:(b + 1) * P], ident[:])
                    mm.then_inc(cnt_turned.h, 1)
                    pe.wait_ge(cnt_back.h, 1)
                    for b in range(ETB):
                        mm = pe.matmul(ps[4][:, 0:NT], cnt_t[:, b, :], hit[:, b, :], start=(b == 0), stop=(b == ETB - 1))
                    mm.then_inc(deg_ready.h, 1)

    degrees()

    class NodeNorm:

        def __init__(self, ctx, name):
            self.stats = sb(name + "_stats", [P, NT, 6], F32, ctx)
            self.mean = sb(name + "_mean", [P, NT], F32, ctx)
            self.var = sb(name + "_var", [P, NT], F32, ctx)
            self.rstd = sb(name + "_rstd", [P, NT], F32, ctx)
            self.tmp = sb(name + "_tmp", [P, NT], F32, ctx)
            self.root = Rsqrt(self.var[:], self.rstd[:], self.tmp[:])
            self.seen = sem(name + "_seen")

        def stats_of(self, v, src):
            with v.Fori(0, NT) as d:
                v.bn_stats(self.stats[:, bass.ds(d, 1), :], src[:, bass.ds(d, 1), :]).then_inc(self.seen.h, 1)
            v.wait_ge(self.seen.h, NT)
            mean_e, sq_e, mean_o, sq_o = (self.stats[:, :, j] for j in (1, 2, 4, 5))
            mean = self.mean[:]
            v.tensor_tensor(self.tmp[:], mean_e, mean_o, ALU.subtract).then_inc(v_step.h, 1)
            v.wait_ge(v_step.h, v_step.next())
            v.tensor_tensor(mean, mean_e, mean_o, ALU.add).then_inc(v_step.h, 1)
            v.wait_ge(v_step.h, v_step.next())
            v.tensor_scalar(mean, mean, 0.5, None, ALU.mult).then_inc(v_step.h, 1)
            v.wait_ge(v_step.h, v_step.next())
            v.tensor_tensor(self.tmp[:], self.tmp[:], self.tmp[:], ALU.mult).then_inc(v_step.h, 1)
            v.wait_ge(v_step.h, v_step.next())
            v.tensor_tensor(self.var[:], sq_e, sq_o, ALU.add).then_inc(v_step.h, 1)
            v.wait_ge(v_step.h, v_step.next())
            v.tensor_scalar(self.var[:], self.var[:], 1.0 / F, EPS, ALU.mult, ALU.add).then_inc(v_step.h, 1)
            v.wait_ge(v_step.h, v_step.next())
            v.scalar_tensor_tensor(self.var[:], self.tmp[:], 0.25, self.var[:], ALU.mult, ALU.add).then_inc(v_step.h, 1)
            v.wait_ge(v_step.h, v_step.next())
            self.root.vector(v)

        def rows(self, v, src, dst, d, ready):
            v.tensor_scalar(dst, src[:, bass.ds(d, 1), :].rearrange("p a f -> p (a f)"), self.mean[:, bass.ds(d, 1)],
                            self.rstd[:, bass.ds(d, 1)], ALU.subtract, ALU.mult).then_inc(ready.h, 1)

    bigs = ExitStack()
    acc = sb("acc", [P, NT, F], F32, bigs)
    feat = sb("feat", [P, NT, F], F32, bigs)
    feat_t = feat[:].rearrange("p d f -> p (d f)").rearrange("p (c n) -> p c n", c=FC)
    vecs = sb("vecs", [P, 3, 3, FC], F32, bigs)
    wts = sb("wts", [P, FC, F], F32, bigs)
    stage = sb("stage", [P, 2, F], F32, bigs)
    lhs = sb("lhs", [P, 2, FC, P], F32, bigs)

    def load_rows(sp, big, src, done):
        sp.dma_start(big[:, 0:NT - 1, :], src[0:(NT - 1) * P, :].rearrange("(d p) f -> p d f", p=P)).then_inc(done.h, 16)
        sp.dma_start(big[0:NLAST, NT - 1, :], src[(NT - 1) * P:N, :]).then_inc(done.h, 16)

    def load_weights(sp, w, dst):
        sp.dma_start(dst, w.rearrange("(c p) n -> p c n", p=P)).then_inc(loaded.h, 16)

    def turn(pe, d, k, rows_ready):
        pe.wait_ge(rows_ready.h, d + 1)
        pe.wait_ge(turned_out.h, turned_out.base + d + 1)
        for c in range(FC):
            mm = pe.transpose(ps[k][:, c * P:(c + 1) * P], stage[:, k, c * P:(c + 1) * P], ident[:])
        mm.then_inc(turned.h, 1)

    def multiply(pe, w, d, k, lhs_ready, lhs_credit, ncols=F, bias=None):
        pe.wait_ge(lhs_ready.h, lhs_ready.base + d + 1 + lhs_credit)
        pe.wait_ge(projected_out.h, projected_out.base + d + 1)
        if bias is not None:
            pe.matmul(ps[2 + k][:, 0:ncols], ones[0:1, :], bias[:, 0:ncols], start=True, stop=False)
        for c in range(FC):
            mm = pe.matmul(ps[2 + k][:, 0:ncols], lhs[:, k, c, :], w[:, c, 0:ncols], start=(c == 0 and bias is None), stop=(c == FC - 1))
        mm.then_inc(projected.h, 1)

    def turn_and_multiply(pe, w, rows_ready, ncols=F, bias=None):
        turn(pe, 0, 0, rows_ready)
        with pe.Fori(0, NT // 2) as i:
            turn(pe, 2 * i + 1, 1, rows_ready)
            multiply(pe, w, 2 * i, 0, turned_out, 2, ncols, bias)
            turn(pe, 2 * i + 2, 0, rows_ready)
            multiply(pe, w, 2 * i + 1, 1, turned_out, 2, ncols, bias)
        multiply(pe, w, NT - 1, 0, turned_out, 2, ncols, bias)

    def turned_to_lhs(a):
        for d, k in node_tiles(a):
            a.wait_ge(turned.h, turned.base + d + 1 + 2)
            a.wait_ge(projected.h, projected.base + d + 1)
            a.activation(lhs[:, k].rearrange("p c n -> p (c n)"), ps[k][:, 0:F], ACT.Copy).then_inc(turned_out.h, 1)

    def scale_to_acc(v, d, k):
        v.wait_ge(projected.h, projected.base + d + 1 + 2)
        v.tensor_scalar(acc[:, bass.ds(d, 1), :].rearrange("p a f -> p (a f)"), ps[2 + k][:, 0:F], dinv[:, bass.ds(d, 1)], None, ALU.mult).then_inc(projected_out.h, 1)

    def store_acc(sp):
        for d, k in node_tiles(sp):
            sp.wait_ge(projected_out.h, projected_out.base + d + 1 + 2)
            sp.dma_start(node_table[bass.ds(d * P, P), :], acc[:, bass.ds(d, 1), :].rearrange("p a f -> p (a f)")).then_inc(stored.h, 16)
        sp.wait_ge(stored.h, stored.base + 16 * NT)

    def project_counted(turned_too=True):
        if turned_too:
            turned.base += NT
            turned_out.base += NT
        projected.base += NT
        projected_out.base += NT
        stored.base += 16 * NT

    def first_projection():
        with ExitStack() as ctx:
            norm = NodeNorm(ctx, "ln0")
            rows_ready, zeroed, vec_in = sem("rows_ready"), sem("zeroed"), sem("vec_in")
            with nc.Block() as block:
                @block.sync
                def _(sp):
                    load_weights(sp, t["L0_gnn_W1"], wts[:])
                    sp.wait_ge(zeroed.h, 1)
                    load_rows(sp, feat, t["x"], x_loaded)
                    with nc.allow_non_contiguous_dma("vectors of 256 features onto partitions"):
                        for k in range(3):
                            for j, name in enumerate(("b", "g", "be")):
                                sp.dma_start(vecs[:, k, j, :], t[f"L0_gnn_{name}{k + 1}"].rearrange("(c p) -> p c", p=P)).then_inc(vec_in.h, 16)
                    store_acc(sp)
                    sp.wait_ge(vec_in.h, 16 * 9)

                @block.vector
                def _(v):
                    v.memset(feat[:, NT - 1, :], 0.0).then_inc(zeroed.h, 1)
                    v.wait_ge(x_loaded.h, x_loaded.base + 32)
                    norm.stats_of(v, feat)

                    def stage_rows(d, k):
                        v.wait_ge(turned.h, turned.base + d + 1)
                        norm.rows(v, feat, stage[:, k, :], d, rows_ready)

                    two_ahead(v, stage_rows, lambda d, k: scale_to_acc(v, d, k))

                @block.scalar
                def _(a):
                    norm.root.scalar(a)
                    turned_to_lhs(a)

                @block.tensor
                def _(pe):
                    pe.wait_ge(loaded.h, loaded.base + 16)
                    turn_and_multiply(pe, wts, rows_ready)
            x_loaded.base += 32
            loaded.base += 16
            project_counted()

    first_projection()

    def gather_rows(g, rows, table):
        with g.Fori(0, ITERS) as i:
            for h in range(2):
                g.wait_ge(aggregated.h, aggregated.base + (i * 2 + h + 1) * G)
                g.tensor_copy(idx[:, h, :], psrc[:, bass.ds(i * 2 * G + h * G, G)]).then_inc(idx_ready.h, 1)
                g.wait_ge(idx_ready.h, idx_ready.base + 2 * i + h + 1)
                g.tensor_tensor(carrier[:], psrc[:, 0:1], psrc[:, 0:1], ALU.add)
                for b in range(G):
                    s = h * G + b
                    g.indirect_dma_start(rows[:, s, :], None, table,
                                         bass.IndirectOffsetOnAxis(ap=idx[:, h, b:b + 1], axis=0)).then_inc(row_sem[s].h, 16)

    def gather_counted():
        aggregated.base += NPAIR
        added.base += NPAIR
        onehot_ready.base += 2 * ITERS + 1
        idx_ready.base += 2 * ITERS
        for s in row_sem:
            s.base += 16 * ITERS

    def mark_pairs(v, hot, q, h):
        v.tensor_tensor(hot[:, h], iota_f[:].rearrange("p (j n) -> p j n", j=1).to_broadcast([P, G, P]),
                        pdl[:, bass.ds(q * G, G)].rearrange("p (j n) -> p j n", n=1).to_broadcast([P, G, P]),
                        ALU.is_equal).then_inc(onehot_ready.h, 1)

    def pair_bank(b, n=F):
        return ps[4 + b // 2][:, b % 2 * F:b % 2 * F + n]

    def aggregate(pe, hot, rows, i, h):
        pe.wait_ge(onehot_ready.h, onehot_ready.base + 2 * i + h + 1)
        for b in range(G):
            s = h * G + b
            pe.wait_ge(row_sem[s].h, row_sem[s].base + 16 * (i + 1))
            if b % 2 == 0:
                pe.wait_ge(added.h, added.base + (2 * i + h) * G + b + 2)
            pe.matmul(pair_bank(b), hot[:, h, b, :], rows[:, s, :], start=True, stop=True).then_inc(aggregated.h, 1)

    def add_pairs(v, i, h):
        for b in range(G):
            n = (2 * i + h) * G + b
            d = v.value_load(prow[0:1, bass.ds(n, 1)], min_val=0, max_val=NT - 1)
            row = acc[:, bass.ds(d, 1), :].rearrange("p a f -> p (a f)")
            if b % 2 == 0:
                v.wait_ge(aggregated.h, aggregated.base + 2 * G + n + 2)
            v.wait_ge(added.h, added.base + G + n)
            v.tensor_tensor(row, row, pair_bank(b), ALU.add).then_inc(added.h, 1)

    def gcn_layer(k):
        last = k == 2
        with ExitStack() as ctx:
            hot = sb("hot", [P, 2, G, P], F32, ctx)
            rows = sb("rows", [P, 2 * G, F], F32, ctx)
            bn = sb("bn", [P, FC, -(-N // 512), 6], F32, ctx)
            mv = sb("bn_mv", [P, FC, 2], F32, ctx)
            var = sb("bn_var", [P, FC], F32, ctx)
            rstd = sb("bn_rstd", [P, FC], F32, ctx)
            tmp = sb("bn_tmp", [P, FC], F32, ctx)
            gain = sb("gain", [P, FC], F32, ctx)
            shift = sb("shift", [P, FC], F32, ctx)
            y_ready, affine_set, affine_ready = sem(f"y_ready{k}"), sem(f"affine_set{k}"), sem(f"affine_ready{k}")
            root = Rsqrt(var[:], rstd[:], tmp[:])
            if k == 0:
                zeros = sb("zeros", [P, F], F32, ctx)
                zeros_set, zeros_out = sem("zeros_set"), sem("zeros_out")
            with nc.Block() as block:
                @block.gpsimd
                def _(g):
                    gather_rows(g, rows, node_table)

                @block.sync
                def _(sp):
                    if k == 0:
                        sp.wait_ge(zeros_set.h, 1)
                        with sp.Fori(0, MT + 2) as m:
                            sp.dma_start(slot_rows[bass.ds(m * P, P), :], zeros[:]).then_inc(zeros_out.h, 16)
                        for j in range(2):
                            sp.dma_start(slot_out[CAP + j * P:CAP + (j + 1) * P, :], zeros[:]).then_inc(zeros_out.h, 16)
                        sp.wait_ge(zeros_out.h, 16 * (MT + 4))
                    if not last:
                        load_weights(sp, t[f"L0_gnn_W{k + 2}"], wts[:])
                        store_acc(sp)
                    else:
                        sp.wait_ge(y_ready.h, NT)
                        load_rows(sp, acc, t["x"], x_loaded)

                @block.vector
                def _(v):
                    if k == 0:
                        v.memset(zeros[:], 0.0).then_inc(zeros_set.h, 1)
                    mark_pairs(v, hot, 0, 0)
                    with v.Fori(0, ITERS) as i:
                        v.wait_ge(aggregated.h, aggregated.base + (i + 1) * 2 * G)
                        mark_pairs(v, hot, 2 * i + 1, 1)
                        add_pairs(v, i, 0)
                        mark_pairs(v, hot, 2 * i + 2, 0)
                        add_pairs(v, i, 1)
                    v.wait_ge(added.h, added.base + G + NPAIR)
                    for d, par in node_tiles(v):
                        v.wait_ge(turned.h, turned.base + d + 1)
                        row = acc[:, bass.ds(d, 1), :].rearrange("p a f -> p (a f)")
                        v.tensor_scalar(stage[:, par, :], row, dinv[:, bass.ds(d, 1)], None, ALU.mult).then_inc(y_ready.h, 1)
                    v.wait_ge(turned_out.h, turned_out.base + NT + 2)
                    for c in range(FC):
                        for j in range(-(-N // 512)):
                            v.bn_stats(bn[:, c, j, :], feat_t[:, c, j * 512:min(N, (j + 1) * 512)]).then_inc(v_step.h, 1)
                            v.wait_ge(v_step.h, v_step.next())
                        v.bn_aggr(mv[:, c, :], bn[:, c].rearrange("p j s -> p (j s)")).then_inc(v_step.h, 1)
                        v.wait_ge(v_step.h, v_step.next())
                    v.tensor_scalar(var[:], mv[:, :, 1], EPS, None, ALU.add).then_inc(v_step.h, 1)
                    v.wait_ge(v_step.h, v_step.next())
                    root.vector(v)
                    v.tensor_tensor(gain[:], rstd[:], vecs[:, k, 1, :], ALU.mult).then_inc(v_step.h, 1)
                    v.wait_ge(v_step.h, v_step.next())
                    v.tensor_tensor(tmp[:], mv[:, :, 0], gain[:], ALU.mult).then_inc(v_step.h, 1)
                    v.wait_ge(v_step.h, v_step.next())
                    v.tensor_tensor(shift[:], vecs[:, k, 2, :], tmp[:], ALU.subtract).then_inc(v_step.h, 1)
                    v.wait_ge(v_step.h, v_step.next())
                    v.nop().then_inc(affine_set.h, 1)
                    if not last:
                        for d, par in node_tiles(v):
                            scale_to_acc(v, d, par)
                    else:
                        v.wait_ge(x_loaded.h, x_loaded.base + 32)
                        for d, par in node_tiles(v):
                            v.wait_ge(projected.h, projected.base + d + 1 + 2)
                            row = acc[:, bass.ds(d, 1), :].rearrange("p a f -> p (a f)")
                            v.tensor_tensor(row, row, ps[2 + par][:, 0:F], ALU.add).then_inc(projected_out.h, 1)

                @block.scalar
                def _(a):
                    for d, par in node_tiles(a):
                        a.wait_ge(turned.h, turned.base + d + 1 + 2)
                        for c in range(FC):
                            op = a.activation(feat_t[:, c, bass.ds(d * P, P)], ps[par][:, c * P:(c + 1) * P], ACT.Identity, bias=vecs[:, k, 0, c:c + 1])
                        op.then_inc(turned_out.h, 1)
                    root.scalar(a)
                    a.wait_ge(affine_set.h, 1)
                    for d, par in node_tiles(a):
                        a.wait_ge(projected.h, projected.base + d + 1)
                        for c in range(FC):
                            op = a.activation(lhs[:, par, c, :], feat_t[:, c, bass.ds(d * P, P)], ACT.Identity, bias=shift[:, c:c + 1], scale=gain[:, c:c + 1])
                        op.then_inc(affine_ready.h, 1)

                @block.tensor
                def _(pe):
                    with pe.Fori(0, ITERS) as i:
                        aggregate(pe, hot, rows, i, 0)
                        aggregate(pe, hot, rows, i, 1)
                    for d, par in node_tiles(pe):
                        turn(pe, d, par, y_ready)
                    if not last:
                        pe.wait_ge(loaded.h, loaded.base + 16)
                        for d, par in node_tiles(pe):
                            multiply(pe, wts, d, par, affine_ready, 0)
                    else:
                        for d, par in node_tiles(pe):
                            pe.wait_ge(affine_ready.h, d + 1)
                            pe.wait_ge(projected_out.h, projected_out.base + d + 1)
                            for c in range(FC):
                                mm = pe.transpose(ps[2 + par][:, c * P:(c + 1) * P], lhs[:, par, c, :], ident[:])
                            mm.then_inc(projected.h, 1)
            gather_counted()
            project_counted()
            if last:
                x_loaded.base += 32
                stored.base -= 16 * NT
            else:
                loaded.base += 16

    for k in range(3):
        gcn_layer(k)
    def route():
        with ExitStack() as ctx:
            norm = NodeNorm(ctx, "ln1")
            inner = NodeNorm(ctx, "ln_moe")
            wr = sb("wr", [P, FC, EXPERTS], F32, ctx)
            br = sb("br", [1, EXPERTS], F32, ctx)
            logits = sb("logits", [P, NT, EXPERTS], F32, ctx)
            low = sb("low", [P, NT, EXPERTS], F32, ctx)
            hits = sb("hits", [P, NT, EXPERTS], F32, ctx)
            pick = sb("pick", [P, 2, NT, EXPERTS], F32, ctx)
            both = sb("both", [P, NT, EXPERTS], F32, ctx)
            tot = sb("tot", [P, NT, EXPERTS], F32, ctx)
            run = sb("run", [P, NT, EXPERTS], F32, ctx)
            best = sb("best", [P, 2, NT], F32, ctx)
            top = sb("top", [P, NT], F32, ctx)
            order = sb("order", [P, EXPERTS], F32, ctx)
            node = sb("node", [P, NT], F32, ctx)
            node_i = sb("node_i", [P, NT], I32, ctx)
            valid = sb("valid", [P, NT], F32, ctx)
            spare = sb("spare", [P, NT], F32, ctx)
            slot_f = sb("slot_f", [P, 2, NT], F32, ctx)
            e8 = sb("e8", [P, 4, EXPERTS], F32, ctx)
            e8_i = sb("e8_i", [P, EXPERTS], I32, ctx)
            upto = sb("upto", [P, MT, EXPERTS], F32, ctx)
            z_done, z_ready, rows_ready, xn_ready = sem("z_done"), sem("z_ready"), sem("z_staged"), sem("xn_ready")
            numbered, exp_ready, exp_done = sem("numbered"), sem("exp_ready"), sem("exp_done")
            picked, ranked, slots_set = sem("picked"), sem("ranked"), sem("slots_set")
            slot_idx = sem("slot_idx")
            scattered = [sem(f"scattered{k}") for k in range(2)]
            with nc.Block() as block:
                @block.sync
                def _(sp):
                    sp.dma_start(resid.rearrange("(d p) f -> p d f", p=P), acc[:]).then_inc(stored.h, 16)
                    sp.dma_start(wr[:], t["L0_ffn_Wr"].rearrange("(c p) e -> p c e", p=P)).then_inc(loaded.h, 16)
                    sp.dma_start(br[:], t["L0_ffn_br"].rearrange("(a e) -> a e", a=1)).then_inc(loaded.h, 16)
                    sp.wait_ge(stored.h, stored.base + 16)

                @block.gpsimd
                def _(g):
                    g.iota(node_i[:], [[P, NT]], base=0, channel_multiplier=1).then_inc(numbered.h, 1)
                    g.wait_ge(slots_set.h, 1)
                    for d, k in node_tiles_apart(g):
                        wait_earlier(g, scattered[k], d, k, 32)
                        g.tensor_copy(idx[:, k, 0:2], slots[:, :, bass.ds(d, 1)].rearrange("p a d -> p (a d)")).then_inc(slot_idx.h, 1)
                        g.wait_ge(xn_ready.h, d + 1)
                        g.wait_ge(slot_idx.h, d + 1)
                        g.tensor_tensor(carrier[:], psrc[:, 0:1], psrc[:, 0:1], ALU.add)
                        for j in range(2):
                            g.indirect_dma_start(slot_rows, bass.IndirectOffsetOnAxis(ap=idx[:, k, j:j + 1], axis=0), stage[:, k, :], None).then_inc(scattered[k].h, 16)
                    g.wait_ge(scattered[0].h, 32 * (NT // 2 + 1))
                    g.wait_ge(scattered[1].h, 32 * (NT // 2))

                @block.vector
                def _(v):
                    norm.stats_of(v, acc)
                    for d, _ in node_tiles(v):
                        norm.rows(v, acc, rows_of(feat, d), d, z_done)
                    v.wait_ge(z_done.h, NT)
                    inner.stats_of(v, feat)

                    def stage_z(d, k):
                        v.wait_ge(turned.h, turned.base + d + 1)
                        v.tensor_copy(stage[:, k, :], rows_of(feat, d)).then_inc(rows_ready.h, 1)

                    def keep_logits(d, k):
                        v.wait_ge(projected.h, projected.base + d + 1 + 2)
                        v.tensor_copy(logits[:, bass.ds(d, 1), :].rearrange("p a e -> p (a e)"), ps[2 + k][:, 0:EXPERTS]).then_inc(projected_out.h, 1)

                    two_ahead(v, stage_z, keep_logits)
                    v.wait_ge(projected_out.h, projected_out.base + NT + 2)

                    def over_e(x):
                        return x.rearrange("p (d a) -> p d a", a=1).to_broadcast([P, NT, EXPERTS])

                    def over_d(x, n=NT):
                        return x.rearrange("p (a e) -> p a e", a=1).to_broadcast([P, n, EXPERTS])

                    v.wait_ge(numbered.h, 1)
                    v.tensor_copy(node[:], node_i[:]).then_inc(v_step.h, 1)
                    v.wait_ge(v_step.h, v_step.next())
                    v.tensor_scalar(valid[:], node[:], float(N), None, ALU.is_lt).then_inc(v_step.h, 1)
                    v.wait_ge(v_step.h, v_step.next())
                    v.tensor_scalar(order[:], iota_f[:, 0:EXPERTS], -1.0, float(EXPERTS), ALU.mult, ALU.add).then_inc(v_step.h, 1)
                    v.wait_ge(v_step.h, v_step.next())
                    src = logits
                    for j in range(2):
                        v.tensor_reduce(best[:, j, :], src[:], AX.X, ALU.max).then_inc(v_step.h, 1)
                        v.wait_ge(v_step.h, v_step.next())
                        v.tensor_tensor(hits[:], src[:], over_e(best[:, j, :]), ALU.is_equal).then_inc(v_step.h, 1)
                        v.wait_ge(v_step.h, v_step.next())
                        v.tensor_tensor(hits[:], hits[:], over_d(order[:]), ALU.mult).then_inc(v_step.h, 1)
                        v.wait_ge(v_step.h, v_step.next())
                        v.tensor_reduce(top[:], hits[:], AX.X, ALU.max).then_inc(v_step.h, 1)
                        v.wait_ge(v_step.h, v_step.next())
                        v.tensor_tensor(pick[:, j], hits[:], over_e(top[:]), ALU.is_equal).then_inc(v_step.h, 1)
                        v.wait_ge(v_step.h, v_step.next())
                        if j == 0:
                            v.scalar_tensor_tensor(low[:], pick[:, 0], -BIG, logits[:], ALU.mult, ALU.add).then_inc(v_step.h, 1)
                            v.wait_ge(v_step.h, v_step.next())
                            src = low
                        v.tensor_tensor(pick[:, j], pick[:, j], over_e(valid[:]), ALU.mult).then_inc(v_step.h, 1)
                        v.wait_ge(v_step.h, v_step.next())
                    v.tensor_tensor(top[:], best[:, 1, :], best[:, 0, :], ALU.subtract).then_inc(v_step.h, 1)
                    v.wait_ge(v_step.h, v_step.next())
                    v.nop().then_inc(exp_ready.h, 1)
                    v.tensor_tensor(both[:], pick[:, 0], pick[:, 1], ALU.add).then_inc(v_step.h, 1)
                    v.wait_ge(v_step.h, v_step.next())
                    v.nop().then_inc(picked.h, 1)
                    v.wait_ge(exp_done.h, 1)
                    v.tensor_scalar(spare[:], best[:, 1, :], 1.0, None, ALU.add).then_inc(v_step.h, 1)
                    v.wait_ge(v_step.h, v_step.next())
                    v.reciprocal(gate[:, 0, :], spare[:]).then_inc(v_step.h, 1)
                    v.wait_ge(v_step.h, v_step.next())
                    v.tensor_tensor(gate[:, 1, :], best[:, 1, :], gate[:, 0, :], ALU.mult).then_inc(v_step.h, 1)
                    v.wait_ge(v_step.h, v_step.next())
                    v.wait_ge(ranked.h, 1)
                    v.tensor_copy(tot[:], ps[1][:, 0:NT * EXPERTS].rearrange("p (d e) -> p d e", e=EXPERTS)).then_inc(v_step.h, 1)
                    v.wait_ge(v_step.h, v_step.next())
                    for e in range(EXPERTS):
                        v.tensor_tensor_scan(run[:, :, e], ones[:, 0:NT], tot[:, :, e], 0.0, ALU.mult, ALU.add).then_inc(v_step.h, 1)
                        v.wait_ge(v_step.h, v_step.next())
                    count, tiles, upto_e, begin = (e8[:, j, :] for j in range(4))
                    v.tensor_scalar(count, run[:, NT - 1, :], float(P - 1), None, ALU.add).then_inc(v_step.h, 1)
                    v.wait_ge(v_step.h, v_step.next())
                    v.tensor_tensor(run[:], run[:], tot[:], ALU.subtract).then_inc(v_step.h, 1)
                    v.wait_ge(v_step.h, v_step.next())
                    v.tensor_tensor(run[:], run[:], ps[0][:, 0:NT * EXPERTS].rearrange("p (d e) -> p d e", e=EXPERTS), ALU.add).then_inc(v_step.h, 1)
                    v.wait_ge(v_step.h, v_step.next())
                    v.tensor_copy(e8_i[:], count).then_inc(v_step.h, 1)
                    v.wait_ge(v_step.h, v_step.next())
                    v.tensor_scalar(e8_i[:], e8_i[:], 7, None, ALU.arith_shift_right).then_inc(v_step.h, 1)
                    v.wait_ge(v_step.h, v_step.next())
                    v.tensor_copy(tiles, e8_i[:]).then_inc(v_step.h, 1)
                    v.wait_ge(v_step.h, v_step.next())
                    v.tensor_tensor_scan(upto_e, ones[:, 0:EXPERTS], tiles, 0.0, ALU.mult, ALU.add).then_inc(v_step.h, 1)
                    v.wait_ge(v_step.h, v_step.next())
                    v.tensor_tensor(begin, upto_e, tiles, ALU.subtract).then_inc(v_step.h, 1)
                    v.wait_ge(v_step.h, v_step.next())
                    v.tensor_scalar(begin, begin, float(P), None, ALU.mult).then_inc(v_step.h, 1)
                    v.wait_ge(v_step.h, v_step.next())
                    v.tensor_tensor(run[:], run[:], over_d(begin), ALU.add).then_inc(v_step.h, 1)
                    v.wait_ge(v_step.h, v_step.next())
                    v.tensor_scalar(spare[:], node[:], float(CAP - (NT - 1) * P), None, ALU.add).then_inc(v_step.h, 1)
                    v.wait_ge(v_step.h, v_step.next())
                    v.tensor_scalar(top[:], valid[:], -1.0, 1.0, ALU.mult, ALU.add).then_inc(v_step.h, 1)
                    v.wait_ge(v_step.h, v_step.next())
                    v.tensor_tensor(spare[:], spare[:], top[:], ALU.mult).then_inc(v_step.h, 1)
                    v.wait_ge(v_step.h, v_step.next())
                    for j in range(2):
                        v.tensor_tensor(hits[:], pick[:, j], run[:], ALU.mult).then_inc(v_step.h, 1)
                        v.wait_ge(v_step.h, v_step.next())
                        v.tensor_reduce(slot_f[:, j, :], hits[:], AX.X, ALU.add).then_inc(v_step.h, 1)
                        v.wait_ge(v_step.h, v_step.next())
                        v.tensor_tensor(slot_f[:, j, :], slot_f[:, j, :], spare[:], ALU.add).then_inc(v_step.h, 1)
                        v.wait_ge(v_step.h, v_step.next())
                        v.scalar_tensor_tensor(spare[:], top[:], float(P), spare[:], ALU.mult, ALU.add).then_inc(v_step.h, 1)
                        v.wait_ge(v_step.h, v_step.next())
                    v.tensor_copy(slots[:], slot_f[:]).then_inc(v_step.h, 1)
                    v.wait_ge(v_step.h, v_step.next())
                    v.nop().then_inc(slots_set.h, 1)
                    v.tensor_tensor(upto[:], over_d(upto_e, MT), iota_f[:, 0:MT].rearrange("p (k a) -> p k a", a=1).to_broadcast([P, MT, EXPERTS]), ALU.is_le).then_inc(v_step.h, 1)
                    v.wait_ge(v_step.h, v_step.next())
                    v.tensor_reduce(tile_expert[:], upto[:], AX.X, ALU.add).then_inc(v_step.h, 1)
                    v.wait_ge(v_step.h, v_step.next())
                    v.tensor_scalar(tile_expert[:], tile_expert[:], float(EXPERTS - 1), None, ALU.min).then_inc(v_step.h, 1)
                    v.wait_ge(v_step.h, v_step.next())
                    v.tensor_copy(tile_expert_i[:], tile_expert[0:1, :]).then_inc(v_step.h, 1)
                    v.wait_ge(v_step.h, v_step.next())
                    for d, k in node_tiles_apart(v):
                        wait_earlier(v, scattered[k], d, k, 32)
                        inner.rows(v, feat, stage[:, k, :], d, xn_ready)

                @block.scalar
                def _(a):
                    norm.root.scalar(a)
                    inner.root.scalar(a)
                    turned_to_lhs(a)
                    a.wait_ge(exp_ready.h, 1)
                    a.activation(best[:, 1, :], top[:], ACT.Exp).then_inc(exp_done.h, 1)

                @block.tensor
                def _(pe):
                    pe.wait_ge(loaded.h, loaded.base + 32)
                    turn_and_multiply(pe, wr, rows_ready, EXPERTS, br)
                    pe.wait_ge(picked.h, 1)
                    flat = both[:].rearrange("p d e -> p (d e)")
                    pe.matmul(ps[0][:, 0:NT * EXPERTS], excl[:], flat, start=True, stop=True)
                    pe.matmul(ps[1][:, 0:NT * EXPERTS], ones[:], flat, start=True, stop=True).then_inc(ranked.h, 1)
            loaded.base += 32
            project_counted()
            stored.base += 16 - 16 * NT

    route()
    bigs.close()

    def experts():
        with ExitStack() as ctx:
            w1 = sb("w1", [P, EXPERTS, FC, HID], F32, ctx)
            w2 = sb("w2", [P, EXPERTS, HC, F], F32, ctx)
            lng = sb("lng", [P, FC, EXPERTS], F32, ctx)
            lnb = sb("lnb", [P, FC, EXPERTS], F32, ctx)
            bias_f = sb("bias_f", [EXPERTS, HID + F], F32, ctx)
            bias = sb("bias", [96, HID + F], BF16, ctx)
            expert_f = sb("expert_f", [96, 1], F32, ctx)
            expert_i = sb("expert_i", [96, 1], I32, ctx)
            sel1 = sb("sel1", [96, 2, P], BF16, ctx)
            sel2 = sb("sel2", [96, 2, P], BF16, ctx)
            xt = sb("xt", [P, 2, F], F32, ctx)
            xe = sb("xe", [P, 2, FC, P], F32, ctx)
            hid = sb("hid", [P, 2, HID], F32, ctx)
            hid_t = sb("hid_t", [P, 2, HC, P], F32, ctx)
            y = sb("y", [P, 2, F], F32, ctx)
            w_in, vec_in, split, lane = sem("w_in"), sem("vec_in_moe"), sem("bias_split"), sem("expert_lane")
            xt_in = [sem(f"xt_in{k}") for k in range(2)]
            y_out = [sem(f"y_out{k}") for k in range(2)]
            x_turned, x_scaled = sem("x_turned"), sem("x_scaled")
            h_done, h_act, h_turned, h_kept = sem("h_done"), sem("h_act"), sem("h_turned"), sem("h_kept")
            y_done, y_kept, sel1_ready, sel2_ready = sem("y_done"), sem("y_kept"), sem("sel1_ready"), sem("sel2_ready")

            def each(eng, lo, hi, body):
                n = (hi - lo) // 2
                if n:
                    with eng.Fori(0, n) as i:
                        body(2 * i + lo, lo % 2)
                        body(2 * i + lo + 1, (lo + 1) % 2)
                if (hi - lo) % 2:
                    body(hi - 1, (hi - 1) % 2)

            with nc.Block() as block:
                @block.sync
                def _(sp):
                    for e in range(EXPERTS):
                        sp.dma_start(w1[:, e], t["L0_ffn_W1"][e].rearrange("(c p) n -> p c n", p=P)).then_inc(w_in.h, 16)
                        sp.dma_start(w2[:, e], t["L0_ffn_W2"][e].rearrange("(c p) n -> p c n", p=P)).then_inc(w_in.h, 16)

                    def load(k, par):
                        sp.dma_start(xt[:, par, :], slot_rows[bass.ds(k * P, P), :]).then_inc(xt_in[par].h, 16)

                    load(0, 0)
                    load(1, 1)

                    def reload(k, par):
                        sp.wait_ge(x_turned.h, k + 1)
                        load(k + 2, par)

                    def store(k, par):
                        sp.wait_ge(y_kept.h, k + 1)
                        sp.dma_start(slot_out[bass.ds(k * P, P), :], y[:, par, :]).then_inc(y_out[par].h, 16)

                    def body(k, par):
                        reload(k, par)
                        store(k - 3, 1 - par)

                    each(sp, 0, 3, reload)
                    each(sp, 3, MT - 2, body)
                    each(sp, MT - 5, MT, store)
                    for s in y_out:
                        sp.wait_ge(s.h, 16 * (MT // 2))

                @block.gpsimd
                def _(g):
                    for j in range(3):
                        g.iota(expert_i[32 * j:32 * j + 32, :], [[0, 1]], base=0, channel_multiplier=1).then_inc(lane.h, 1)

                @block.vector
                def _(v):
                    v.memset(bias[:], 0.0).then_inc(v_step.h, 1)
                    v.wait_ge(v_step.h, v_step.next())
                    v.wait_ge(lane.h, 3)
                    v.tensor_copy(expert_f[:], expert_i[:]).then_inc(v_step.h, 1)
                    v.wait_ge(v_step.h, v_step.next())
                    v.wait_ge(vec_in.h, 16 * (2 + 2 * EXPERTS))
                    for j in range(3):
                        part = bias[32 * j:32 * j + EXPERTS, :]
                        v.tensor_copy(part, bias_f[:]).then_inc(v_step.h, 1)
                        v.wait_ge(v_step.h, v_step.next())
                        if j < 2:
                            v.tensor_tensor(bias_f[:], bias_f[:], part, ALU.subtract).then_inc(v_step.h, 1)
                            v.wait_ge(v_step.h, v_step.next())
                    v.nop().then_inc(split.h, 1)

                    def select(sel, ready, k, par):
                        v.tensor_scalar(sel[:, par, :], tile_expert[0:96, bass.ds(k, 1)].to_broadcast([96, P]), expert_f[:], None, ALU.is_equal).then_inc(ready.h, 1)

                    def keep_y(k, par):
                        v.wait_ge(y_done.h, k + 1)
                        wait_earlier(v, y_out[par], k, par, 16)
                        v.tensor_copy(y[:, par, :], ps[6 + par][:, 0:F]).then_inc(y_kept.h, 1)

                    def keep_h(k, par):
                        for j in range(2):
                            v.wait_ge(h_turned.h, 2 * k + j + 1)
                            v.tensor_copy(hid_t[:, par, 4 * j:4 * j + 4, :].rearrange("p c n -> p (c n)"), ps[4 + j][:]).then_inc(h_kept.h, 1)

                    select(sel1, sel1_ready, 0, 0)
                    select(sel1, sel1_ready, 1, 1)
                    select(sel2, sel2_ready, 0, 0)
                    keep_h(0, 0)
                    select(sel1, sel1_ready, 2, 0)
                    select(sel2, sel2_ready, 1, 1)

                    def body(k, par):
                        keep_y(k - 1, 1 - par)
                        keep_h(k, par)
                        select(sel1, sel1_ready, k + 2, par)
                        select(sel2, sel2_ready, k + 1, 1 - par)

                    body(1, 1)
                    body(2, 0)
                    each(v, 3, MT - 3, body)
                    body(MT - 3, (MT - 3) % 2)
                    for k in (MT - 2, MT - 1):
                        keep_y(k - 1, (k - 1) % 2)
                        keep_h(k, k % 2)
                        if k + 1 < MT:
                            select(sel2, sel2_ready, k + 1, (k + 1) % 2)
                    keep_y(MT - 1, (MT - 1) % 2)

                @block.scalar
                def _(a):
                    with nc.allow_non_contiguous_dma("vectors of 256 features onto partitions"):
                        for e in range(EXPERTS):
                            a.dma_start(lng[:, :, e], t["L0_ffn_ln_g"][e].rearrange("(c p) -> p c", p=P)).then_inc(vec_in.h, 16)
                            a.dma_start(lnb[:, :, e], t["L0_ffn_ln_b"][e].rearrange("(c p) -> p c", p=P)).then_inc(vec_in.h, 16)
                    a.dma_start(bias_f[:, 0:HID], t["L0_ffn_b1"]).then_inc(vec_in.h, 16)
                    a.dma_start(bias_f[:, HID:HID + F], t["L0_ffn_b2"]).then_inc(vec_in.h, 16)
                    a.wait_ge(vec_in.h, 16 * (2 + 2 * EXPERTS))

                    def scale_x(k, par):
                        e = a.value_load(tile_expert_i[0:1, bass.ds(k, 1)], min_val=0, max_val=EXPERTS - 1)
                        a.wait_ge(x_turned.h, k + 1)
                        for c in range(FC):
                            op = a.activation(xe[:, par, c, :], ps[par][:, c * P:(c + 1) * P], ACT.Identity,
                                              bias=lnb[:, c, bass.ds(e, 1)], scale=lng[:, c, bass.ds(e, 1)])
                        op.then_inc(x_scaled.h, 1)

                    def act_h(k, par):
                        for j in range(2):
                            a.wait_ge(h_done.h, 2 * k + j + 1)
                            a.activation(hid[:, par, j * 512:(j + 1) * 512], ps[2 + j][:], ACT.Gelu).then_inc(h_act.h, 1)

                    scale_x(0, 0)
                    scale_x(1, 1)
                    act_h(0, 0)

                    def body(k, par):
                        act_h(k + 1, 1 - par)
                        scale_x(k + 2, par)

                    each(a, 0, MT - 2, body)
                    act_h(MT - 1, (MT - 1) % 2)

                @block.tensor
                def _(pe):
                    def turn_x(k, par):
                        pe.wait_ge(xt_in[par].h, (k - par) * 8 + 16)
                        for c in range(FC):
                            mm = pe.transpose(ps[par][:, c * P:(c + 1) * P], xt[:, par, c * P:(c + 1) * P], ident[:])
                        mm.then_inc(x_turned.h, 1)

                    def up(k, par):
                        e = pe.value_load(tile_expert_i[0:1, bass.ds(k, 1)], min_val=0, max_val=EXPERTS - 1)
                        pe.wait_ge(x_scaled.h, k + 1)
                        pe.wait_ge(sel1_ready.h, k + 1)
                        for j in range(2):
                            pe.matmul(ps[2 + j][:], sel1[:, par, :], bias[:, j * 512:(j + 1) * 512], start=True, stop=False)
                            for c in range(FC):
                                mm = pe.matmul(ps[2 + j][:], xe[:, par, c, :], w1[:, bass.ds(e, 1), c, j * 512:(j + 1) * 512].rearrange("p a n -> p (a n)"),
                                               start=False, stop=(c == FC - 1))
                            mm.then_inc(h_done.h, 1)

                    def turn_h(k, par):
                        for j in range(2):
                            pe.wait_ge(h_act.h, 2 * k + j + 1)
                            for c in range(4):
                                mm = pe.transpose(ps[4 + j][:, c * P:(c + 1) * P], hid[:, par, (4 * j + c) * P:(4 * j + c + 1) * P], ident[:])
                            mm.then_inc(h_turned.h, 1)

                    def down(k, par):
                        e = pe.value_load(tile_expert_i[0:1, bass.ds(k, 1)], min_val=0, max_val=EXPERTS - 1)
                        pe.wait_ge(h_kept.h, 2 * k + 2)
                        pe.wait_ge(sel2_ready.h, k + 1)
                        pe.matmul(ps[6 + par][:, 0:F], sel2[:, par, :], bias[:, HID:HID + F], start=True, stop=False)
                        for c in range(HC):
                            mm = pe.matmul(ps[6 + par][:, 0:F], hid_t[:, par, c, :], w2[:, bass.ds(e, 1), c, :].rearrange("p a n -> p (a n)"),
                                           start=False, stop=(c == HC - 1))
                        mm.then_inc(y_done.h, 1)

                    turn_x(0, 0)
                    turn_x(1, 1)
                    pe.wait_ge(w_in.h, 16 * 2 * EXPERTS)
                    pe.wait_ge(split.h, 1)
                    up(0, 0)
                    pe.wait_ge(h_act.h, 2)
                    up(1, 1)
                    turn_h(0, 0)
                    pe.wait_ge(x_scaled.h, 1)
                    turn_x(2, 0)

                    def body(k, par):
                        pe.wait_ge(h_act.h, 2 * k + 2)
                        up(k + 1, 1 - par)
                        down(k - 1, 1 - par)
                        turn_h(k, par)
                        pe.wait_ge(x_scaled.h, k + 1)
                        turn_x(k + 2, par)

                    each(pe, 1, MT - 3, body)
                    body(MT - 3, (MT - 3) % 2)
                    pe.wait_ge(h_act.h, 2 * (MT - 2) + 2)
                    up(MT - 1, (MT - 1) % 2)
                    for k in (MT - 2, MT - 1):
                        down(k - 1, (k - 1) % 2)
                        turn_h(k, k % 2)
                    down(MT - 1, (MT - 1) % 2)

    experts()

    bigs = ExitStack()
    acc = sb("acc", [P, NT, F], F32, bigs)
    et = sb("et", [P, NT, HEADS], F32, bigs)
    WCOLS = F + 2 * HEADS
    ee = sb("ee", [P, NPAIR + G, HEADS], F32, bigs)
    edge_w = sb("edge_w", [P, 2 * HEADS], F32, bigs)
    src_term = dram("src_term", [NPAD, HEADS])

    def combine():
        with ExitStack() as ctx:
            norm = NodeNorm(ctx, "ln2")
            expert_rows = sb("y_rows", [P, 2, 2, F], F32, ctx)
            y_in = [sem(f"y_in{k}") for k in range(2)]
            y_used, slot_idx, y_first = sem("y_used"), sem("slot_idx_back"), sem("y_first")
            stage2 = sb("stage2", [P, 2, WCOLS], F32, ctx)
            wcat = sb("wcat", [P, FC, WCOLS], F32, ctx)
            attn = sb("attn", [P, 3, F], F32, ctx)
            we = sb("we", [P, F], F32, ctx)
            prod = sb("prod", [P, F], F32, ctx)
            rows_ready, attn_in, wcat_ready = sem("z2_staged"), sem("attn_in"), sem("wcat_ready")
            ft_out = [sem(f"ft_out{k}") for k in range(2)]
            ft_ready = sem("ft_ready")
            with nc.Block() as block:
                @block.sync
                def _(sp):
                    sp.dma_start(acc[:], resid.rearrange("(d p) f -> p d f", p=P)).then_inc(x_loaded.h, 16)
                    sp.dma_start(wcat[:, :, 0:F], t["L1_gnn_W_fc"].rearrange("(c p) n -> p c n", p=P)).then_inc(attn_in.h, 16)
                    for j in range(2):
                        sp.dma_start(we[j * EDIM:(j + 1) * EDIM, :], t["L1_gnn_W_e"]).then_inc(attn_in.h, 16)
                    for j, name in enumerate(("attn_h", "attn_t", "attn_e")):
                        sp.dma_start(attn[:, j, :], t[f"L1_gnn_{name}"].rearrange("(a h) d -> a (h d)", a=1).to_broadcast([P, F])).then_inc(attn_in.h, 16)
                    for d, k in node_tiles(sp):
                        sp.wait_ge(ft_ready.h, d + 1)
                        sp.dma_start(node_table[bass.ds(d * P, P), :], stage2[:, k, 0:F]).then_inc(ft_out[k].h, 16)
                        sp.dma_start(src_term[bass.ds(d * P, P), :], stage2[:, k, F:F + HEADS]).then_inc(ft_out[k].h, 16)
                    sp.wait_ge(ft_out[0].h, 32 * (NT // 2 + 1))
                    sp.wait_ge(ft_out[1].h, 32 * (NT // 2))

                @block.gpsimd
                def _(g):
                    for d, k in node_tiles(g):
                        g.wait_ge(y_used.h, d + 1)
                        g.tensor_copy(idx[:, k, 0:2], slots[:, :, bass.ds(d, 1)].rearrange("p a d -> p (a d)")).then_inc(slot_idx.h, 1)
                        g.wait_ge(slot_idx.h, d + 1)
                        g.tensor_tensor(carrier[:], psrc[:, 0:1], psrc[:, 0:1], ALU.add)
                        for j in range(2):
                            g.indirect_dma_start(expert_rows[:, k, j, :], None, slot_out,
                                                 bass.IndirectOffsetOnAxis(ap=idx[:, k, j:j + 1], axis=0)).then_inc(y_in[k].h, 16)

                @block.vector
                def _(v):
                    v.sem_inc(y_used.h, 2)
                    v.wait_ge(attn_in.h, 16 * 6)

                    def fold(w, j, dst):
                        v.tensor_tensor(prod[:], w, attn[:, j, :], ALU.mult).then_inc(v_step.h, 1)
                        v.wait_ge(v_step.h, v_step.next())
                        v.tensor_reduce(dst, prod[:].rearrange("p (h d) -> p h d", d=HD), AX.X, ALU.add).then_inc(v_step.h, 1)
                        v.wait_ge(v_step.h, v_step.next())

                    for c in range(FC):
                        for j in range(2):
                            fold(wcat[:, c, 0:F], j, wcat[:, c, F + j * HEADS:F + (j + 1) * HEADS])
                    v.memset(edge_w[:], 0.0).then_inc(v_step.h, 1)
                    v.wait_ge(v_step.h, v_step.next())
                    v.tensor_tensor(prod[:], we[:], attn[:, 2, :], ALU.mult).then_inc(v_step.h, 1)
                    v.wait_ge(v_step.h, v_step.next())
                    for j in range(2):
                        r = slice(j * EDIM, (j + 1) * EDIM)
                        v.tensor_reduce(edge_w[r, j * HEADS:(j + 1) * HEADS], prod[r, :].rearrange("p (h d) -> p h d", d=HD), AX.X, ALU.add).then_inc(v_step.h, 1)
                        v.wait_ge(v_step.h, v_step.next())
                    v.nop().then_inc(wcat_ready.h, 1)
                    v.wait_ge(x_loaded.h, x_loaded.base + 16)
                    for d, k in node_tiles(v):
                        v.wait_ge(y_in[k].h, 32 * (d // 2 + 1) if isinstance(d, int) else (d - k) * 16 + 32)
                        row = rows_of(acc, d)
                        v.scalar_tensor_tensor(row, expert_rows[:, k, 0, :], gate[:, 0, bass.ds(d, 1)], row, ALU.mult, ALU.add).then_inc(y_first.h, 1)
                        v.wait_ge(y_first.h, d + 1)
                        v.scalar_tensor_tensor(row, expert_rows[:, k, 1, :], gate[:, 1, bass.ds(d, 1)], row, ALU.mult, ALU.add).then_inc(y_used.h, 1)
                    v.wait_ge(y_used.h, NT + 2)
                    norm.stats_of(v, acc)

                    def stage_rows(d, k):
                        v.wait_ge(turned.h, turned.base + d + 1)
                        norm.rows(v, acc, stage[:, k, :], d, rows_ready)

                    def keep(d, k):
                        v.wait_ge(projected.h, projected.base + d + 1 + 2)
                        wait_earlier(v, ft_out[k], d, k, 32)
                        v.tensor_copy(et[:, bass.ds(d, 1), :].rearrange("p a h -> p (a h)"), ps[2 + k][:, F + HEADS:WCOLS])
                        v.tensor_copy(stage2[:, k, 0:F + HEADS], ps[2 + k][:, 0:F + HEADS]).then_inc(projected_out.h, 1)
                        v.wait_ge(projected_out.h, projected_out.base + d + 1 + 2)
                        v.nop().then_inc(ft_ready.h, 1)

                    two_ahead(v, stage_rows, keep)

                @block.scalar
                def _(a):
                    norm.root.scalar(a)
                    turned_to_lhs(a)

                @block.tensor
                def _(pe):
                    pe.wait_ge(wcat_ready.h, 1)
                    turn_and_multiply(pe, wcat, rows_ready, WCOLS)
            x_loaded.base += 16
            project_counted()
            stored.base -= 16 * NT

    with ExitStack() as proj:
        stage = sb("stage", [P, 2, F], F32, proj)
        lhs = sb("lhs", [P, 2, FC, P], F32, proj)
        combine()

    peak = sb("peak", [P, NT, 2 * HEADS], F32, bigs)

    def maxima():
        with ExitStack() as ctx:
            hot = sb("hot", [P, 2, G, P], F32, ctx)
            src_rows = sb("src_rows", [P, 2, G, HEADS], F32, ctx)
            edge_rows = sb("edge_rows", [P, 2, G, EDIM], F32, ctx)
            edge_t = sb("edge_t", [P, 2, G // 2, P], F32, ctx)
            logit = sb("logit", [P, 2 * G, HEADS], F32, ctx)
            logit_t = sb("logit_t", [P, P], F32, ctx)
            runmax = sb("runmax", [P, P], F32, ctx)
            cand = sb("cand", [P, 2 * G, HEADS + 1], F32, ctx)
            off = sb("off", [P, 2 * G], F32, ctx)
            best = sb("best", [P, 2 * G, HEADS], F32, ctx)
            spread = sb("spread", [P, G, P], BF16, ctx)
            first_b = sb("first_b", [P, ETB, P], BF16, ctx)
            nmax = sb("nmax", [P, NT, HEADS], F32, ctx)
            tmp = sb("max_tmp", [P, NT, HEADS], F32, ctx)
            spread_i = sb("spread_i", [P, G * P], I32, ctx)
            lane_i = sb("lane_i", [P, 1], I32, ctx)
            lane = sb("lane", [P, 1], F32, ctx)
            spread_f = sb("spread_f", [P, G * P], F32, ctx)
            edge_in = [sem(f"edge_in{h}") for h in range(2)]
            patterns, spread_set = sem("patterns"), sem("spread_set")
            edge_turned, edge_kept, edge_done = sem("edge_turned"), sem("edge_kept"), sem("edge_done")
            logit_set, logit_kept, logit_turned, logit_t_set = sem("logit_set"), sem("logit_kept"), sem("logit_turned"), sem("logit_t_set")
            scanned, run_turned, cand_set, met, best_set, maxed = sem("run_scanned"), sem("run_turned"), sem("cand_set"), sem("met"), sem("best_set"), sem("maxed")
            H2 = 2 * G * HEADS
            with nc.Block() as block:
                @block.sync
                def _(sp):
                    with sp.Fori(0, ITERS) as i:
                        for h in range(2):
                            sp.wait_ge(edge_turned.h, 2 * i + h + 1)
                            for b in range(G):
                                e0 = sp.value_load(prow[1:2, bass.ds(i * 2 * G + h * G + b, 1)], min_val=0, max_val=E - P)
                                sp.dma_start(edge_rows[:, h, b, :], t["edge_attr_64"][bass.ds(e0, P), :]).then_inc(edge_in[h].h, 16)

                @block.gpsimd
                def _(g):
                    g.iota(spread_i[:], [[2 * G, G], [1, 2 * G], [0, HEADS]], base=0, channel_multiplier=0).then_inc(patterns.h, 1)
                    g.iota(lane_i[:], [[0, 1]], base=0, channel_multiplier=1).then_inc(patterns.h, 1)
                    with g.Fori(0, ITERS) as i:
                        for h in range(2):
                            g.wait_ge(logit_set.h, 2 * i + h + 1)
                            g.tensor_copy(idx[:, h, :], psrc[:, bass.ds(i * 2 * G + h * G, G)]).then_inc(idx_ready.h, 1)
                            g.wait_ge(idx_ready.h, idx_ready.base + 2 * i + h + 1)
                            g.tensor_tensor(carrier[:], psrc[:, 0:1], psrc[:, 0:1], ALU.add)
                            for b in range(G):
                                s = h * G + b
                                g.indirect_dma_start(src_rows[:, h, b, :], None, src_term,
                                                     bass.IndirectOffsetOnAxis(ap=idx[:, h, b:b + 1], axis=0)).then_inc(row_sem[s].h, 16)

                @block.vector
                def _(v):
                    v.sem_inc(edge_turned.h, 2)
                    v.sem_inc(logit_set.h, 2)
                    v.sem_inc(logit_kept.h, 2)
                    v.memset(ee[:, NPAIR:NPAIR + G, :], 0.0).then_inc(v_step.h, 1)
                    v.wait_ge(v_step.h, v_step.next())
                    v.memset(nmax[:], -BIG).then_inc(v_step.h, 1)
                    v.wait_ge(v_step.h, v_step.next())
                    v.tensor_copy(first_b[:], first[:]).then_inc(v_step.h, 1)
                    v.wait_ge(v_step.h, v_step.next())
                    v.wait_ge(patterns.h, 2)
                    v.tensor_copy(spread_f[:], spread_i[:]).then_inc(v_step.h, 1)
                    v.wait_ge(v_step.h, v_step.next())
                    v.tensor_copy(lane[:], lane_i[:]).then_inc(v_step.h, 1)
                    v.wait_ge(v_step.h, v_step.next())
                    v.tensor_scalar(spread[:].rearrange("p g m -> p (g m)"), spread_f[:], lane[:], None, ALU.is_equal).then_inc(v_step.h, 1)
                    v.wait_ge(v_step.h, v_step.next())
                    v.nop().then_inc(spread_set.h, 1)
                    with v.Fori(0, ITERS) as i:
                        for h in range(2):
                            mark_pairs(v, hot, 2 * i + h, h)
                        for h in range(2):
                            for b in range(G):
                                v.wait_ge(row_sem[h * G + b].h, row_sem[h * G + b].base + 16 * (i + 1))
                            v.wait_ge(edge_done.h, 2 * i + h + 1)
                            v.wait_ge(logit_kept.h, 2 * i + h + 1)
                            v.tensor_tensor(logit[:, h * G:(h + 1) * G, :], ps[2 + h][:, 0:G * HEADS].rearrange("p (j e) -> p j e", e=HEADS),
                                            src_rows[:, h], ALU.add).then_inc(logit_set.h, 1)
                        v.wait_ge(logit_t_set.h, i + 1)
                        v.tensor_tensor_scan(runmax[:], ps[5][:, 0:P], logit_t[:], -BIG, ALU.add, ALU.max).then_inc(scanned.h, 1)
                        v.wait_ge(run_turned.h, i + 1)
                        last = plast[:, bass.ds(i * 2 * G, 2 * G)].rearrange("p (j a) -> p j a", a=1)
                        v.tensor_tensor(cand[:, :, 0:HEADS], ps[6][:, 0:H2].rearrange("p (j e) -> p j e", e=HEADS),
                                        last.to_broadcast([P, 2 * G, HEADS]), ALU.mult)
                        v.tensor_copy(cand[:, :, HEADS:HEADS + 1], last).then_inc(cand_set.h, 1)
                        v.wait_ge(met.h, i + 1)
                        got = ps[7][:, 0:2 * G * (HEADS + 1)].rearrange("p (j e) -> p j e", e=HEADS + 1)
                        v.tensor_scalar(off[:].rearrange("p (j a) -> p j a", a=1), got[:, :, HEADS:HEADS + 1], BIG, -BIG, ALU.mult, ALU.add).then_inc(best_set.h, 1)
                        v.wait_ge(best_set.h, 2 * i + 1)
                        v.tensor_tensor(best[:], got[:, :, 0:HEADS], off[:].rearrange("p (j a) -> p j a", a=1).to_broadcast([P, 2 * G, HEADS]), ALU.add).then_inc(best_set.h, 1)
                        v.wait_ge(best_set.h, 2 * i + 2)
                        for b in range(2 * G):
                            n = i * 2 * G + b
                            d = v.value_load(prow[0:1, bass.ds(n, 1)], min_val=0, max_val=NT - 1)
                            node = nmax[:, bass.ds(d, 1), :].rearrange("p a e -> p (a e)")
                            if b > 0:
                                v.wait_ge(maxed.h, n)
                            v.tensor_tensor(node, node, best[:, b, :], ALU.max).then_inc(maxed.h, 1)
                        v.wait_ge(maxed.h, 2 * G * i + 2 * G)
                    v.tensor_tensor(tmp[:], nmax[:], et[:], ALU.add).then_inc(v_step.h, 1)
                    v.wait_ge(v_step.h, v_step.next())
                    v.scalar_tensor_tensor(peak[:, :, HEADS:2 * HEADS], tmp[:], SLOPE, tmp[:], ALU.mult, ALU.max).then_inc(v_step.h, 1)
                    v.wait_ge(v_step.h, v_step.next())
                    v.tensor_copy(peak[:, :, 0:HEADS], et[:]).then_inc(v_step.h, 1)
                    v.wait_ge(v_step.h, v_step.next())

                @block.scalar
                def _(a):
                    with a.Fori(0, ITERS) as i:
                        for h in range(2):
                            a.wait_ge(edge_turned.h, 2 * i + h + 1 + 2)
                            a.activation(edge_t[:, h].rearrange("p j n -> p (j n)"), ps[h][:], ACT.Copy).then_inc(edge_kept.h, 1)
                        for h in range(2):
                            a.wait_ge(logit_set.h, 2 * i + h + 1 + 2)
                            a.activation(ee[:, bass.ds(i * 2 * G + h * G, G), :], logit[:, h * G:(h + 1) * G, :], ACT.Copy).then_inc(logit_kept.h, 1)
                        a.wait_ge(logit_turned.h, i + 1)
                        a.activation(logit_t[:], ps[4][:, 0:P], ACT.Copy).then_inc(logit_t_set.h, 1)

                @block.tensor
                def _(pe):
                    pe.wait_ge(spread_set.h, 1)
                    with pe.Fori(0, ITERS) as i:
                        for h in range(2):
                            pe.wait_ge(edge_in[h].h, 16 * G * (i + 1))
                            for j in range(G // 2):
                                mm = pe.transpose(ps[h][:, j * P:(j + 1) * P], edge_rows[:, h, 2 * j:2 * j + 2, :].rearrange("p a c -> p (a c)"), ident[:])
                            mm.then_inc(edge_turned.h, 1)
                        pe.matmul(ps[5][:, 0:P], spread[:, bass.ds(i % G, 1), :].rearrange("p a m -> p (a m)"),
                                  first_b[:, bass.ds(i // G, 1), :].rearrange("p a m -> p (a m)"), start=True, stop=True)
                        for h in range(2):
                            pe.wait_ge(edge_kept.h, 2 * i + h + 1)
                            for j in range(G // 2):
                                mm = pe.matmul(ps[2 + h][:, j * 2 * HEADS:(j + 1) * 2 * HEADS], edge_t[:, h, j, :], edge_w[:], start=True, stop=True)
                            mm.then_inc(edge_done.h, 1)
                        pe.wait_ge(logit_set.h, 2 * i + 2 + 2)
                        pe.transpose(ps[4][:, 0:P], logit[:].rearrange("p j e -> p (j e)"), ident[:]).then_inc(logit_turned.h, 1)
                        pe.wait_ge(scanned.h, i + 1)
                        pe.transpose(ps[6][:, 0:P], runmax[:], ident[:]).then_inc(run_turned.h, 1)
                        pe.wait_ge(cand_set.h, i + 1)
                        pe.wait_ge(onehot_ready.h, onehot_ready.base + 2 * i + 2)
                        for b in range(2 * G):
                            mm = pe.matmul(ps[7][:, b * (HEADS + 1):(b + 1) * (HEADS + 1)], hot[:, b // G, b % G, :], cand[:, b, :], start=True, stop=True)
                        mm.then_inc(met.h, 1)
            onehot_ready.base += 2 * ITERS
            idx_ready.base += 2 * ITERS
            for s in row_sem:
                s.base += 16 * ITERS

    maxima()

    SUMS = F + HEADS
    lateb = ExitStack()
    sums = sb("sums", [P, NT, SUMS], F32, lateb)

    def attend():
        with ExitStack() as ctx:
            hot = sb("hot", [P, 2, G, P], F32, ctx)
            hot_t = sb("hot_t", [P, 2, G, P], F32, ctx)
            rows = sb("rows", [P, 2 * G, F], F32, ctx)
            msg = sb("msg", [P, 2, G, SUMS], F32, ctx)
            arg = sb("arg", [P, 2, G, HEADS], F32, ctx)
            hot_turned, hot_kept, node_terms, arg_ready, weighed = sem("hot_turned"), sem("hot_kept"), sem("node_terms"), sem("arg_ready"), sem("weighed")
            arg_step, msg_ready = sem("arg_step"), sem("msg_ready")
            with nc.Block() as block:
                @block.gpsimd
                def _(g):
                    with g.Fori(0, ITERS) as i:
                        for h in range(2):
                            g.wait_ge(msg_ready.h, 2 * i + h + 1)
                            g.tensor_copy(idx[:, h, :], psrc[:, bass.ds(i * 2 * G + h * G, G)]).then_inc(idx_ready.h, 1)
                            g.wait_ge(idx_ready.h, idx_ready.base + 2 * i + h + 1)
                            g.tensor_tensor(carrier[:], psrc[:, 0:1], psrc[:, 0:1], ALU.add)
                            for b in range(G):
                                s = h * G + b
                                g.indirect_dma_start(rows[:, s, :], None, node_table,
                                                     bass.IndirectOffsetOnAxis(ap=idx[:, h, b:b + 1], axis=0)).then_inc(row_sem[s].h, 16)

                @block.vector
                def _(v):
                    v.sem_inc(msg_ready.h, 2)
                    v.memset(sums[:], 0.0).then_inc(added.h, 1)

                    def argument(q, h):
                        v.wait_ge(node_terms.h, q + 1)
                        term = ps[2 + h][:, 0:G * 2 * HEADS].rearrange("p (j e) -> p j e", e=2 * HEADS)
                        a = arg[:, h]
                        v.tensor_tensor(a, ee[:, bass.ds(q * G, G), :], term[:, :, 0:HEADS], ALU.add).then_inc(arg_step.h, 1)
                        v.wait_ge(arg_step.h, 3 * q + 1)
                        v.scalar_tensor_tensor(a, a, SLOPE, a, ALU.mult, ALU.max).then_inc(arg_step.h, 1)
                        v.wait_ge(arg_step.h, 3 * q + 2)
                        v.tensor_tensor(a, a, term[:, :, HEADS:2 * HEADS], ALU.subtract).then_inc(arg_step.h, 1)
                        v.wait_ge(arg_step.h, 3 * q + 3)
                        v.tensor_scalar(a, a, 0.0, None, ALU.min).then_inc(arg_ready.h, 1)

                    def messages(i, h):
                        q = 2 * i + h
                        v.wait_ge(weighed.h, q + 1)
                        for b in range(G):
                            v.wait_ge(row_sem[h * G + b].h, row_sem[h * G + b].base + 16 * (i + 1))
                        v.tensor_tensor(msg[:, h, :, 0:F].rearrange("p j (e d) -> p j e d", d=HD),
                                        rows[:, h * G:(h + 1) * G, :].rearrange("p j (e d) -> p j e d", d=HD),
                                        msg[:, h, :, F:SUMS].rearrange("p j (e a) -> p j e a", a=1).to_broadcast([P, G, HEADS, HD]),
                                        ALU.mult).then_inc(msg_ready.h, 1)

                    def add_sums(i, h):
                        for b in range(G):
                            n = (2 * i + h) * G + b
                            d = v.value_load(prow[0:1, bass.ds(n, 1)], min_val=0, max_val=NT - 1)
                            row = rows_of(sums, d)
                            v.wait_ge(aggregated.h, aggregated.base + 2 * G + n + 1)
                            v.wait_ge(added.h, added.base + G + n + 1)
                            v.tensor_tensor(row, row, ps[4 + b % 4][:, 0:SUMS], ALU.add).then_inc(added.h, 1)

                    mark_pairs(v, hot, 0, 0)
                    argument(0, 0)
                    with v.Fori(0, ITERS) as i:
                        v.wait_ge(aggregated.h, aggregated.base + (i + 1) * 2 * G)
                        mark_pairs(v, hot, 2 * i + 1, 1)
                        messages(i, 0)
                        argument(2 * i + 1, 1)
                        add_sums(i, 0)
                        mark_pairs(v, hot, 2 * i + 2, 0)
                        messages(i, 1)
                        argument(2 * i + 2, 0)
                        add_sums(i, 1)

                @block.scalar
                def _(a):
                    def turn_marks(q, h):
                        for j in range(2):
                            a.wait_ge(hot_turned.h, 2 * q + j + 1)
                            a.activation(hot_t[:, h, 4 * j:4 * j + 4, :].rearrange("p b n -> p (b n)"), ps[j][:], ACT.Copy).then_inc(hot_kept.h, 1)

                    def weigh(q, h):
                        a.wait_ge(arg_ready.h, q + 1)
                        a.wait_ge(aggregated.h, aggregated.base + (q + 1) * G)
                        a.activation(msg[:, h, :, F:SUMS], arg[:, h], ACT.Exp).then_inc(weighed.h, 1)

                    turn_marks(0, 0)
                    weigh(0, 0)
                    with a.Fori(0, ITERS) as i:
                        turn_marks(2 * i + 1, 1)
                        weigh(2 * i + 1, 1)
                        turn_marks(2 * i + 2, 0)
                        weigh(2 * i + 2, 0)

                @block.tensor
                def _(pe):
                    def turn_marks(q, h):
                        pe.wait_ge(onehot_ready.h, onehot_ready.base + q + 1)
                        for j in range(2):
                            if not (isinstance(q, int) and q == 0):
                                pe.wait_ge(hot_kept.h, 2 * q + j - 1)
                            for b in range(4):
                                mm = pe.transpose(ps[j][:, b * P:(b + 1) * P], hot[:, h, 4 * j + b, :], ident[:])
                            mm.then_inc(hot_turned.h, 1)

                    def spread_terms(q, h):
                        pe.wait_ge(hot_kept.h, 2 * q + 2)
                        for b in range(G):
                            d = pe.value_load(prow[0:1, bass.ds(q * G + b, 1)], min_val=0, max_val=NT - 1)
                            mm = pe.matmul(ps[2 + h][:, b * 2 * HEADS:(b + 1) * 2 * HEADS], hot_t[:, h, b, :],
                                           peak[:, bass.ds(d, 1), :].rearrange("p a e -> p (a e)"), start=True, stop=True)
                        mm.then_inc(node_terms.h, 1)

                    def sum_pairs(i, h):
                        pe.wait_ge(msg_ready.h, 2 * i + h + 1 + 2)
                        for b in range(G):
                            n = (2 * i + h) * G + b
                            pe.wait_ge(added.h, added.base + n + 1 + 4 + 1)
                            pe.matmul(ps[4 + b % 4][:, 0:SUMS], hot[:, h, b, :], msg[:, h, b, :], start=True, stop=True).then_inc(aggregated.h, 1)

                    turn_marks(0, 0)
                    spread_terms(0, 0)
                    with pe.Fori(0, ITERS) as i:
                        turn_marks(2 * i + 1, 1)
                        spread_terms(2 * i + 1, 1)
                        sum_pairs(i, 0)
                        turn_marks(2 * i + 2, 0)
                        spread_terms(2 * i + 2, 0)
                        sum_pairs(i, 1)
            gather_counted()
            added.base += 1

    attend()

    ONE = NT // 7
    BW = ONE * P
    HALF = BW // 2
    TAKE = N // 2 - 1
    assert NT % 7 == 0

    def close_attention():
        with ExitStack() as ctx:
            den = sb("den", [P, NT, HEADS], F32, ctx)
            bias = sb("gat_bias", [P, F], F32, ctx)
            part = sb("part", [P, 2, F], F32, ctx)
            divided, biased, summed = sem("divided"), sem("biased"), sem("summed")
            with nc.Block() as block:
                @block.sync
                def _(sp):
                    sp.dma_start(bias[:], t["L1_gnn_bias"].rearrange("(a h) d -> a (h d)", a=1).to_broadcast([P, F])).then_inc(loaded.h, 16)

                @block.vector
                def _(v):
                    v.tensor_scalar(den[:], sums[:, :, F:SUMS], 1.0 / BIG, None, ALU.max).then_inc(v_step.h, 1)
                    v.wait_ge(v_step.h, v_step.next())
                    v.reciprocal(den[:], den[:]).then_inc(v_step.h, 1)
                    v.wait_ge(v_step.h, v_step.next())
                    v.wait_ge(loaded.h, loaded.base + 16)
                    for d, k in node_tiles(v):
                        v.tensor_tensor(part[:, k, :].rearrange("p (h d) -> p h d", d=HD), sums[:, bass.ds(d, 1), 0:F].rearrange("p a (h d) -> p (a h) d", d=HD),
                                        den[:, bass.ds(d, 1), :].rearrange("p a (h b) -> p (a h) b", b=1).to_broadcast([P, HEADS, HD]), ALU.mult).then_inc(divided.h, 1)
                        v.tensor_tensor(rows_of(acc, d), rows_of(acc, d), bias[:], ALU.add).then_inc(biased.h, 1)
                        v.wait_ge(divided.h, d + 1)
                        v.wait_ge(biased.h, d + 1)
                        v.tensor_tensor(rows_of(acc, d), rows_of(acc, d), part[:, k, :], ALU.add).then_inc(summed.h, 1)
                    v.wait_ge(summed.h, NT)
            loaded.base += 16

    close_attention()
    lateb.close()

    zt = sb("zt", [P, FC, NPAD], F32, bigs)

    def feed_forward():
        with ExitStack() as ctx:
            norm = NodeNorm(ctx, "ln3")
            stage = sb("stage", [P, 2, F], F32, ctx)
            wr = sb("wr3", [P, FC, 1], F32, ctx)
            br = sb("br3", [P, 1], F32, ctx)
            w1 = sb("w1_3", [P, FC, HID], F32, ctx)
            b1 = sb("b1_3", [P, HC], F32, ctx)
            w2 = sb("w2_3", [P, HC, F], F32, ctx)
            b2 = sb("b2_3", [P, F], F32, ctx)
            hid = sb("hid3", [P, HC, BW], F32, ctx)
            part = sb("part3", [P, 2, F], F32, ctx)
            weight = sb("weight", [P, NT], F32, ctx)
            key = sb("key", [P, NT], I32, ctx)
            sign = sb("sign", [P, NT], I32, ctx)
            half_i = sb("half_i", [P, 2, NT], I32, ctx)
            half = sb("half", [P, 2, NT], F32, ctx)
            node_i = sb("node3_i", [P, NT], I32, ctx)
            valid = sb("valid3", [P, NT], F32, ctx)
            junk = sb("junk3", [P, NT], F32, ctx)
            count = sb("count3", [P, 1], F32, ctx)
            cut = sb("cut", [P, 1], F32, ctx)
            trial = sb("trial", [P, 1], F32, ctx)
            reach = sb("reach", [P, 1], F32, ctx)
            quota = sb("quota", [P, 2], F32, ctx)
            above = sb("above", [P, NT], F32, ctx)
            ties = sb("ties", [P, NT], F32, ctx)
            runs = sb("runs", [P, NT], F32, ctx)
            taken = sb("taken", [P, NT], F32, ctx)
            rows_ready, zt_set, weights_in, numbered = sem("z3_staged"), sem("zt_set"), sem("weights_in"), sem("numbered3")
            routed, counted, summed = sem("routed"), sem("counted3"), sem("count_summed")
            up_done, up_act, down_done, part_set, out_set = sem("up_done"), sem("up_act"), sem("down_done"), sem("part_set"), sem("out_set")
            scaled, freed = sem("scaled"), sem("hid_freed")
            with nc.Block() as block:
                @block.sync
                def _(sp):
                    for c in range(FC):
                        sp.dma_start(wr[:, c, :], t["L1_ffn_wr"][c * P:(c + 1) * P, :]).then_inc(weights_in.h, 16)
                    sp.dma_start(br[:], t["L1_ffn_br"].rearrange("(a e) -> a e", a=1).to_broadcast([P, 1])).then_inc(weights_in.h, 16)
                    sp.dma_start(w1[:], t["L1_ffn_w1"].rearrange("(c p) n -> p c n", p=P)).then_inc(weights_in.h, 16)
                    with nc.allow_non_contiguous_dma("bias of the hidden units onto partitions"):
                        sp.dma_start(b1[:], t["L1_ffn_b1"].rearrange("(c p) -> p c", p=P)).then_inc(weights_in.h, 16)
                    sp.dma_start(w2[:], t["L1_ffn_w2"].rearrange("(c p) n -> p c n", p=P)).then_inc(weights_in.h, 16)
                    sp.dma_start(b2[:], t["L1_ffn_b2"].rearrange("(a n) -> a n", a=1).to_broadcast([P, F])).then_inc(weights_in.h, 16)
                    with sp.Fori(0, NT - 1) as d:
                        sp.wait_ge(out_set.h, d + 2)
                        sp.dma_start(out[bass.ds(d * P, P), :], rows_of(acc, d)).then_inc(stored.h, 16)
                    sp.wait_ge(out_set.h, NT + 1)
                    sp.dma_start(out[(NT - 1) * P:N, :], acc[0:NLAST, NT - 1, :]).then_inc(stored.h, 16)
                    sp.wait_ge(stored.h, stored.base + 16 * NT)

                @block.gpsimd
                def _(g):
                    g.iota(node_i[:], [[P, NT]], base=0, channel_multiplier=1).then_inc(numbered.h, 1)

                @block.vector
                def _(v):
                    v.sem_inc(part_set.h, 2)
                    v.sem_inc(out_set.h, 1)
                    norm.stats_of(v, acc)

                    def stage_rows(d, k):
                        v.wait_ge(turned.h, turned.base + d + 1)
                        norm.rows(v, acc, stage[:, k, :], d, rows_ready)
                        v.wait_ge(rows_ready.h, d + 1)
                        v.tensor_tensor(rows_of(acc, d), rows_of(acc, d), stage[:, k, :], ALU.add).then_inc(scaled.h, 1)

                    for d, k in node_tiles(v):
                        stage_rows(d, k)
                    v.wait_ge(numbered.h, 1)
                    v.tensor_copy(junk[:], node_i[:]).then_inc(v_step.h, 1)
                    v.wait_ge(v_step.h, v_step.next())
                    v.tensor_scalar(valid[:], junk[:], float(N), None, ALU.is_lt).then_inc(v_step.h, 1)
                    v.wait_ge(v_step.h, v_step.next())
                    v.wait_ge(routed.h, 1)
                    v.tensor_scalar(weight[:], ps[2][:, 0:NT], br[:], 0.0, ALU.add, ALU.add).then_inc(v_step.h, 1)
                    v.wait_ge(v_step.h, v_step.next())
                    bits = weight[:].bitcast(I32)
                    v.tensor_scalar(sign[:], bits, 31, None, ALU.arith_shift_right).then_inc(v_step.h, 1)
                    v.wait_ge(v_step.h, v_step.next())
                    v.tensor_scalar(sign[:], sign[:], -(1 << 31), None, ALU.bitwise_or).then_inc(v_step.h, 1)
                    v.wait_ge(v_step.h, v_step.next())
                    v.tensor_tensor(key[:], bits, sign[:], ALU.bitwise_xor).then_inc(v_step.h, 1)
                    v.wait_ge(v_step.h, v_step.next())
                    v.tensor_scalar(half_i[:, 0, :], key[:], 16, 0xFFFF, ALU.arith_shift_right, ALU.bitwise_and).then_inc(v_step.h, 1)
                    v.wait_ge(v_step.h, v_step.next())
                    v.tensor_scalar(half_i[:, 1, :], key[:], 0xFFFF, None, ALU.bitwise_and).then_inc(v_step.h, 1)
                    v.wait_ge(v_step.h, v_step.next())
                    v.tensor_copy(half[:], half_i[:]).then_inc(v_step.h, 1)
                    v.wait_ge(v_step.h, v_step.next())

                    def masked(x, mask):
                        v.scalar_tensor_tensor(x, x, 1.0, mask, ALU.add, ALU.mult).then_inc(v_step.h, 1)
                        v.wait_ge(v_step.h, v_step.next())
                        v.tensor_scalar(x, x, -1.0, None, ALU.add).then_inc(v_step.h, 1)
                        v.wait_ge(v_step.h, v_step.next())

                    calls = [0]

                    def total(x, op, bound):
                        v.tensor_scalar(junk[:], x, bound, 0.0, op, ALU.add, accum_out=count[:]).then_inc(v_step.h, 1)
                        v.wait_ge(v_step.h, v_step.next())
                        v.nop().then_inc(counted.h, 1)
                        calls[0] += 1
                        v.wait_ge(summed.h, calls[0])
                        return ps[3][:, 0:1]

                    def kth(x, goal):
                        v.memset(cut[:], 0.0).then_inc(v_step.h, 1)
                        v.wait_ge(v_step.h, v_step.next())
                        for bit in range(15, -1, -1):
                            v.tensor_scalar(trial[:], cut[:], float(1 << bit), None, ALU.add).then_inc(v_step.h, 1)
                            v.wait_ge(v_step.h, v_step.next())
                            n = total(x, ALU.is_ge, trial[:])
                            v.tensor_tensor(reach[:], n, goal, ALU.is_ge).then_inc(v_step.h, 1)
                            v.wait_ge(v_step.h, v_step.next())
                            v.scalar_tensor_tensor(cut[:], reach[:], float(1 << bit), cut[:], ALU.mult, ALU.add).then_inc(v_step.h, 1)
                            v.wait_ge(v_step.h, v_step.next())

                    masked(half[:, 0, :], valid[:])
                    v.memset(quota[:], float(TAKE)).then_inc(v_step.h, 1)
                    v.wait_ge(v_step.h, v_step.next())
                    kth(half[:, 0, :], quota[:, 0:1])
                    n = total(half[:, 0, :], ALU.is_gt, cut[:])
                    v.tensor_tensor(quota[:, 1:2], quota[:, 0:1], n, ALU.subtract).then_inc(v_step.h, 1)
                    v.wait_ge(v_step.h, v_step.next())
                    v.tensor_scalar(above[:], half[:, 0, :], cut[:], None, ALU.is_gt).then_inc(v_step.h, 1)
                    v.wait_ge(v_step.h, v_step.next())
                    v.tensor_scalar(ties[:], half[:, 0, :], cut[:], None, ALU.is_equal).then_inc(v_step.h, 1)
                    v.wait_ge(v_step.h, v_step.next())
                    masked(half[:, 1, :], ties[:])
                    kth(half[:, 1, :], quota[:, 1:2])
                    n = total(half[:, 1, :], ALU.is_gt, cut[:])
                    v.tensor_tensor(quota[:, 1:2], quota[:, 1:2], n, ALU.subtract).then_inc(v_step.h, 1)
                    v.wait_ge(v_step.h, v_step.next())
                    v.tensor_scalar(junk[:], half[:, 1, :], cut[:], None, ALU.is_gt).then_inc(v_step.h, 1)
                    v.wait_ge(v_step.h, v_step.next())
                    v.tensor_tensor(above[:], above[:], junk[:], ALU.add).then_inc(v_step.h, 1)
                    v.wait_ge(v_step.h, v_step.next())
                    v.tensor_scalar(ties[:], half[:, 1, :], cut[:], None, ALU.is_equal).then_inc(v_step.h, 1)
                    v.wait_ge(v_step.h, v_step.next())
                    v.nop().then_inc(counted.h, 1)
                    calls[0] += 1
                    v.wait_ge(summed.h, calls[0])
                    v.tensor_copy(taken[:], ps[3][:, 64:64 + NT]).then_inc(v_step.h, 1)
                    v.wait_ge(v_step.h, v_step.next())
                    v.tensor_tensor_scan(runs[:], ones[:, 0:NT], taken[:], 0.0, ALU.mult, ALU.add).then_inc(v_step.h, 1)
                    v.wait_ge(v_step.h, v_step.next())
                    v.tensor_tensor(runs[:], runs[:], taken[:], ALU.subtract).then_inc(v_step.h, 1)
                    v.wait_ge(v_step.h, v_step.next())
                    v.tensor_tensor(runs[:], runs[:], ps[3][:, 0:NT], ALU.add).then_inc(v_step.h, 1)
                    v.wait_ge(v_step.h, v_step.next())
                    v.tensor_scalar(runs[:], runs[:], quota[:, 1:2], None, ALU.is_lt).then_inc(v_step.h, 1)
                    v.wait_ge(v_step.h, v_step.next())
                    v.tensor_tensor(ties[:], ties[:], runs[:], ALU.mult).then_inc(v_step.h, 1)
                    v.wait_ge(v_step.h, v_step.next())
                    v.tensor_tensor(taken[:], above[:], ties[:], ALU.add).then_inc(v_step.h, 1)
                    v.wait_ge(v_step.h, v_step.next())
                    v.tensor_tensor(weight[:], weight[:], taken[:], ALU.mult).then_inc(v_step.h, 1)
                    v.wait_ge(v_step.h, v_step.next())
                    v.wait_ge(scaled.h, NT)
                    with v.Fori(0, NT // ONE) as blk:
                        for j in range(ONE):
                            d = blk * ONE + j
                            k = j % 2
                            v.wait_ge(down_done.h, d + 1)
                            if j == 0:
                                v.wait_ge(out_set.h, d + 1)
                            v.tensor_tensor(part[:, k, :], ps[6 + k][:, 0:F], b2[:], ALU.add).then_inc(part_set.h, 1)
                            v.wait_ge(part_set.h, d + 1 + 2)
                            v.scalar_tensor_tensor(rows_of(acc, d), part[:, k, :], weight[:, bass.ds(d, 1)], rows_of(acc, d), ALU.mult, ALU.add).then_inc(out_set.h, 1)

                @block.scalar
                def _(a):
                    norm.root.scalar(a)
                    for d, k in node_tiles(a):
                        a.wait_ge(turned.h, turned.base + d + 1 + 2)
                        a.activation(zt[:, :, bass.ds(d * P, P)], ps[k][:, 0:F].rearrange("p (c n) -> p c n", c=FC), ACT.Copy).then_inc(turned_out.h, 1)
                    a.wait_ge(weights_in.h, 16 * (5 + FC))
                    with a.Fori(0, NT // ONE) as blk:
                        a.wait_ge(freed.h, blk + 1)
                        for c in range(HC):
                            for j in range(2):
                                a.wait_ge(up_done.h, blk * 2 * HC + 2 * c + j + 1)
                                a.activation(hid[:, c, j * HALF:(j + 1) * HALF], ps[4 + j][:, 0:HALF], ACT.Gelu_apprx_tanh, bias=b1[:, c:c + 1]).then_inc(up_act.h, 1)

                @block.tensor
                def _(pe):
                    pe.sem_inc(freed.h, 1)
                    pe.sem_inc(up_act.h, 2)
                    for d, k in node_tiles(pe):
                        turn_staged(pe, stage, d, k, rows_ready)
                    pe.wait_ge(turned_out.h, turned_out.base + NT + 2)
                    pe.wait_ge(weights_in.h, 16 * (5 + FC))
                    for d in range(NT):
                        for c in range(FC):
                            mm = pe.matmul(ps[2][:, d:d + 1], zt[:, c, d * P:(d + 1) * P], wr[:, c, :], start=(c == 0), stop=(c == FC - 1))
                    mm.then_inc(routed.h, 1)
                    for n in range(2 * 17):
                        pe.wait_ge(counted.h, n + 1)
                        pe.matmul(ps[3][:, 0:1], ones[:], count[:], start=True, stop=True).then_inc(summed.h, 1)
                    pe.wait_ge(counted.h, 2 * 17 + 1)
                    pe.matmul(ps[3][:, 0:NT], excl[:], ties[:], start=True, stop=True)
                    pe.matmul(ps[3][:, 64:64 + NT], ones[:], ties[:], start=True, stop=True).then_inc(summed.h, 1)
                    with pe.Fori(0, NT // ONE) as blk:
                        for c in range(HC):
                            for j in range(2):
                                pe.wait_ge(up_act.h, blk * 2 * HC + 2 * c + j + 1)
                                for f in range(FC):
                                    mm = pe.matmul(ps[4 + j][:, 0:HALF], w1[:, f, c * P:(c + 1) * P], zt[:, f, bass.ds(blk * BW + j * HALF, HALF)], start=(f == 0), stop=(f == FC - 1))
                                mm.then_inc(up_done.h, 1)
                        pe.wait_ge(up_act.h, (blk + 1) * 2 * HC + 2)
                        for j in range(ONE):
                            pe.wait_ge(part_set.h, blk * ONE + j + (2 if j == 0 else 1))
                            for c in range(HC):
                                mm = pe.matmul(ps[6 + j % 2][:, 0:F], hid[:, c, j * P:(j + 1) * P], w2[:, c, :], start=(c == 0), stop=(c == HC - 1))
                            mm.then_inc(down_done.h, 1)
                        pe.drain().then_inc(freed.h, 1)
            turned.base += NT
            turned_out.base += NT
            stored.base += 16 * NT

    def turn_staged(pe, stage, d, k, rows_ready):
        pe.wait_ge(rows_ready.h, d + 1)
        pe.wait_ge(turned_out.h, turned_out.base + d + 1)
        for c in range(FC):
            mm = pe.transpose(ps[k][:, c * P:(c + 1) * P], stage[:, k, c * P:(c + 1) * P], ident[:])
        mm.then_inc(turned.h, 1)

    feed_forward()
    bigs.close()


_OUT = ((N, F), "float32")


def kernel(**inputs):
    import numpy as _np
    import concourse.bacc as _bacc
    from concourse import mybir as _mybir
    from concourse.bass_utils import run_bass_kernel_spmd as _run

    nc = _bacc.Bacc("TRN2", target_bir_lowering=False, num_devices=1)
    arrays, tensors = {}, {}
    for name, value in inputs.items():
        a = _np.ascontiguousarray(value)
        arrays[f"in_{name}_dram"] = a
        tensors[name] = nc.dram_tensor(f"in_{name}_dram", a.shape, _mybir.dt.from_np(a.dtype), kind="ExternalInput").ap()
    shape, dtype = _OUT
    out = nc.dram_tensor("out_0_dram", shape, _mybir.dt.from_np(_np.dtype(dtype)), kind="ExternalOutput").ap()
    build(nc, tensors, out)
    r = _run(nc, [arrays], core_ids=[0])
    return r.results[0]["out_0_dram"]
```

```python
from contextlib import ExitStack

import concourse.bass as bass
from concourse import mybir
import numpy as np

F32 = mybir.dt.float32
BF16 = mybir.dt.bfloat16
I32 = mybir.dt.int32
ALU = mybir.AluOpType
ACT = mybir.ActivationFunctionType
AX = mybir.AxisListType

P = 128
N = 6250
E = 100000
F = 256
FC = F // P
NT = -(-N // P)
NPAD = NT * P
NLAST = N - (NT - 1) * P
ET = -(-E // P)
ETB = -(-ET // P)
G = 8
ITERS = -(-(ET + NT - 1) // (2 * G))
NPAIR = ITERS * 2 * G
PCOL = ETB * P
NODST = 1 << 20
BIG = 1.0e30
EPS = 1e-5
HEADS = 8
HD = F // HEADS
EDIM = 64
EXPERTS = 8
HID = 1024
HC = HID // P
SLOPE = 0.2


class Sem:

    def __init__(self, handle):
        self.h, self.base = handle, 0

    def next(self):
        self.base += 1
        return self.base


def node_tiles(eng):
    with eng.Fori(0, NT // 2) as i:
        yield 2 * i, 0
        yield 2 * i + 1, 1
    for d in range(NT // 2 * 2, NT):
        yield d, d % 2


def two_ahead(eng, early, late):
    early(0, 0)
    early(1, 1)
    loops = (NT - 2) // 2
    for k in range(2):
        early(2 + k, k)
        late(k, k)
    with eng.Fori(1, loops) as i:
        for k in range(2):
            early(2 * i + 2 + k, k)
            late(2 * i + k, k)
    for d in range(2 * loops, NT):
        if d + 2 < NT:
            early(d + 2, d % 2)
        late(d, d % 2)


def node_tiles_apart(eng):
    yield 0, 0
    yield 1, 1
    with eng.Fori(1, NT // 2) as i:
        yield 2 * i, 0
        yield 2 * i + 1, 1
    for d in range(NT // 2 * 2, NT):
        yield d, d % 2


def wait_earlier(eng, sem, d, k, each):
    if not isinstance(d, int):
        eng.wait_ge(sem.h, sem.base + (d - k) * (each // 2))
    elif d >= 2:
        eng.wait_ge(sem.h, sem.base + d // 2 * each)


def build(nc, t, out):
    with ExitStack() as top:
        _build(nc, t, out, top)


def _build(nc, t, out, top):
    uses = {}

    def sb(name, shape, dt=F32, ctx=top):
        uses[name] = uses.get(name, 0) + 1
        return ctx.enter_context(nc.sbuf_tensor(f"{name}_{uses[name]}", shape, dt))

    def sem(name):
        return Sem(top.enter_context(nc.semaphore(name)))

    class PhaseSems:

        def __enter__(self):
            self.used = []
            return self

        def __call__(self, name):
            self.used.append(nc.alloc_semaphore(name=name))
            return Sem(self.used[-1])

        def __exit__(self, *failed):
            if not any(failed):
                nc.clear_and_free_semaphores(self.used)
                nc.all_engine_barrier()

    def dram(name, shape, dt=F32):
        return nc.dram_tensor(name, shape, dt, kind="Internal").ap()

    ps = [top.enter_context(nc.psum_tensor(f"ps{i}", [P, 512], F32)) for i in range(8)]

    ident = sb("ident", [P, P])
    iota_f = sb("iota_f", [P, P])
    ones = sb("ones", [P, P])
    excl = sb("excl", [P, P])
    psrc = sb("psrc", [P, PCOL], I32)
    pdl = sb("pdl", [P, PCOL])
    plast = sb("plast", [P, PCOL])
    run_start = sb("run_start", [P, ETB, P], BF16)
    prow = sb("prow", [2, PCOL], I32)
    dinv = sb("dinv", [P, NT])
    change = sb("change", [P, NPAIR // G, G + 1])
    idx = sb("idx", [P, 4, G], I32)
    carrier = sb("carrier", [P, 1], I32)

    MT = -(-(2 * N) // P) + EXPERTS
    MT += MT % 2
    CAP = MT * P
    slot_rows = dram("slot_rows", [CAP + 2 * P, F])
    slot_out = dram("slot_out", [CAP + 2 * P, F])
    resid = dram("resid", [NPAD, F])
    slots = sb("slots", [P, 2, NT], I32)
    gate = sb("gate", [P, 2, NT], F32)
    tile_expert = sb("tile_expert", [P, MT], F32)
    tile_expert_i = sb("tile_expert_i", [1, MT], I32)

    edge_table = dram("edge_table", [PCOL, 2 * P + 1])
    node_table = dram("node_table", [NPAD, F])
    HROW = HD + 1
    attn_table = dram("attn_table", [NPAD, HEADS * HROW])
    ee_table = dram("ee_table", [P, NPAIR * HEADS])

    v_step = sem("v_step")
    row_sem = [sem(f"row_landed{s}") for s in range(2 * G)]
    idx_ready = sem("idx_ready")
    onehot_ready, aggregated, added = sem("onehot_ready"), sem("aggregated"), sem("added")
    loaded, stored, x_loaded = sem("loaded"), sem("stored"), sem("x_loaded")
    turned, turned_out = sem("turned"), sem("turned_out")
    projected, projected_out = sem("projected"), sem("projected_out")
    credit = {aggregated: 2 * G, added: G, turned: 2, turned_out: 2, projected: 2, projected_out: 2}

    root_ready, root_done = sem("root_ready"), sem("root_done")
    roots = [0]

    class Rsqrt:

        def __init__(self, var, res, tmp):
            self.var, self.res, self.tmp, self.n = var, res, tmp, roots[0] + 1
            roots[0] += 1

        def scalar(self, a):
            a.wait_ge(root_ready.h, self.n)
            a.activation(self.res, self.var, ACT.Sqrt).then_inc(root_done.h, 1)

        def vector(self, v):
            var, res, tmp = self.var, self.res, self.tmp
            v.nop().then_inc(root_ready.h, 1)
            v.wait_ge(root_done.h, self.n)
            v.reciprocal(tmp, res).then_inc(v_step.h, 1)
            v.wait_ge(v_step.h, v_step.next())
            v.tensor_tensor(res, tmp, tmp, ALU.mult).then_inc(v_step.h, 1)
            v.wait_ge(v_step.h, v_step.next())
            v.tensor_tensor(res, res, var, ALU.mult).then_inc(v_step.h, 1)
            v.wait_ge(v_step.h, v_step.next())
            v.tensor_scalar(res, res, -0.5, 1.5, ALU.mult, ALU.add).then_inc(v_step.h, 1)
            v.wait_ge(v_step.h, v_step.next())
            v.tensor_tensor(res, res, tmp, ALU.mult).then_inc(v_step.h, 1)
            v.wait_ge(v_step.h, v_step.next())

    def rows_of(big, d):
        return big[:, bass.ds(d, 1), :].rearrange("p a f -> p (a f)")

    def in_registers(eng, row, most):
        return nc.values_load_multi_w_load_instructions(row, [eng.engine], min_val=0, max_val=most,
                                                        skip_runtime_bounds_check_because="held to that range on the chip")[1]

    def node_tiles_of(eng, q):
        return in_registers(eng, prow[0:1, bass.ds(q * G, G)], NT - 1)

    def edge_tables():
        with ExitStack() as ctx, PhaseSems() as sem:
            iota_i = sb("iota_i", [P, P], I32, ctx)
            col_i = sb("col_i", [P, 1], I32, ctx)
            pv_i = sb("pv_i", [P, ETB], I32, ctx)
            col_f = sb("col_f", [P, 1], F32, ctx)
            pv = sb("pv", [P, ETB], F32, ctx)
            incl = sb("incl", [P, P], F32, ctx)
            edges_i = sb("edges_i", [P, ETB, 2, P], I32, ctx)
            edges_f = sb("edges_f", [P, ETB, 2 * P + 1], F32, ctx)
            tmp = sb("tmp", [P, ETB, P], F32, ctx)
            mm = sb("mm", [P, 2, ETB], F32, ctx)
            mm_i = sb("mm_i", [P, 2, ETB], I32, ctx)
            small = sb("small", [P, 8, ETB], F32, ctx)
            cumrow = sb("cumrow", [P, PCOL], F32, ctx)
            junk = sb("junk", [P, PCOL], F32, ctx)
            tile_of = sb("tile_of", [P, ETB], F32, ctx)
            tile_i = sb("tile_i", [P, ETB], I32, ctx)
            pair_edges = sb("pair_edges", [P, ETB, 2 * P + 1], F32, ctx)
            pair_dst = sb("pair_dst", [P, ETB, P], F32, ctx)
            lastf = sb("lastf", [P, ETB, P], F32, ctx)
            drow = sb("drow", [P, ETB, 2], F32, ctx)
            consts, padded, edges_in = sem("consts"), sem("padded"), sem("edges_in")
            counted, scanned, spread, spread_done = sem("counted"), sem("scanned"), sem("spread"), sem("spread_done")
            table_ready, tiles_found, pairs_in = sem("table_ready"), sem("tiles_found"), sem("pairs_in")
            pairs_ready, pairs_turned = sem("pairs_ready"), sem("pairs_turned")
            full = (ETB - 1) * P * P
            lastb = ETB - 1
            rows = (E - full) // P
            rest = E - full - rows * P

            block = nc.Block()
            with block as block:
                @block.gpsimd
                def _(g):
                    g.iota(iota_i[:], [[1, P]], base=0, channel_multiplier=0).then_inc(consts.h, 1)
                    g.iota(col_i[:], [[0, 1]], base=0, channel_multiplier=1).then_inc(consts.h, 1)
                    g.iota(pv_i[:], [[P, ETB]], base=0, channel_multiplier=1).then_inc(consts.h, 1)
                    g.memset(edges_i[:, lastb, 0, :], 0).then_inc(padded.h, 1)
                    g.memset(edges_i[:, lastb, 1, :], NODST).then_inc(padded.h, 1)
                    g.memset(ones[:], 1.0).then_inc(consts.h, 1)
                    g.wait_ge(tiles_found.h, 1)
                    g.wait_ge(stored.h, stored.base + 16)
                    for b in range(ETB):
                        g.indirect_dma_start(pair_edges[:, b, :], None, edge_table,
                                             bass.IndirectOffsetOnAxis(ap=tile_i[:, b:b + 1], axis=0)).then_inc(pairs_in.h, 16)

                @block.sync
                def _(sp):
                    sp.wait_ge(padded.h, 2)
                    for k, a in enumerate((t["src"], t["dst"])):
                        sp.dma_start(edges_i[:, 0:lastb, k, :], a[0:full].rearrange("(b p l) -> p b l", p=P, l=P)).then_inc(edges_in.h, 16)
                        sp.dma_start(edges_i[0:rows, lastb, k, :], a[full:full + rows * P].rearrange("(p l) -> p l", l=P)).then_inc(edges_in.h, 16)
                        sp.dma_start(edges_i[rows:rows + 1, lastb, k, P - rest:P], a[E - rest:E].rearrange("(p l) -> p l", p=1)).then_inc(edges_in.h, 16)
                    sp.wait_ge(table_ready.h, 1)
                    sp.dma_start(edge_table.rearrange("(b p) c -> p b c", p=P), edges_f[:]).then_inc(stored.h, 16)

                @block.vector
                def _(v):
                    for s, n in credit.items():
                        v.sem_inc(s.h, n)
                    v.wait_ge(consts.h, 4)
                    v.tensor_copy(iota_f[:], iota_i[:]).then_inc(v_step.h, 1)
                    v.wait_ge(v_step.h, v_step.next())
                    v.tensor_copy(col_f[:], col_i[:]).then_inc(v_step.h, 1)
                    v.wait_ge(v_step.h, v_step.next())
                    v.tensor_copy(pv[:], pv_i[:]).then_inc(v_step.h, 1)
                    v.wait_ge(v_step.h, v_step.next())
                    v.tensor_scalar(ident[:], iota_f[:], col_f[:], None, ALU.is_equal).then_inc(v_step.h, 1)
                    v.wait_ge(v_step.h, v_step.next())
                    v.tensor_scalar(excl[:], iota_f[:], col_f[:], None, ALU.is_gt).then_inc(v_step.h, 1)
                    v.wait_ge(v_step.h, v_step.next())
                    v.tensor_scalar(incl[:], iota_f[:], col_f[:], None, ALU.is_ge).then_inc(v_step.h, 1)
                    v.wait_ge(v_step.h, v_step.next())
                    v.wait_ge(edges_in.h, 6 * 16)
                    v.tensor_copy(edges_f[:, :, 0:2 * P], edges_i[:].rearrange("p b k l -> p b (k l)")).then_inc(v_step.h, 1)
                    v.wait_ge(v_step.h, v_step.next())
                    dst = edges_f[:, :, P:2 * P]
                    v.scalar_tensor_tensor(tmp[:], dst, float(NODST // 2), dst, ALU.is_lt, ALU.mult).then_inc(v_step.h, 1)
                    v.wait_ge(v_step.h, v_step.next())
                    v.tensor_reduce(mm[:, 0, :], dst, AX.X, ALU.min).then_inc(v_step.h, 1)
                    v.wait_ge(v_step.h, v_step.next())
                    v.tensor_reduce(mm[:, 1, :], tmp[:], AX.X, ALU.max).then_inc(v_step.h, 1)
                    v.wait_ge(v_step.h, v_step.next())
                    valid, cnt, tot, cum, off = (small[:, k, :] for k in range(5))
                    v.tensor_scalar(valid, mm[:, 0, :], float(NODST // 2), None, ALU.is_lt).then_inc(v_step.h, 1)
                    v.wait_ge(v_step.h, v_step.next())
                    v.tensor_copy(mm_i[:], mm[:]).then_inc(v_step.h, 1)
                    v.wait_ge(v_step.h, v_step.next())
                    v.tensor_scalar(mm_i[:], mm_i[:], 7, None, ALU.arith_shift_right).then_inc(v_step.h, 1)
                    v.wait_ge(v_step.h, v_step.next())
                    v.tensor_copy(mm[:], mm_i[:]).then_inc(v_step.h, 1)
                    v.wait_ge(v_step.h, v_step.next())
                    v.tensor_tensor(cnt, mm[:, 1, :], mm[:, 0, :], ALU.subtract).then_inc(v_step.h, 1)
                    v.wait_ge(v_step.h, v_step.next())
                    v.scalar_tensor_tensor(cnt, cnt, 1.0, valid, ALU.add, ALU.mult).then_inc(v_step.h, 1)
                    v.wait_ge(v_step.h, v_step.next())
                    v.nop().then_inc(counted.h, 1)
                    v.wait_ge(scanned.h, 1)
                    v.tensor_copy(tot, ps[0][:, 16:16 + ETB]).then_inc(v_step.h, 1)
                    v.wait_ge(v_step.h, v_step.next())
                    v.tensor_tensor_scan(cum, ones[:, 0:ETB], tot, 0.0, ALU.mult, ALU.add).then_inc(v_step.h, 1)
                    v.wait_ge(v_step.h, v_step.next())
                    v.tensor_tensor(cum, cum, ps[0][:, 0:ETB], ALU.add).then_inc(v_step.h, 1)
                    v.wait_ge(v_step.h, v_step.next())
                    v.tensor_tensor(cum, cum, tot, ALU.subtract).then_inc(v_step.h, 1)
                    v.wait_ge(v_step.h, v_step.next())
                    v.tensor_tensor(off, cum, cnt, ALU.subtract).then_inc(v_step.h, 1)
                    v.wait_ge(v_step.h, v_step.next())
                    v.tensor_tensor(off, mm[:, 0, :], off, ALU.subtract).then_inc(v_step.h, 1)
                    v.wait_ge(v_step.h, v_step.next())
                    v.tensor_tensor(edges_f[:, :, 2 * P], off, valid, ALU.mult).then_inc(v_step.h, 1)
                    v.wait_ge(v_step.h, v_step.next())
                    v.nop().then_inc(table_ready.h, 1)
                    v.tensor_tensor(tmp[:], ident[:].rearrange("p (b l) -> p b l", b=1).to_broadcast([P, ETB, P]),
                                    cum.rearrange("p (b l) -> p b l", l=1).to_broadcast([P, ETB, P]), ALU.mult).then_inc(v_step.h, 1)
                    v.wait_ge(v_step.h, v_step.next())
                    v.nop().then_inc(spread.h, 1)
                    v.wait_ge(spread_done.h, 1)
                    v.tensor_copy(cumrow[:, 0:512], ps[1][:]).then_inc(v_step.h, 1)
                    v.wait_ge(v_step.h, v_step.next())
                    v.tensor_copy(cumrow[:, 512:PCOL], ps[2][:, 0:PCOL - 512]).then_inc(v_step.h, 1)
                    v.wait_ge(v_step.h, v_step.next())
                    for b in range(ETB):
                        v.tensor_scalar(junk[:], cumrow[:], pv[:, b:b + 1], 0.0, ALU.is_le, ALU.add, accum_out=tile_of[:, b:b + 1]).then_inc(v_step.h, 1)
                        v.wait_ge(v_step.h, v_step.next())
                    v.tensor_scalar(tile_of[:], tile_of[:], float(PCOL - 1), None, ALU.min).then_inc(v_step.h, 1)
                    v.wait_ge(v_step.h, v_step.next())
                    v.tensor_copy(tile_i[:], tile_of[:]).then_inc(v_step.h, 1)
                    v.wait_ge(v_step.h, v_step.next())
                    v.nop().then_inc(tiles_found.h, 1)
                    v.wait_ge(pairs_in.h, 16 * ETB)
                    dp = drow[:, :, 0]
                    v.tensor_tensor(dp, pv[:], pair_edges[:, :, 2 * P], ALU.add).then_inc(v_step.h, 1)
                    v.wait_ge(v_step.h, v_step.next())
                    v.tensor_scalar(dp, dp, float(NT - 1), 0.0, ALU.min, ALU.max).then_inc(v_step.h, 1)
                    v.wait_ge(v_step.h, v_step.next())
                    v.tensor_scalar(small[:, 5, :], dp, float(P), None, ALU.mult).then_inc(v_step.h, 1)
                    v.wait_ge(v_step.h, v_step.next())
                    v.tensor_scalar(drow[:, :, 1], tile_of[:], float(P), float(E - P), ALU.mult, ALU.min).then_inc(v_step.h, 1)
                    v.wait_ge(v_step.h, v_step.next())
                    v.tensor_tensor(pair_dst[:], pair_edges[:, :, P:2 * P],
                                    small[:, 5, :].rearrange("p (b l) -> p b l", l=1).to_broadcast([P, ETB, P]), ALU.subtract).then_inc(v_step.h, 1)
                    v.wait_ge(v_step.h, v_step.next())
                    v.memset(lastf[:], 1.0).then_inc(v_step.h, 1)
                    v.wait_ge(v_step.h, v_step.next())
                    v.memset(run_start[:], -BIG).then_inc(v_step.h, 1)
                    v.wait_ge(v_step.h, v_step.next())
                    v.tensor_tensor(lastf[:, :, 0:P - 1], pair_dst[:, :, 0:P - 1], pair_dst[:, :, 1:P], ALU.not_equal).then_inc(v_step.h, 1)
                    v.wait_ge(v_step.h, v_step.next())
                    v.tensor_scalar(run_start[:, :, 1:P], lastf[:, :, 0:P - 1], -BIG, None, ALU.mult).then_inc(v_step.h, 1)
                    v.wait_ge(v_step.h, v_step.next())
                    v.nop().then_inc(pairs_ready.h, 1)
                    for b in range(ETB):
                        v.wait_ge(pairs_turned.h, b + 1)
                        c = slice(b * P, (b + 1) * P)
                        v.tensor_copy(psrc[:, c], ps[b][:, 0:P]).then_inc(v_step.h, 1)
                        v.wait_ge(v_step.h, v_step.next())
                        v.tensor_copy(pdl[:, c], ps[b][:, P:2 * P]).then_inc(v_step.h, 1)
                        v.wait_ge(v_step.h, v_step.next())
                        v.tensor_copy(plast[:, c], ps[b][:, 2 * P:3 * P]).then_inc(v_step.h, 1)
                        v.wait_ge(v_step.h, v_step.next())
                        v.tensor_copy(prow[:, c], ps[b][0:2, 3 * P:4 * P]).then_inc(v_step.h, 1)
                        v.wait_ge(v_step.h, v_step.next())

                @block.tensor
                def _(pe):
                    pe.wait_ge(counted.h, 1)
                    pe.matmul(ps[0][:, 0:ETB], incl[:], small[:, 1, :], start=True, stop=True)
                    pe.matmul(ps[0][:, 16:16 + ETB], ones[:], small[:, 1, :], start=True, stop=True).then_inc(scanned.h, 1)
                    pe.wait_ge(spread.h, 1)
                    diag = tmp[:].rearrange("p b l -> p (b l)")
                    pe.matmul(ps[1][:], ones[:], diag[:, 0:512], start=True, stop=True)
                    pe.matmul(ps[2][:, 0:PCOL - 512], ones[:], diag[:, 512:PCOL], start=True, stop=True).then_inc(spread_done.h, 1)
                    pe.wait_ge(pairs_ready.h, 1)
                    for b in range(ETB):
                        pe.transpose(ps[b][:, 0:P], pair_edges[:, b, 0:P], ident[:])
                        pe.transpose(ps[b][:, P:2 * P], pair_dst[:, b, :], ident[:])
                        pe.transpose(ps[b][:, 2 * P:3 * P], lastf[:, b, :], ident[:])
                        pe.matmul(ps[b][0:2, 3 * P:4 * P], drow[:, b, :], ident[:], start=True, stop=True).then_inc(pairs_turned.h, 1)
            stored.base += 16

    edge_tables()

    def degrees():
        with ExitStack() as ctx, PhaseSems() as sem:
            hot = sb("hot", [P, 2, 2 * G, P], BF16, ctx)
            ones_b = sb("ones_b", [P, 1], BF16, ctx)
            cnt = sb("cnt", [P, PCOL], F32, ctx)
            cnt_t = sb("cnt_t", [P, ETB, P], F32, ctx)
            hit = sb("hit", [P, ETB, NT], F32, ctx)
            drow_f = sb("drow_f", [1, PCOL], F32, ctx)
            dcol = sb("dcol", [P, ETB], F32, ctx)
            tile_row = sb("tile_row", [P, PCOL], F32, ctx)
            differs = sb("differs", [P, PCOL], F32, ctx)
            deg = sb("deg", [P, NT], F32, ctx)
            tmp = sb("deg_tmp", [P, NT], F32, ctx)
            hot_ready, hot_used, count_out = sem("hot_ready"), sem("hot_used"), sem("count_out")
            row_ready, col_ready = sem("row_ready"), sem("col_ready")
            cnt_ready, cnt_turned, cnt_back, deg_ready = sem("cnt_ready"), sem("cnt_turned"), sem("cnt_back"), sem("deg_ready")
            root = Rsqrt(deg[:], dinv[:], tmp[:])
            with nc.Block() as block:
                @block.vector
                def _(v):
                    v.memset(ones_b[:], 1.0).then_inc(v_step.h, 1)
                    v.wait_ge(v_step.h, v_step.next())
                    v.memset(cnt[:], 0.0).then_inc(v_step.h, 1)
                    v.wait_ge(v_step.h, v_step.next())
                    v.tensor_copy(drow_f[:], prow[0:1, :]).then_inc(v_step.h, 1)
                    v.wait_ge(v_step.h, v_step.next())
                    v.nop().then_inc(row_ready.h, 1)

                    def mark(i, k):
                        v.tensor_tensor(hot[:, k], iota_f[:].rearrange("p (j n) -> p j n", j=1).to_broadcast([P, 2 * G, P]),
                                        pdl[:, bass.ds(i * 2 * G, 2 * G)].rearrange("p (j n) -> p j n", n=1).to_broadcast([P, 2 * G, P]),
                                        ALU.is_equal).then_inc(hot_ready.h, 1)

                    def keep(i, k):
                        v.wait_ge(hot_used.h, i + 1)
                        v.tensor_copy(cnt[:, bass.ds(i * 2 * G, 2 * G)], ps[k][:, 0:2 * G]).then_inc(count_out.h, 1)

                    mark(0, 0)
                    with v.Fori(0, ITERS // 2) as j:
                        mark(2 * j + 1, 1)
                        keep(2 * j, 0)
                        mark(2 * j + 2, 0)
                        keep(2 * j + 1, 1)
                    v.wait_ge(count_out.h, ITERS)
                    v.nop().then_inc(cnt_ready.h, 1)
                    v.wait_ge(col_ready.h, 1)
                    v.tensor_copy(dcol[:], ps[7][:, 0:ETB]).then_inc(v_step.h, 1)
                    v.wait_ge(v_step.h, v_step.next())
                    v.tensor_copy(tile_row[:, 0:512], ps[5][:]).then_inc(v_step.h, 1)
                    v.wait_ge(v_step.h, v_step.next())
                    v.tensor_copy(tile_row[:, 512:PCOL], ps[6][:, 0:PCOL - 512]).then_inc(v_step.h, 1)
                    v.wait_ge(v_step.h, v_step.next())
                    v.memset(differs[:, 0:1], 1.0).then_inc(v_step.h, 1)
                    v.wait_ge(v_step.h, v_step.next())
                    v.tensor_tensor(differs[:, 1:PCOL], tile_row[:, 1:PCOL], tile_row[:, 0:PCOL - 1], ALU.not_equal).then_inc(v_step.h, 1)
                    v.wait_ge(v_step.h, v_step.next())
                    v.memset(change[:, :, 0:1], -BIG).then_inc(v_step.h, 1)
                    v.wait_ge(v_step.h, v_step.next())
                    v.tensor_scalar(change[:, :, 1:G + 1], differs[:, 0:NPAIR].rearrange("p (n j) -> p n j", j=G), -BIG, None, ALU.mult).then_inc(v_step.h, 1)
                    v.wait_ge(v_step.h, v_step.next())
                    for b in range(ETB):
                        v.tensor_scalar(hit[:, b, :], iota_f[:, 0:NT], dcol[:, b:b + 1], None, ALU.is_equal).then_inc(v_step.h, 1)
                        v.wait_ge(v_step.h, v_step.next())
                    v.wait_ge(cnt_turned.h, 1)
                    v.tensor_copy(cnt_t[:, 0:4, :], ps[2][:].rearrange("p (b l) -> p b l", l=P)).then_inc(v_step.h, 1)
                    v.wait_ge(v_step.h, v_step.next())
                    v.tensor_copy(cnt_t[:, 4:ETB, :], ps[3][:, 0:(ETB - 4) * P].rearrange("p (b l) -> p b l", l=P)).then_inc(v_step.h, 1)
                    v.wait_ge(v_step.h, v_step.next())
                    v.nop().then_inc(cnt_back.h, 1)
                    v.wait_ge(deg_ready.h, 1)
                    v.tensor_scalar(deg[:], ps[4][:, 0:NT], 1.0, None, ALU.add).then_inc(v_step.h, 1)
                    v.wait_ge(v_step.h, v_step.next())
                    root.vector(v)

                @block.scalar
                def _(a):
                    root.scalar(a)

                @block.tensor
                def _(pe):
                    pe.wait_ge(row_ready.h, 1)
                    pe.matmul(ps[5][:], ones[0:1, :], drow_f[:, 0:512], start=True, stop=True)
                    pe.matmul(ps[6][:, 0:PCOL - 512], ones[0:1, :], drow_f[:, 512:PCOL], start=True, stop=True)
                    for b in range(ETB):
                        mm = pe.matmul(ps[7][:, b:b + 1], drow_f[0:1, b * P:(b + 1) * P], ones[0:1, 0:1], start=True, stop=True)
                    mm.then_inc(col_ready.h, 1)
                    with pe.Fori(0, ITERS // 2) as j:
                        for k in range(2):
                            pe.wait_ge(hot_ready.h, 2 * j + k + 1)
                            for b in range(2 * G):
                                mm = pe.matmul(ps[k][:, b:b + 1], hot[:, k, b, :], ones_b[:], start=True, stop=True)
                            mm.then_inc(hot_used.h, 1)
                    pe.wait_ge(cnt_ready.h, 1)
                    for b in range(ETB):
                        mm = pe.transpose(ps[2 + b // 4][:, b % 4 * P:(b % 4 + 1) * P], cnt[:, b * P:(b + 1) * P], ident[:])
                    mm.then_inc(cnt_turned.h, 1)
                    pe.wait_ge(cnt_back.h, 1)
                    for b in range(ETB):
                        mm = pe.matmul(ps[4][:, 0:NT], cnt_t[:, b, :], hit[:, b, :], start=(b == 0), stop=(b == ETB - 1))
                    mm.then_inc(deg_ready.h, 1)

    degrees()

    class NodeNorm:

        def __init__(self, ctx, name):
            self.stats = sb(name + "_stats", [P, NT, 6], F32, ctx)
            self.mean = sb(name + "_mean", [P, NT], F32, ctx)
            self.var = sb(name + "_var", [P, NT], F32, ctx)
            self.rstd = sb(name + "_rstd", [P, NT], F32, ctx)
            self.tmp = sb(name + "_tmp", [P, NT], F32, ctx)
            self.root = Rsqrt(self.var[:], self.rstd[:], self.tmp[:])
            self.seen = sem(name + "_seen")

        def stats_of(self, v, src):
            with v.Fori(0, NT) as d:
                v.bn_stats(self.stats[:, bass.ds(d, 1), :], src[:, bass.ds(d, 1), :]).then_inc(self.seen.h, 1)
            v.wait_ge(self.seen.h, NT)
            mean_e, sq_e, mean_o, sq_o = (self.stats[:, :, j] for j in (1, 2, 4, 5))
            mean = self.mean[:]
            v.tensor_tensor(self.tmp[:], mean_e, mean_o, ALU.subtract).then_inc(v_step.h, 1)
            v.wait_ge(v_step.h, v_step.next())
            v.tensor_tensor(mean, mean_e, mean_o, ALU.add).then_inc(v_step.h, 1)
            v.wait_ge(v_step.h, v_step.next())
            v.tensor_scalar(mean, mean, 0.5, None, ALU.mult).then_inc(v_step.h, 1)
            v.wait_ge(v_step.h, v_step.next())
            v.tensor_tensor(self.tmp[:], self.tmp[:], self.tmp[:], ALU.mult).then_inc(v_step.h, 1)
            v.wait_ge(v_step.h, v_step.next())
            v.tensor_tensor(self.var[:], sq_e, sq_o, ALU.add).then_inc(v_step.h, 1)
            v.wait_ge(v_step.h, v_step.next())
            v.tensor_scalar(self.var[:], self.var[:], 1.0 / F, EPS, ALU.mult, ALU.add).then_inc(v_step.h, 1)
            v.wait_ge(v_step.h, v_step.next())
            v.scalar_tensor_tensor(self.var[:], self.tmp[:], 0.25, self.var[:], ALU.mult, ALU.add).then_inc(v_step.h, 1)
            v.wait_ge(v_step.h, v_step.next())
            self.root.vector(v)

        def rows(self, v, src, dst, d, ready):
            v.tensor_scalar(dst, src[:, bass.ds(d, 1), :].rearrange("p a f -> p (a f)"), self.mean[:, bass.ds(d, 1)],
                            self.rstd[:, bass.ds(d, 1)], ALU.subtract, ALU.mult).then_inc(ready.h, 1)

    bigs = ExitStack()
    acc = sb("acc", [P, NT, F], F32, bigs)
    feat = sb("feat", [P, NT, F], F32, bigs)
    feat_t = feat[:].rearrange("p d f -> p (d f)").rearrange("p (c n) -> p c n", c=FC)
    vecs = sb("vecs", [P, 3, 3, FC], F32, bigs)
    wts = sb("wts", [P, FC, F], F32, bigs)
    stage = sb("stage", [P, 2, F], F32, bigs)
    lhs = sb("lhs", [P, 2, FC, P], F32, bigs)

    def load_rows(sp, big, src, done):
        sp.dma_start(big[:, 0:NT - 1, :], src[0:(NT - 1) * P, :].rearrange("(d p) f -> p d f", p=P)).then_inc(done.h, 16)
        sp.dma_start(big[0:NLAST, NT - 1, :], src[(NT - 1) * P:N, :]).then_inc(done.h, 16)

    def load_weights(sp, w, dst):
        sp.dma_start(dst, w.rearrange("(c p) n -> p c n", p=P)).then_inc(loaded.h, 16)

    def turn(pe, d, k, rows_ready):
        pe.wait_ge(rows_ready.h, d + 1)
        pe.wait_ge(turned_out.h, turned_out.base + d + 1)
        for c in range(FC):
            mm = pe.transpose(ps[k][:, c * P:(c + 1) * P], stage[:, k, c * P:(c + 1) * P], ident[:])
        mm.then_inc(turned.h, 1)

    def multiply(pe, w, d, k, lhs_ready, lhs_credit, ncols=F, bias=None):
        pe.wait_ge(lhs_ready.h, lhs_ready.base + d + 1 + lhs_credit)
        pe.wait_ge(projected_out.h, projected_out.base + d + 1)
        if bias is not None:
            pe.matmul(ps[2 + k][:, 0:ncols], ones[0:1, :], bias[:, 0:ncols], start=True, stop=False)
        for c in range(FC):
            mm = pe.matmul(ps[2 + k][:, 0:ncols], lhs[:, k, c, :], w[:, c, 0:ncols], start=(c == 0 and bias is None), stop=(c == FC - 1))
        mm.then_inc(projected.h, 1)

    def turn_and_multiply(pe, w, rows_ready, ncols=F, bias=None):
        turn(pe, 0, 0, rows_ready)
        with pe.Fori(0, NT // 2) as i:
            turn(pe, 2 * i + 1, 1, rows_ready)
            multiply(pe, w, 2 * i, 0, turned_out, 2, ncols, bias)
            turn(pe, 2 * i + 2, 0, rows_ready)
            multiply(pe, w, 2 * i + 1, 1, turned_out, 2, ncols, bias)
        multiply(pe, w, NT - 1, 0, turned_out, 2, ncols, bias)

    def turned_to_lhs(a):
        for d, k in node_tiles(a):
            a.wait_ge(turned.h, turned.base + d + 1 + 2)
            a.wait_ge(projected.h, projected.base + d + 1)
            a.activation(lhs[:, k].rearrange("p c n -> p (c n)"), ps[k][:, 0:F], ACT.Copy).then_inc(turned_out.h, 1)

    def scale_to_acc(v, d, k):
        v.wait_ge(projected.h, projected.base + d + 1 + 2)
        v.tensor_scalar(acc[:, bass.ds(d, 1), :].rearrange("p a f -> p (a f)"), ps[2 + k][:, 0:F], dinv[:, bass.ds(d, 1)], None, ALU.mult).then_inc(projected_out.h, 1)

    def store_acc(sp):
        for d, k in node_tiles(sp):
            sp.wait_ge(projected_out.h, projected_out.base + d + 1 + 2)
            sp.dma_start(node_table[bass.ds(d * P, P), :], acc[:, bass.ds(d, 1), :].rearrange("p a f -> p (a f)")).then_inc(stored.h, 16)
        sp.wait_ge(stored.h, stored.base + 16 * NT)

    def project_counted(turned_too=True):
        if turned_too:
            turned.base += NT
            turned_out.base += NT
        projected.base += NT
        projected_out.base += NT
        stored.base += 16 * NT

    def first_projection():
        with ExitStack() as ctx:
            norm = NodeNorm(ctx, "ln0")
            rows_ready, zeroed, vec_in = sem("rows_ready"), sem("zeroed"), sem("vec_in")
            with nc.Block() as block:
                @block.sync
                def _(sp):
                    load_weights(sp, t["L0_gnn_W1"], wts[:])
                    sp.wait_ge(zeroed.h, 1)
                    load_rows(sp, feat, t["x"], x_loaded)
                    with nc.allow_non_contiguous_dma("vectors of 256 features onto partitions"):
                        for k in range(3):
                            for j, name in enumerate(("b", "g", "be")):
                                sp.dma_start(vecs[:, k, j, :], t[f"L0_gnn_{name}{k + 1}"].rearrange("(c p) -> p c", p=P)).then_inc(vec_in.h, 16)
                    store_acc(sp)
                    sp.wait_ge(vec_in.h, 16 * 9)

                @block.vector
                def _(v):
                    v.memset(feat[:, NT - 1, :], 0.0).then_inc(zeroed.h, 1)
                    v.wait_ge(x_loaded.h, x_loaded.base + 32)
                    norm.stats_of(v, feat)

                    def stage_rows(d, k):
                        v.wait_ge(turned.h, turned.base + d + 1)
                        norm.rows(v, feat, stage[:, k, :], d, rows_ready)

                    two_ahead(v, stage_rows, lambda d, k: scale_to_acc(v, d, k))

                @block.scalar
                def _(a):
                    norm.root.scalar(a)
                    turned_to_lhs(a)

                @block.tensor
                def _(pe):
                    pe.wait_ge(loaded.h, loaded.base + 16)
                    turn_and_multiply(pe, wts, rows_ready)
            x_loaded.base += 32
            loaded.base += 16
            project_counted()

    first_projection()

    def gather_rows(g, rows, table):
        with g.Fori(0, ITERS) as i:
            for h in range(2):
                g.wait_ge(aggregated.h, aggregated.base + (i * 2 + h + 1) * G)
                g.tensor_copy(idx[:, h, :], psrc[:, bass.ds(i * 2 * G + h * G, G)]).then_inc(idx_ready.h, 1)
                g.wait_ge(idx_ready.h, idx_ready.base + 2 * i + h + 1)
                g.tensor_tensor(carrier[:], psrc[:, 0:1], psrc[:, 0:1], ALU.add)
                for b in range(G):
                    s = h * G + b
                    g.indirect_dma_start(rows[:, s, :], None, table,
                                         bass.IndirectOffsetOnAxis(ap=idx[:, h, b:b + 1], axis=0)).then_inc(row_sem[s].h, 16)

    def gather_counted():
        aggregated.base += NPAIR
        added.base += NPAIR
        onehot_ready.base += 2 * ITERS + 1
        idx_ready.base += 2 * ITERS
        for s in row_sem:
            s.base += 16 * ITERS

    def mark_pairs(v, hot, q, h):
        v.tensor_tensor(hot[:, h], iota_f[:].rearrange("p (j n) -> p j n", j=1).to_broadcast([P, G, P]),
                        pdl[:, bass.ds(q * G, G)].rearrange("p (j n) -> p j n", n=1).to_broadcast([P, G, P]),
                        ALU.is_equal).then_inc(onehot_ready.h, 1)

    def pair_bank(b, n=F):
        return ps[4 + b // 2][:, b % 2 * F:b % 2 * F + n]

    def aggregate(pe, hot, rows, i, h):
        pe.wait_ge(onehot_ready.h, onehot_ready.base + 2 * i + h + 1)
        for b in range(G):
            s = h * G + b
            pe.wait_ge(row_sem[s].h, row_sem[s].base + 16 * (i + 1))
            if b % 2 == 0:
                pe.wait_ge(added.h, added.base + (2 * i + h) * G + b + 2)
            pe.matmul(pair_bank(b), hot[:, h, b, :], rows[:, s, :], start=True, stop=True).then_inc(aggregated.h, 1)

    def add_pairs(v, i, h):
        for b in range(G):
            n = (2 * i + h) * G + b
            d = v.value_load(prow[0:1, bass.ds(n, 1)], min_val=0, max_val=NT - 1)
            row = acc[:, bass.ds(d, 1), :].rearrange("p a f -> p (a f)")
            if b % 2 == 0:
                v.wait_ge(aggregated.h, aggregated.base + 2 * G + n + 2)
            v.wait_ge(added.h, added.base + G + n)
            v.tensor_tensor(row, row, pair_bank(b), ALU.add).then_inc(added.h, 1)

    class EdgeTerms:

        def __init__(self, ctx):
            self.terms = sb("edge_terms", [P, NPAIR, HEADS], F32, ctx)
            self.rows = sb("edge_rows", [P, 2, G, EDIM], F32, ctx)
            self.turned_rows = sb("edge_t", [P, 2, G // 2, P], F32, ctx)
            self.weights = sb("edge_w", [P, 2 * HEADS], F32, ctx)
            self.we = sb("we", [P, F], F32, ctx)
            self.attn = sb("attn_e", [P, F], F32, ctx)
            self.weights_in, self.weights_set, self.done = sem("edge_w_in"), sem("edge_w_set"), sem("edge_terms_out")
            self.landed = [sem(f"edge_in{h}") for h in range(2)]
            self.turned, self.kept = sem("edge_turned"), sem("edge_kept")
            self.multiplied, self.stored = sem("edge_multiplied"), sem("edge_terms_kept")

        def sync(self, sp):
            for j in range(2):
                sp.dma_start(self.we[j * EDIM:(j + 1) * EDIM, :], t["L1_gnn_W_e"]).then_inc(self.weights_in.h, 16)
            sp.dma_start(self.attn[:], t["L1_gnn_attn_e"].rearrange("(a h) d -> a (h d)", a=1).to_broadcast([P, F])).then_inc(self.weights_in.h, 16)
            with sp.Fori(0, ITERS) as i:
                for h in range(2):
                    first_edges = in_registers(sp, prow[1:2, bass.ds((2 * i + h) * G, G)], E - P)
                    sp.wait_ge(self.turned.h, 2 * i + h + 1)
                    for b in range(G):
                        sp.dma_start(self.rows[:, h, b, :], t["edge_attr_64"][bass.ds(first_edges[b], P), :]).then_inc(self.landed[h].h, 16)

        def store(self, sp):
            sp.wait_ge(self.stored.h, 2 * ITERS + 2)
            sp.dma_start(ee_table, self.terms[:].rearrange("p n e -> p (n e)")).then_inc(self.done.h, 16)

        def vector(self, v):
            for s in (self.turned, self.kept, self.multiplied, self.stored):
                v.sem_inc(s.h, 2)
            v.wait_ge(self.weights_in.h, 16 * 3)
            v.memset(self.weights[:], 0.0).then_inc(v_step.h, 1)
            v.tensor_tensor(self.we[:], self.we[:], self.attn[:], ALU.mult).then_inc(v_step.h, 1)
            v_step.next()
            v.wait_ge(v_step.h, v_step.next())
            for j in range(2):
                r = slice(j * EDIM, (j + 1) * EDIM)
                v.tensor_reduce(self.weights[r, j * HEADS:(j + 1) * HEADS], self.we[r, :].rearrange("p (h d) -> p h d", d=HD), AX.X, ALU.add).then_inc(self.weights_set.h, 1)

        def scalar(self, a):
            with a.Fori(0, ITERS) as i:
                for h in range(2):
                    a.wait_ge(self.turned.h, 2 * i + h + 1 + 2)
                    a.wait_ge(self.multiplied.h, 2 * i + h + 1)
                    a.activation(self.turned_rows[:, h].rearrange("p j n -> p (j n)"), ps[h][:], ACT.Copy).then_inc(self.kept.h, 1)
                    a.wait_ge(self.multiplied.h, 2 * i + h + 1 + 2)
                    a.activation(self.terms[:, bass.ds((2 * i + h) * G, G), :], ps[2 + h][:, 0:G * HEADS].rearrange("p (j e) -> p j e", e=HEADS), ACT.Copy).then_inc(self.stored.h, 1)

        def turn(self, pe, q, i, h):
            pe.wait_ge(self.landed[h].h, 16 * G * (i + 1))
            pe.wait_ge(self.kept.h, q + 1)
            for j in range(G // 2):
                mm = pe.transpose(ps[h][:, j * P:(j + 1) * P], self.rows[:, h, 2 * j:2 * j + 2, :].rearrange("p a c -> p (a c)"), ident[:])
            mm.then_inc(self.turned.h, 1)

        def multiply(self, pe, q, h):
            pe.wait_ge(self.kept.h, q + 1 + 2)
            pe.wait_ge(self.stored.h, q + 1)
            for j in range(G // 2):
                mm = pe.matmul(ps[2 + h][:, j * 2 * HEADS:(j + 1) * 2 * HEADS], self.turned_rows[:, h, j, :], self.weights[:], start=True, stop=True)
            mm.then_inc(self.multiplied.h, 1)

    def gcn_layer(k):
        last = k == 2
        with ExitStack() as ctx:
            hot = sb("hot", [P, 2, G, P], F32, ctx)
            rows = sb("rows", [P, 2 * G, F], F32, ctx)
            bn = sb("bn", [P, FC, -(-N // 512), 6], F32, ctx)
            mv = sb("bn_mv", [P, FC, 2], F32, ctx)
            var = sb("bn_var", [P, FC], F32, ctx)
            rstd = sb("bn_rstd", [P, FC], F32, ctx)
            tmp = sb("bn_tmp", [P, FC], F32, ctx)
            gain = sb("gain", [P, FC], F32, ctx)
            shift = sb("shift", [P, FC], F32, ctx)
            y_ready, affine_set, affine_ready = sem(f"y_ready{k}"), sem(f"affine_set{k}"), sem(f"affine_ready{k}")
            root = Rsqrt(var[:], rstd[:], tmp[:])
            if k == 0:
                edges = EdgeTerms(ctx)
                zeros = sb("zeros", [P, F], F32, ctx)
                zeros_set, zeros_out = sem("zeros_set"), sem("zeros_out")
            with nc.Block() as block:
                @block.gpsimd
                def _(g):
                    gather_rows(g, rows, node_table)

                @block.sync
                def _(sp):
                    if not last:
                        load_weights(sp, t[f"L0_gnn_W{k + 2}"], wts[:])
                    if k == 0:
                        edges.sync(sp)
                        sp.wait_ge(zeros_set.h, 1)
                        with sp.Fori(0, MT + 2) as m:
                            sp.dma_start(slot_rows[bass.ds(m * P, P), :], zeros[:]).then_inc(zeros_out.h, 16)
                        for j in range(2):
                            sp.dma_start(slot_out[CAP + j * P:CAP + (j + 1) * P, :], zeros[:]).then_inc(zeros_out.h, 16)
                        edges.store(sp)
                    if not last:
                        store_acc(sp)
                    else:
                        sp.wait_ge(y_ready.h, NT)
                        load_rows(sp, acc, t["x"], x_loaded)
                    if k == 0:
                        sp.wait_ge(zeros_out.h, 16 * (MT + 4))
                        sp.wait_ge(edges.done.h, 16)

                @block.vector
                def _(v):
                    if k == 0:
                        v.memset(zeros[:], 0.0).then_inc(zeros_set.h, 1)
                        edges.vector(v)
                    mark_pairs(v, hot, 0, 0)
                    with v.Fori(0, ITERS) as i:
                        v.wait_ge(aggregated.h, aggregated.base + (i + 1) * 2 * G)
                        mark_pairs(v, hot, 2 * i + 1, 1)
                        add_pairs(v, i, 0)
                        mark_pairs(v, hot, 2 * i + 2, 0)
                        add_pairs(v, i, 1)
                    v.wait_ge(added.h, added.base + G + NPAIR)
                    for d, par in node_tiles(v):
                        v.wait_ge(turned.h, turned.base + d + 1)
                        row = acc[:, bass.ds(d, 1), :].rearrange("p a f -> p (a f)")
                        v.tensor_scalar(stage[:, par, :], row, dinv[:, bass.ds(d, 1)], None, ALU.mult).then_inc(y_ready.h, 1)
                    v.wait_ge(turned_out.h, turned_out.base + NT + 2)
                    for c in range(FC):
                        for j in range(-(-N // 512)):
                            v.bn_stats(bn[:, c, j, :], feat_t[:, c, j * 512:min(N, (j + 1) * 512)]).then_inc(v_step.h, 1)
                            v.wait_ge(v_step.h, v_step.next())
                        v.bn_aggr(mv[:, c, :], bn[:, c].rearrange("p j s -> p (j s)")).then_inc(v_step.h, 1)
                        v.wait_ge(v_step.h, v_step.next())
                    v.tensor_scalar(var[:], mv[:, :, 1], EPS, None, ALU.add).then_inc(v_step.h, 1)
                    v.wait_ge(v_step.h, v_step.next())
                    root.vector(v)
                    v.tensor_tensor(gain[:], rstd[:], vecs[:, k, 1, :], ALU.mult).then_inc(v_step.h, 1)
                    v.wait_ge(v_step.h, v_step.next())
                    v.tensor_tensor(tmp[:], mv[:, :, 0], gain[:], ALU.mult).then_inc(v_step.h, 1)
                    v.wait_ge(v_step.h, v_step.next())
                    v.tensor_tensor(shift[:], vecs[:, k, 2, :], tmp[:], ALU.subtract).then_inc(v_step.h, 1)
                    v.wait_ge(v_step.h, v_step.next())
                    v.nop().then_inc(affine_set.h, 1)
                    if not last:
                        for d, par in node_tiles(v):
                            scale_to_acc(v, d, par)
                    else:
                        v.wait_ge(x_loaded.h, x_loaded.base + 32)
                        for d, par in node_tiles(v):
                            v.wait_ge(projected.h, projected.base + d + 1 + 2)
                            row = acc[:, bass.ds(d, 1), :].rearrange("p a f -> p (a f)")
                            v.tensor_tensor(row, row, ps[2 + par][:, 0:F], ALU.add).then_inc(projected_out.h, 1)

                @block.scalar
                def _(a):
                    if k == 0:
                        edges.scalar(a)
                    for d, par in node_tiles(a):
                        a.wait_ge(turned.h, turned.base + d + 1 + 2)
                        for c in range(FC):
                            op = a.activation(feat_t[:, c, bass.ds(d * P, P)], ps[par][:, c * P:(c + 1) * P], ACT.Identity, bias=vecs[:, k, 0, c:c + 1])
                        op.then_inc(turned_out.h, 1)
                    root.scalar(a)
                    a.wait_ge(affine_set.h, 1)
                    for d, par in node_tiles(a):
                        a.wait_ge(projected.h, projected.base + d + 1)
                        for c in range(FC):
                            op = a.activation(lhs[:, par, c, :], feat_t[:, c, bass.ds(d * P, P)], ACT.Identity, bias=shift[:, c:c + 1], scale=gain[:, c:c + 1])
                        op.then_inc(affine_ready.h, 1)

                @block.tensor
                def _(pe):
                    if k == 0:
                        pe.wait_ge(edges.weights_set.h, 2)
                    with pe.Fori(0, ITERS) as i:
                        for h in range(2):
                            if k == 0:
                                edges.turn(pe, 2 * i + h, i, h)
                            aggregate(pe, hot, rows, i, h)
                            if k == 0:
                                edges.multiply(pe, 2 * i + h, h)
                    for d, par in node_tiles(pe):
                        turn(pe, d, par, y_ready)
                    if not last:
                        pe.wait_ge(loaded.h, loaded.base + 16)
                        for d, par in node_tiles(pe):
                            multiply(pe, wts, d, par, affine_ready, 0)
                    else:
                        for d, par in node_tiles(pe):
                            pe.wait_ge(affine_ready.h, d + 1)
                            pe.wait_ge(projected_out.h, projected_out.base + d + 1)
                            for c in range(FC):
                                mm = pe.transpose(ps[2 + par][:, c * P:(c + 1) * P], lhs[:, par, c, :], ident[:])
                            mm.then_inc(projected.h, 1)
            gather_counted()
            project_counted()
            if last:
                x_loaded.base += 32
                stored.base -= 16 * NT
            else:
                loaded.base += 16

    for k in range(3):
        gcn_layer(k)
    def route():
        with ExitStack() as ctx:
            norm = NodeNorm(ctx, "ln1")
            inner = NodeNorm(ctx, "ln_moe")
            wr = sb("wr", [P, FC, EXPERTS], F32, ctx)
            br = sb("br", [1, EXPERTS], F32, ctx)
            logits = sb("logits", [P, NT, EXPERTS], F32, ctx)
            low = sb("low", [P, NT, EXPERTS], F32, ctx)
            hits = sb("hits", [P, NT, EXPERTS], F32, ctx)
            pick = sb("pick", [P, 2, NT, EXPERTS], F32, ctx)
            both = sb("both", [P, NT, EXPERTS], F32, ctx)
            tot = sb("tot", [P, NT, EXPERTS], F32, ctx)
            run = sb("run", [P, NT, EXPERTS], F32, ctx)
            best = sb("best", [P, 2, NT], F32, ctx)
            top = sb("top", [P, NT], F32, ctx)
            order = sb("order", [P, EXPERTS], F32, ctx)
            node = sb("node", [P, NT], F32, ctx)
            node_i = sb("node_i", [P, NT], I32, ctx)
            valid = sb("valid", [P, NT], F32, ctx)
            spare = sb("spare", [P, NT], F32, ctx)
            slot_f = sb("slot_f", [P, 2, NT], F32, ctx)
            e8 = sb("e8", [P, 4, EXPERTS], F32, ctx)
            e8_i = sb("e8_i", [P, EXPERTS], I32, ctx)
            upto = sb("upto", [P, MT, EXPERTS], F32, ctx)
            z_done, z_ready, rows_ready, xn_ready = sem("z_done"), sem("z_ready"), sem("z_staged"), sem("xn_ready")
            numbered, exp_ready, exp_done = sem("numbered"), sem("exp_ready"), sem("exp_done")
            picked, ranked, slots_set = sem("picked"), sem("ranked"), sem("slots_set")
            slot_idx = sem("slot_idx")
            scattered = [sem(f"scattered{k}") for k in range(2)]
            with nc.Block() as block:
                @block.sync
                def _(sp):
                    sp.dma_start(resid.rearrange("(d p) f -> p d f", p=P), acc[:]).then_inc(stored.h, 16)
                    sp.dma_start(wr[:], t["L0_ffn_Wr"].rearrange("(c p) e -> p c e", p=P)).then_inc(loaded.h, 16)
                    sp.dma_start(br[:], t["L0_ffn_br"].rearrange("(a e) -> a e", a=1)).then_inc(loaded.h, 16)
                    sp.wait_ge(stored.h, stored.base + 16)

                @block.gpsimd
                def _(g):
                    g.iota(node_i[:], [[P, NT]], base=0, channel_multiplier=1).then_inc(numbered.h, 1)
                    g.wait_ge(slots_set.h, 1)
                    for d, k in node_tiles_apart(g):
                        wait_earlier(g, scattered[k], d, k, 32)
                        g.tensor_copy(idx[:, k, 0:2], slots[:, :, bass.ds(d, 1)].rearrange("p a d -> p (a d)")).then_inc(slot_idx.h, 1)
                        g.wait_ge(xn_ready.h, d + 1)
                        g.wait_ge(slot_idx.h, d + 1)
                        g.tensor_tensor(carrier[:], psrc[:, 0:1], psrc[:, 0:1], ALU.add)
                        for j in range(2):
                            g.indirect_dma_start(slot_rows, bass.IndirectOffsetOnAxis(ap=idx[:, k, j:j + 1], axis=0), stage[:, k, :], None).then_inc(scattered[k].h, 16)
                    g.wait_ge(scattered[0].h, 32 * (NT // 2 + 1))
                    g.wait_ge(scattered[1].h, 32 * (NT // 2))

                @block.vector
                def _(v):
                    norm.stats_of(v, acc)
                    for d, _ in node_tiles(v):
                        norm.rows(v, acc, rows_of(feat, d), d, z_done)
                    v.wait_ge(z_done.h, NT)
                    inner.stats_of(v, feat)

                    def stage_z(d, k):
                        v.wait_ge(turned.h, turned.base + d + 1)
                        v.tensor_copy(stage[:, k, :], rows_of(feat, d)).then_inc(rows_ready.h, 1)

                    def keep_logits(d, k):
                        v.wait_ge(projected.h, projected.base + d + 1 + 2)
                        v.tensor_copy(logits[:, bass.ds(d, 1), :].rearrange("p a e -> p (a e)"), ps[2 + k][:, 0:EXPERTS]).then_inc(projected_out.h, 1)

                    two_ahead(v, stage_z, keep_logits)
                    v.wait_ge(projected_out.h, projected_out.base + NT + 2)

                    def over_e(x):
                        return x.rearrange("p (d a) -> p d a", a=1).to_broadcast([P, NT, EXPERTS])

                    def over_d(x, n=NT):
                        return x.rearrange("p (a e) -> p a e", a=1).to_broadcast([P, n, EXPERTS])

                    v.wait_ge(numbered.h, 1)
                    v.tensor_copy(node[:], node_i[:]).then_inc(v_step.h, 1)
                    v.wait_ge(v_step.h, v_step.next())
                    v.tensor_scalar(valid[:], node[:], float(N), None, ALU.is_lt).then_inc(v_step.h, 1)
                    v.wait_ge(v_step.h, v_step.next())
                    v.tensor_scalar(order[:], iota_f[:, 0:EXPERTS], -1.0, float(EXPERTS), ALU.mult, ALU.add).then_inc(v_step.h, 1)
                    v.wait_ge(v_step.h, v_step.next())
                    src = logits
                    for j in range(2):
                        v.tensor_reduce(best[:, j, :], src[:], AX.X, ALU.max).then_inc(v_step.h, 1)
                        v.wait_ge(v_step.h, v_step.next())
                        v.tensor_tensor(hits[:], src[:], over_e(best[:, j, :]), ALU.is_equal).then_inc(v_step.h, 1)
                        v.wait_ge(v_step.h, v_step.next())
                        v.tensor_tensor(hits[:], hits[:], over_d(order[:]), ALU.mult).then_inc(v_step.h, 1)
                        v.wait_ge(v_step.h, v_step.next())
                        v.tensor_reduce(top[:], hits[:], AX.X, ALU.max).then_inc(v_step.h, 1)
                        v.wait_ge(v_step.h, v_step.next())
                        v.tensor_tensor(pick[:, j], hits[:], over_e(top[:]), ALU.is_equal).then_inc(v_step.h, 1)
                        v.wait_ge(v_step.h, v_step.next())
                        if j == 0:
                            v.scalar_tensor_tensor(low[:], pick[:, 0], -BIG, logits[:], ALU.mult, ALU.add).then_inc(v_step.h, 1)
                            v.wait_ge(v_step.h, v_step.next())
                            src = low
                        v.tensor_tensor(pick[:, j], pick[:, j], over_e(valid[:]), ALU.mult).then_inc(v_step.h, 1)
                        v.wait_ge(v_step.h, v_step.next())
                    v.tensor_tensor(top[:], best[:, 1, :], best[:, 0, :], ALU.subtract).then_inc(v_step.h, 1)
                    v.wait_ge(v_step.h, v_step.next())
                    v.nop().then_inc(exp_ready.h, 1)
                    v.tensor_tensor(both[:], pick[:, 0], pick[:, 1], ALU.add).then_inc(v_step.h, 1)
                    v.wait_ge(v_step.h, v_step.next())
                    v.nop().then_inc(picked.h, 1)
                    v.wait_ge(exp_done.h, 1)
                    v.tensor_scalar(spare[:], best[:, 1, :], 1.0, None, ALU.add).then_inc(v_step.h, 1)
                    v.wait_ge(v_step.h, v_step.next())
                    v.reciprocal(gate[:, 0, :], spare[:]).then_inc(v_step.h, 1)
                    v.wait_ge(v_step.h, v_step.next())
                    v.tensor_tensor(gate[:, 1, :], best[:, 1, :], gate[:, 0, :], ALU.mult).then_inc(v_step.h, 1)
                    v.wait_ge(v_step.h, v_step.next())
                    v.wait_ge(ranked.h, 1)
                    v.tensor_copy(tot[:], ps[1][:, 0:NT * EXPERTS].rearrange("p (d e) -> p d e", e=EXPERTS)).then_inc(v_step.h, 1)
                    v.wait_ge(v_step.h, v_step.next())
                    for e in range(EXPERTS):
                        v.tensor_tensor_scan(run[:, :, e], ones[:, 0:NT], tot[:, :, e], 0.0, ALU.mult, ALU.add).then_inc(v_step.h, 1)
                        v.wait_ge(v_step.h, v_step.next())
                    count, tiles, upto_e, begin = (e8[:, j, :] for j in range(4))
                    v.tensor_scalar(count, run[:, NT - 1, :], float(P - 1), None, ALU.add).then_inc(v_step.h, 1)
                    v.wait_ge(v_step.h, v_step.next())
                    v.tensor_tensor(run[:], run[:], tot[:], ALU.subtract).then_inc(v_step.h, 1)
                    v.wait_ge(v_step.h, v_step.next())
                    v.tensor_tensor(run[:], run[:], ps[0][:, 0:NT * EXPERTS].rearrange("p (d e) -> p d e", e=EXPERTS), ALU.add).then_inc(v_step.h, 1)
                    v.wait_ge(v_step.h, v_step.next())
                    v.tensor_copy(e8_i[:], count).then_inc(v_step.h, 1)
                    v.wait_ge(v_step.h, v_step.next())
                    v.tensor_scalar(e8_i[:], e8_i[:], 7, None, ALU.arith_shift_right).then_inc(v_step.h, 1)
                    v.wait_ge(v_step.h, v_step.next())
                    v.tensor_copy(tiles, e8_i[:]).then_inc(v_step.h, 1)
                    v.wait_ge(v_step.h, v_step.next())
                    v.tensor_tensor_scan(upto_e, ones[:, 0:EXPERTS], tiles, 0.0, ALU.mult, ALU.add).then_inc(v_step.h, 1)
                    v.wait_ge(v_step.h, v_step.next())
                    v.tensor_tensor(begin, upto_e, tiles, ALU.subtract).then_inc(v_step.h, 1)
                    v.wait_ge(v_step.h, v_step.next())
                    v.tensor_scalar(begin, begin, float(P), None, ALU.mult).then_inc(v_step.h, 1)
                    v.wait_ge(v_step.h, v_step.next())
                    v.tensor_tensor(run[:], run[:], over_d(begin), ALU.add).then_inc(v_step.h, 1)
                    v.wait_ge(v_step.h, v_step.next())
                    v.tensor_scalar(spare[:], node[:], float(CAP - (NT - 1) * P), None, ALU.add).then_inc(v_step.h, 1)
                    v.wait_ge(v_step.h, v_step.next())
                    v.tensor_scalar(top[:], valid[:], -1.0, 1.0, ALU.mult, ALU.add).then_inc(v_step.h, 1)
                    v.wait_ge(v_step.h, v_step.next())
                    v.tensor_tensor(spare[:], spare[:], top[:], ALU.mult).then_inc(v_step.h, 1)
                    v.wait_ge(v_step.h, v_step.next())
                    for j in range(2):
                        v.tensor_tensor(hits[:], pick[:, j], run[:], ALU.mult).then_inc(v_step.h, 1)
                        v.wait_ge(v_step.h, v_step.next())
                        v.tensor_reduce(slot_f[:, j, :], hits[:], AX.X, ALU.add).then_inc(v_step.h, 1)
                        v.wait_ge(v_step.h, v_step.next())
                        v.tensor_tensor(slot_f[:, j, :], slot_f[:, j, :], spare[:], ALU.add).then_inc(v_step.h, 1)
                        v.wait_ge(v_step.h, v_step.next())
                        v.scalar_tensor_tensor(spare[:], top[:], float(P), spare[:], ALU.mult, ALU.add).then_inc(v_step.h, 1)
                        v.wait_ge(v_step.h, v_step.next())
                    v.tensor_copy(slots[:], slot_f[:]).then_inc(v_step.h, 1)
                    v.wait_ge(v_step.h, v_step.next())
                    v.nop().then_inc(slots_set.h, 1)
                    v.tensor_tensor(upto[:], over_d(upto_e, MT), iota_f[:, 0:MT].rearrange("p (k a) -> p k a", a=1).to_broadcast([P, MT, EXPERTS]), ALU.is_le).then_inc(v_step.h, 1)
                    v.wait_ge(v_step.h, v_step.next())
                    v.tensor_reduce(tile_expert[:], upto[:], AX.X, ALU.add).then_inc(v_step.h, 1)
                    v.wait_ge(v_step.h, v_step.next())
                    v.tensor_scalar(tile_expert[:], tile_expert[:], float(EXPERTS - 1), None, ALU.min).then_inc(v_step.h, 1)
                    v.wait_ge(v_step.h, v_step.next())
                    v.tensor_copy(tile_expert_i[:], tile_expert[0:1, :]).then_inc(v_step.h, 1)
                    v.wait_ge(v_step.h, v_step.next())
                    for d, k in node_tiles_apart(v):
                        wait_earlier(v, scattered[k], d, k, 32)
                        inner.rows(v, feat, stage[:, k, :], d, xn_ready)

                @block.scalar
                def _(a):
                    norm.root.scalar(a)
                    inner.root.scalar(a)
                    turned_to_lhs(a)
                    a.wait_ge(exp_ready.h, 1)
                    a.activation(best[:, 1, :], top[:], ACT.Exp).then_inc(exp_done.h, 1)

                @block.tensor
                def _(pe):
                    pe.wait_ge(loaded.h, loaded.base + 32)
                    turn_and_multiply(pe, wr, rows_ready, EXPERTS, br)
                    pe.wait_ge(picked.h, 1)
                    flat = both[:].rearrange("p d e -> p (d e)")
                    pe.matmul(ps[0][:, 0:NT * EXPERTS], excl[:], flat, start=True, stop=True)
                    pe.matmul(ps[1][:, 0:NT * EXPERTS], ones[:], flat, start=True, stop=True).then_inc(ranked.h, 1)
            loaded.base += 32
            project_counted()
            stored.base += 16 - 16 * NT

    route()
    bigs.close()

    def experts():
        with ExitStack() as ctx:
            w1 = sb("w1", [P, EXPERTS, FC, HID], F32, ctx)
            w2 = sb("w2", [P, EXPERTS, HC, F], F32, ctx)
            lng = sb("lng", [P, FC, EXPERTS], F32, ctx)
            lnb = sb("lnb", [P, FC, EXPERTS], F32, ctx)
            bias_f = sb("bias_f", [EXPERTS, HID + F], F32, ctx)
            bias = sb("bias", [96, HID + F], BF16, ctx)
            expert_f = sb("expert_f", [96, 1], F32, ctx)
            expert_i = sb("expert_i", [96, 1], I32, ctx)
            sel1 = sb("sel1", [96, 2, P], BF16, ctx)
            sel2 = sb("sel2", [96, 2, P], BF16, ctx)
            xt = sb("xt", [P, 2, F], F32, ctx)
            xe = sb("xe", [P, 2, FC, P], F32, ctx)
            hid = sb("hid", [P, 2, HID], F32, ctx)
            hid_t = sb("hid_t", [P, 2, HC, P], F32, ctx)
            y = sb("y", [P, 2, F], F32, ctx)
            w_in, vec_in, split, lane = sem("w_in"), sem("vec_in_moe"), sem("bias_split"), sem("expert_lane")
            xt_in = [sem(f"xt_in{k}") for k in range(2)]
            y_out = [sem(f"y_out{k}") for k in range(2)]
            x_turned, x_scaled = sem("x_turned"), sem("x_scaled")
            h_done, h_act, h_turned, h_kept = sem("h_done"), sem("h_act"), sem("h_turned"), sem("h_kept")
            y_done, y_kept, sel1_ready, sel2_ready = sem("y_done"), sem("y_kept"), sem("sel1_ready"), sem("sel2_ready")

            def each(eng, lo, hi, body):
                n = (hi - lo) // 2
                if n:
                    with eng.Fori(0, n) as i:
                        body(2 * i + lo, lo % 2)
                        body(2 * i + lo + 1, (lo + 1) % 2)
                if (hi - lo) % 2:
                    body(hi - 1, (hi - 1) % 2)

            with nc.Block() as block:
                @block.sync
                def _(sp):
                    for e in range(EXPERTS):
                        sp.dma_start(w1[:, e], t["L0_ffn_W1"][e].rearrange("(c p) n -> p c n", p=P)).then_inc(w_in.h, 16)
                        sp.dma_start(w2[:, e], t["L0_ffn_W2"][e].rearrange("(c p) n -> p c n", p=P)).then_inc(w_in.h, 16)

                    def load(k, par):
                        sp.dma_start(xt[:, par, :], slot_rows[bass.ds(k * P, P), :]).then_inc(xt_in[par].h, 16)

                    load(0, 0)
                    load(1, 1)

                    def reload(k, par):
                        sp.wait_ge(x_turned.h, k + 1)
                        load(k + 2, par)

                    def store(k, par):
                        sp.wait_ge(y_kept.h, k + 1)
                        sp.dma_start(slot_out[bass.ds(k * P, P), :], y[:, par, :]).then_inc(y_out[par].h, 16)

                    def body(k, par):
                        reload(k, par)
                        store(k - 3, 1 - par)

                    each(sp, 0, 3, reload)
                    each(sp, 3, MT - 2, body)
                    each(sp, MT - 5, MT, store)
                    for s in y_out:
                        sp.wait_ge(s.h, 16 * (MT // 2))

                @block.gpsimd
                def _(g):
                    for j in range(3):
                        g.iota(expert_i[32 * j:32 * j + 32, :], [[0, 1]], base=0, channel_multiplier=1).then_inc(lane.h, 1)

                @block.vector
                def _(v):
                    v.memset(bias[:], 0.0).then_inc(v_step.h, 1)
                    v.wait_ge(v_step.h, v_step.next())
                    v.wait_ge(lane.h, 3)
                    v.tensor_copy(expert_f[:], expert_i[:]).then_inc(v_step.h, 1)
                    v.wait_ge(v_step.h, v_step.next())
                    v.wait_ge(vec_in.h, 16 * (2 + 2 * EXPERTS))
                    for j in range(3):
                        part = bias[32 * j:32 * j + EXPERTS, :]
                        v.tensor_copy(part, bias_f[:]).then_inc(v_step.h, 1)
                        v.wait_ge(v_step.h, v_step.next())
                        if j < 2:
                            v.tensor_tensor(bias_f[:], bias_f[:], part, ALU.subtract).then_inc(v_step.h, 1)
                            v.wait_ge(v_step.h, v_step.next())
                    v.nop().then_inc(split.h, 1)

                    def select(sel, ready, k, par):
                        v.tensor_scalar(sel[:, par, :], tile_expert[0:96, bass.ds(k, 1)].to_broadcast([96, P]), expert_f[:], None, ALU.is_equal).then_inc(ready.h, 1)

                    def keep_y(k, par):
                        v.wait_ge(y_done.h, k + 1)
                        wait_earlier(v, y_out[par], k, par, 16)
                        v.tensor_copy(y[:, par, :], ps[6 + par][:, 0:F]).then_inc(y_kept.h, 1)

                    def keep_h(k, par):
                        for j in range(2):
                            v.wait_ge(h_turned.h, 2 * k + j + 1)
                            v.tensor_copy(hid_t[:, par, 4 * j:4 * j + 4, :].rearrange("p c n -> p (c n)"), ps[4 + j][:]).then_inc(h_kept.h, 1)

                    select(sel1, sel1_ready, 0, 0)
                    select(sel1, sel1_ready, 1, 1)
                    select(sel2, sel2_ready, 0, 0)
                    keep_h(0, 0)
                    select(sel1, sel1_ready, 2, 0)
                    select(sel2, sel2_ready, 1, 1)

                    def body(k, par):
                        keep_y(k - 1, 1 - par)
                        keep_h(k, par)
                        select(sel1, sel1_ready, k + 2, par)
                        select(sel2, sel2_ready, k + 1, 1 - par)

                    body(1, 1)
                    body(2, 0)
                    each(v, 3, MT - 3, body)
                    body(MT - 3, (MT - 3) % 2)
                    for k in (MT - 2, MT - 1):
                        keep_y(k - 1, (k - 1) % 2)
                        keep_h(k, k % 2)
                        if k + 1 < MT:
                            select(sel2, sel2_ready, k + 1, (k + 1) % 2)
                    keep_y(MT - 1, (MT - 1) % 2)

                @block.scalar
                def _(a):
                    with nc.allow_non_contiguous_dma("vectors of 256 features onto partitions"):
                        for e in range(EXPERTS):
                            a.dma_start(lng[:, :, e], t["L0_ffn_ln_g"][e].rearrange("(c p) -> p c", p=P)).then_inc(vec_in.h, 16)
                            a.dma_start(lnb[:, :, e], t["L0_ffn_ln_b"][e].rearrange("(c p) -> p c", p=P)).then_inc(vec_in.h, 16)
                    a.dma_start(bias_f[:, 0:HID], t["L0_ffn_b1"]).then_inc(vec_in.h, 16)
                    a.dma_start(bias_f[:, HID:HID + F], t["L0_ffn_b2"]).then_inc(vec_in.h, 16)
                    a.wait_ge(vec_in.h, 16 * (2 + 2 * EXPERTS))

                    def scale_x(k, par):
                        e = a.value_load(tile_expert_i[0:1, bass.ds(k, 1)], min_val=0, max_val=EXPERTS - 1)
                        a.wait_ge(x_turned.h, k + 1)
                        for c in range(FC):
                            op = a.activation(xe[:, par, c, :], ps[par][:, c * P:(c + 1) * P], ACT.Identity,
                                              bias=lnb[:, c, bass.ds(e, 1)], scale=lng[:, c, bass.ds(e, 1)])
                        op.then_inc(x_scaled.h, 1)

                    def act_h(k, par):
                        for j in range(2):
                            a.wait_ge(h_done.h, 2 * k + j + 1)
                            a.activation(hid[:, par, j * 512:(j + 1) * 512], ps[2 + j][:], ACT.Gelu).then_inc(h_act.h, 1)

                    scale_x(0, 0)
                    scale_x(1, 1)
                    act_h(0, 0)

                    def body(k, par):
                        act_h(k + 1, 1 - par)
                        scale_x(k + 2, par)

                    each(a, 0, MT - 2, body)
                    act_h(MT - 1, (MT - 1) % 2)

                @block.tensor
                def _(pe):
                    def turn_x(k, par):
                        pe.wait_ge(xt_in[par].h, (k - par) * 8 + 16)
                        for c in range(FC):
                            mm = pe.transpose(ps[par][:, c * P:(c + 1) * P], xt[:, par, c * P:(c + 1) * P], ident[:])
                        mm.then_inc(x_turned.h, 1)

                    def up(k, par):
                        e = pe.value_load(tile_expert_i[0:1, bass.ds(k, 1)], min_val=0, max_val=EXPERTS - 1)
                        pe.wait_ge(x_scaled.h, k + 1)
                        pe.wait_ge(sel1_ready.h, k + 1)
                        for j in range(2):
                            pe.matmul(ps[2 + j][:], sel1[:, par, :], bias[:, j * 512:(j + 1) * 512], start=True, stop=False)
                            for c in range(FC):
                                mm = pe.matmul(ps[2 + j][:], xe[:, par, c, :], w1[:, bass.ds(e, 1), c, j * 512:(j + 1) * 512].rearrange("p a n -> p (a n)"),
                                               start=False, stop=(c == FC - 1))
                            mm.then_inc(h_done.h, 1)

                    def turn_h(k, par):
                        for j in range(2):
                            pe.wait_ge(h_act.h, 2 * k + j + 1)
                            for c in range(4):
                                mm = pe.transpose(ps[4 + j][:, c * P:(c + 1) * P], hid[:, par, (4 * j + c) * P:(4 * j + c + 1) * P], ident[:])
                            mm.then_inc(h_turned.h, 1)

                    def down(k, par):
                        e = pe.value_load(tile_expert_i[0:1, bass.ds(k, 1)], min_val=0, max_val=EXPERTS - 1)
                        pe.wait_ge(h_kept.h, 2 * k + 2)
                        pe.wait_ge(sel2_ready.h, k + 1)
                        pe.matmul(ps[6 + par][:, 0:F], sel2[:, par, :], bias[:, HID:HID + F], start=True, stop=False)
                        for c in range(HC):
                            mm = pe.matmul(ps[6 + par][:, 0:F], hid_t[:, par, c, :], w2[:, bass.ds(e, 1), c, :].rearrange("p a n -> p (a n)"),
                                           start=False, stop=(c == HC - 1))
                        mm.then_inc(y_done.h, 1)

                    turn_x(0, 0)
                    turn_x(1, 1)
                    pe.wait_ge(w_in.h, 16 * 2 * EXPERTS)
                    pe.wait_ge(split.h, 1)
                    up(0, 0)
                    pe.wait_ge(h_act.h, 2)
                    up(1, 1)
                    turn_h(0, 0)
                    pe.wait_ge(x_scaled.h, 1)
                    turn_x(2, 0)

                    def body(k, par):
                        pe.wait_ge(h_act.h, 2 * k + 2)
                        up(k + 1, 1 - par)
                        down(k - 1, 1 - par)
                        turn_h(k, par)
                        pe.wait_ge(x_scaled.h, k + 1)
                        turn_x(k + 2, par)

                    each(pe, 1, MT - 3, body)
                    body(MT - 3, (MT - 3) % 2)
                    pe.wait_ge(h_act.h, 2 * (MT - 2) + 2)
                    up(MT - 1, (MT - 1) % 2)
                    for k in (MT - 2, MT - 1):
                        down(k - 1, (k - 1) % 2)
                        turn_h(k, k % 2)
                    down(MT - 1, (MT - 1) % 2)

    experts()

    bigs = ExitStack()
    acc = sb("acc", [P, NT, F], F32, bigs)
    node_terms = sb("node_terms", [P, NT, HEADS], F32, bigs)
    HCOLS = HEADS * HROW
    WCOLS = HCOLS + HEADS

    def combine():
        with ExitStack() as ctx:
            norm = NodeNorm(ctx, "ln2")
            expert_rows = sb("y_rows", [P, 2, 2, F], F32, ctx)
            y_in = [sem(f"y_in{k}") for k in range(2)]
            y_used, slot_idx, y_first = sem("y_used"), sem("slot_idx_back"), sem("y_first")
            stage2 = sb("stage2", [P, 2, HCOLS], F32, ctx)
            wcat = sb("wcat", [P, FC, WCOLS], F32, ctx)
            attn = sb("attn", [P, 2, F], F32, ctx)
            prod = sb("prod", [P, F], F32, ctx)
            rows_ready, attn_in, wcat_ready = sem("z2_staged"), sem("attn_in"), sem("wcat_ready")
            ft_out = [sem(f"ft_out{k}") for k in range(2)]
            ft_ready = sem("ft_ready")
            with nc.Block() as block:
                @block.sync
                def _(sp):
                    sp.dma_start(acc[:], resid.rearrange("(d p) f -> p d f", p=P)).then_inc(x_loaded.h, 16)
                    for c in range(FC):
                        sp.dma_start(wcat[:, c, 0:HCOLS].rearrange("p (h d) -> p h d", d=HROW)[:, :, 0:HD],
                                     t["L1_gnn_W_fc"][c * P:(c + 1) * P, :].rearrange("p (h d) -> p h d", d=HD)).then_inc(attn_in.h, 16)
                    for j, name in enumerate(("attn_h", "attn_t")):
                        sp.dma_start(attn[:, j, :], t[f"L1_gnn_{name}"].rearrange("(a h) d -> a (h d)", a=1).to_broadcast([P, F])).then_inc(attn_in.h, 16)
                    for d, k in node_tiles(sp):
                        sp.wait_ge(ft_ready.h, d + 1)
                        sp.dma_start(attn_table[bass.ds(d * P, P), :], stage2[:, k, :]).then_inc(ft_out[k].h, 16)
                    sp.wait_ge(ft_out[0].h, 16 * (NT // 2 + 1))
                    sp.wait_ge(ft_out[1].h, 16 * (NT // 2))

                @block.gpsimd
                def _(g):
                    for d, k in node_tiles(g):
                        g.wait_ge(y_used.h, d + 1)
                        g.tensor_copy(idx[:, k, 0:2], slots[:, :, bass.ds(d, 1)].rearrange("p a d -> p (a d)")).then_inc(slot_idx.h, 1)
                        g.wait_ge(slot_idx.h, d + 1)
                        g.tensor_tensor(carrier[:], psrc[:, 0:1], psrc[:, 0:1], ALU.add)
                        for j in range(2):
                            g.indirect_dma_start(expert_rows[:, k, j, :], None, slot_out,
                                                 bass.IndirectOffsetOnAxis(ap=idx[:, k, j:j + 1], axis=0)).then_inc(y_in[k].h, 16)

                @block.vector
                def _(v):
                    v.sem_inc(y_used.h, 2)
                    v.wait_ge(attn_in.h, 16 * (FC + 2))
                    for c in range(FC):
                        heads = wcat[:, c, 0:HCOLS].rearrange("p (h d) -> p h d", d=HROW)
                        for j, dst in enumerate((heads[:, :, HD], wcat[:, c, HCOLS:WCOLS])):
                            v.tensor_tensor(prod[:].rearrange("p (h d) -> p h d", d=HD), heads[:, :, 0:HD], attn[:, j, :].rearrange("p (h d) -> p h d", d=HD), ALU.mult).then_inc(v_step.h, 1)
                            v.wait_ge(v_step.h, v_step.next())
                            v.tensor_reduce(dst, prod[:].rearrange("p (h d) -> p h d", d=HD), AX.X, ALU.add).then_inc(v_step.h, 1)
                            v.wait_ge(v_step.h, v_step.next())
                    v.nop().then_inc(wcat_ready.h, 1)
                    v.wait_ge(x_loaded.h, x_loaded.base + 16)
                    for d, k in node_tiles(v):
                        v.wait_ge(y_in[k].h, 32 * (d // 2 + 1) if isinstance(d, int) else (d - k) * 16 + 32)
                        row = rows_of(acc, d)
                        v.scalar_tensor_tensor(row, expert_rows[:, k, 0, :], gate[:, 0, bass.ds(d, 1)], row, ALU.mult, ALU.add).then_inc(y_first.h, 1)
                        v.wait_ge(y_first.h, d + 1)
                        v.scalar_tensor_tensor(row, expert_rows[:, k, 1, :], gate[:, 1, bass.ds(d, 1)], row, ALU.mult, ALU.add).then_inc(y_used.h, 1)
                    v.wait_ge(y_used.h, NT + 2)
                    norm.stats_of(v, acc)

                    def stage_rows(d, k):
                        v.wait_ge(turned.h, turned.base + d + 1)
                        norm.rows(v, acc, stage[:, k, :], d, rows_ready)

                    def keep(d, k):
                        v.wait_ge(projected.h, projected.base + d + 1 + 2)
                        wait_earlier(v, ft_out[k], d, k, 16)
                        v.tensor_copy(rows_of(node_terms, d), ps[2 + k][:, HCOLS:WCOLS])
                        v.tensor_copy(stage2[:, k, :], ps[2 + k][:, 0:HCOLS]).then_inc(projected_out.h, 1)
                        v.wait_ge(projected_out.h, projected_out.base + d + 1 + 2)
                        v.nop().then_inc(ft_ready.h, 1)

                    two_ahead(v, stage_rows, keep)

                @block.scalar
                def _(a):
                    norm.root.scalar(a)
                    turned_to_lhs(a)

                @block.tensor
                def _(pe):
                    pe.wait_ge(wcat_ready.h, 1)
                    turn_and_multiply(pe, wcat, rows_ready, WCOLS)
            x_loaded.base += 16
            project_counted()
            stored.base -= 16 * NT

    with ExitStack() as proj:
        stage = sb("stage", [P, 2, F], F32, proj)
        lhs = sb("lhs", [P, 2, FC, P], F32, proj)
        combine()

    QUADS = NPAIR // (4 * G)
    GROUPS = 4 * QUADS
    assert GROUPS * G == NPAIR
    lateb = ExitStack()
    sums = sb("sums", [P, NT, HCOLS], F32, lateb)

    def attend():
        with ExitStack() as ctx:
            rows = sb("rows", [P, 4, G, HCOLS], F32, ctx)
            hot = sb("hot", [P, 4, G, P], F32, ctx)
            hot_b = sb("hot_b", [P, 4, G, P], BF16, ctx)
            hot_t = sb("hot_t", [P, 2, G, P], BF16, ctx)
            spread = sb("spread", [P, 16, G * HEADS], BF16, ctx)
            spread_i = sb("spread_i", [P, G * HEADS], I32, ctx)
            spread_f = sb("spread_f", [P, G * HEADS], F32, ctx)
            lane_i = sb("lane_i", [P, 16], I32, ctx)
            lane = sb("lane", [P, 16], F32, ctx)
            edge_terms = sb("edge_terms", [P, 4, G, HEADS], F32, ctx)
            terms = sb("terms", [P, G, HEADS], F32, ctx)
            total = sb("total", [P, G, HEADS], F32, ctx)
            logit = sb("logit", [P, 2, 2 * G, HEADS], F32, ctx)
            ident_b = sb("ident_b", [P, P], BF16, ctx)
            starts = sb("starts", [G * HEADS, P], F32, ctx)
            runmax = sb("runmax", [P, P], F32, ctx)
            cand = sb("cand", [P, 3, G, HEADS + 1], F32, ctx)
            node_rest = sb("node_rest", [P, 2, NT, HEADS], F32, ctx)
            node_parts = sb("node_parts", [P, NT, 3, HEADS], BF16, ctx)
            dst_terms = sb("dst_terms", [P, G, HEADS], F32, ctx)
            run_best = sb("run_best", [P, G, HEADS], F32, ctx)
            edge_peak = sb("edge_peak", [P, G, HEADS], F32, ctx)
            unmet = sb("unmet", [P, G], F32, ctx)
            best = sb("best", [P, HEADS, G + 1], F32, ctx)
            upto = sb("upto", [P, HEADS, G + 1], F32, ctx)
            peak = sb("peak", [P, 3, HEADS, G + 1], F32, ctx)
            changes = sb("changes", [P, HEADS * (G + 1) + 1], F32, ctx)
            below = sb("below", [P, G, HEADS], F32, ctx)
            below_pos = sb("below_pos", [P, G, HEADS], F32, ctx)
            growth = sb("growth", [P, HEADS], F32, ctx)
            shrink = sb("shrink", [P, HEADS], F32, ctx)
            edge_terms_in = [sem(f"edge_terms_in{u}") for u in range(4)]
            terms_used = sem("terms_used")
            changes_free, changes_set = sem("changes_free"), sem("changes_set")
            rows_in = [sem(f"rows_in{u}") for u in range(4)]
            rows_used, patterns, patterns_set = sem("rows_used"), sem("patterns"), sem("patterns_set")
            marked, mark_step, marks_turned, marks_kept = sem("marked"), sem("mark_step"), sem("marks_turned"), sem("marks_kept")
            starts_spread, starts_kept, terms_spread = sem("starts_spread"), sem("starts_kept"), sem("terms_spread")
            logit_set, logit_turned, scanned, run_turned = sem("logit_set"), sem("logit_turned"), sem("run_scanned"), sem("run_turned")
            cand_set, met, peaked, peak_spread = sem("cand_set"), sem("met"), sem("peaked"), sem("peak_spread")
            below_ready, weighed, weigh_step = sem("below_ready"), sem("weighed"), sem("weigh_step")
            growth_ready, shrink_ready = sem("growth_ready"), sem("shrink_ready")
            messages_ready, summed, sums_added = sem("messages_ready"), sem("pair_summed"), sem("sums_added")

            def steps(begin, both, last):

                def run(eng):
                    begin()
                    with eng.Fori(0, QUADS - 1) as i:
                        for u in range(4):
                            both(4 * i + u, u)
                    for q in range(GROUPS - 4, GROUPS - 1):
                        both(q, q % 4)
                    last(GROUPS - 1, (GROUPS - 1) % 4)

                return run

            def upper(a):
                return a.bitcast(BF16)[:, :, :, 1::2]

            def there(n):
                return not isinstance(n, int) or n < GROUPS

            with nc.Block() as block:
                @block.sync
                def _(sp):
                    with sp.Fori(0, QUADS) as i:
                        for u in range(4):
                            sp.wait_ge(terms_used.h, 4 * i + u + 1)
                            sp.dma_start(edge_terms[:, u].rearrange("p j e -> p (j e)"), ee_table[:, bass.ds((4 * i + u) * G * HEADS, G * HEADS)]).then_inc(edge_terms_in[u].h, 16)

                @block.gpsimd
                def _(g):
                    g.iota(spread_i[:], [[1, G], [0, HEADS]], base=0, channel_multiplier=0).then_inc(patterns.h, 1)
                    g.iota(lane_i[:], [[-G, 16]], base=0, channel_multiplier=1).then_inc(patterns.h, 1)
                    with g.Fori(0, QUADS) as i:
                        for u in range(4):
                            q = 4 * i + u
                            g.wait_ge(rows_used.h, q + 1)
                            g.tensor_copy(idx[:, u, :], psrc[:, bass.ds(q * G, G)]).then_inc(idx_ready.h, 1)
                            g.wait_ge(idx_ready.h, idx_ready.base + q + 1)
                            g.tensor_tensor(carrier[:], psrc[:, 0:1], psrc[:, 0:1], ALU.add)
                            for b in range(G):
                                g.indirect_dma_start(rows[:, u, b, :], None, attn_table,
                                                     bass.IndirectOffsetOnAxis(ap=idx[:, u, b:b + 1], axis=0)).then_inc(rows_in[u].h, 16)

                @block.vector
                def _(v):
                    def heads(u):
                        return rows[:, u].rearrange("p j (e d) -> p j e d", d=HROW)

                    def logits_steps(n, turn, u):

                        def spread_sum():
                            v.wait_ge(terms_spread.h, n + 1)
                            v.tensor_reduce(dst_terms[:], ps[0][:, 2 * P:2 * P + 3 * G * HEADS].rearrange("p (j k e) -> p j e k", k=3, e=HEADS), AX.X, ALU.add)

                        def known_terms():
                            v.wait_ge(edge_terms_in[u].h, 16 * (turn + 1))
                            v.tensor_tensor(terms[:], edge_terms[:, u], dst_terms[:], ALU.add).then_inc(terms_used.h, 1)

                        def all_terms():
                            v.wait_ge(rows_in[u].h, 16 * G * (turn + 1))
                            v.tensor_tensor(total[:], heads(u)[:, :, :, HD], terms[:], ALU.add)

                        def leaky():
                            v.scalar_tensor_tensor(logit[:, u % 2, 0:G, :], total[:], SLOPE, total[:], ALU.mult, ALU.max).then_inc(logit_set.h, 1)

                        return spread_sum, known_terms, all_terms, leaky

                    def logits(n, turn, u):
                        for step in logits_steps(n, turn, u):
                            step()
                            v.drain()

                    def run_maxima(n):
                        v.wait_ge(logit_turned.h, n + 1)
                        v.tensor_tensor_scan(runmax[0:G * HEADS, :], starts[:], ps[0][0:G * HEADS, 0:P], -BIG, ALU.add, ALU.max).then_inc(scanned.h, 1)

                    def candidates(n, beside):
                        last = plast[:, bass.ds(n * G, G)].rearrange("p (j a) -> p j a", a=1)
                        v.tensor_copy(cand[:, 0, :, HEADS:HEADS + 1], last)
                        v.wait_ge(run_turned.h, n + 1)
                        v.tensor_tensor(cand[:, 0, :, 0:HEADS], ps[1][:, 0:G * HEADS].rearrange("p (j e) -> p j e", e=HEADS),
                                        last.to_broadcast([P, G, HEADS]), ALU.mult)
                        beside[0]()
                        v.drain()
                        v.tensor_tensor(cand[:, 1], cand[:, 0], upper(cand[:])[:, 0], ALU.subtract)
                        beside[1]()
                        v.drain()
                        v.tensor_tensor(cand[:, 2], cand[:, 1], upper(cand[:])[:, 1], ALU.subtract).then_inc(cand_set.h, 1)
                        beside[2]()

                    def node_maxima(n, beside):
                        v.drain()
                        v.tensor_copy(best[:, :, 0:1], upto[:, :, G:G + 1])
                        v.wait_ge(met.h, n + 1)
                        got = ps[1][:, P:P + 3 * G * (HEADS + 1)].rearrange("p (j k e) -> p j e k", k=3, e=HEADS + 1)
                        v.tensor_reduce(run_best[:], got[:, :, 0:HEADS, :], AX.X, ALU.add)
                        v.tensor_scalar(unmet[:].rearrange("p (j a) -> p j a", a=1), got[:, :, HEADS:HEADS + 1, 0], BIG, -BIG, ALU.mult, ALU.add)
                        beside[0]()
                        v.drain()
                        v.tensor_tensor(best[:, :, 1:G + 1].rearrange("p e j -> p j e"), run_best[:],
                                        unmet[:].rearrange("p (j a) -> p j a", a=1).to_broadcast([P, G, HEADS]), ALU.add)
                        beside[1]()
                        v.drain()
                        v.wait_ge(changes_set.h, n + 1)
                        flat = HEADS * (G + 1)
                        up = upto[:].rearrange("p e j -> p (e j)")
                        v.tensor_tensor_scan(up, changes[:, 0:flat], best[:].rearrange("p e j -> p (e j)"), -BIG, ALU.add, ALU.max)
                        beside[2]()
                        v.drain()
                        v.tensor_tensor_scan(peak[:, 0].rearrange("p e j -> p (e j)")[:, ::-1], changes[:, flat:0:-1], up[:, ::-1], -BIG, ALU.add, ALU.max)
                        beside[3]()
                        for k in range(2):
                            v.drain()
                            op = v.tensor_tensor(peak[:, k + 1], peak[:, k], upper(peak[:])[:, k], ALU.subtract)
                        op.then_inc(peaked.h, 1)
                        v.scalar_tensor_tensor(growth[:], best[:, :, 0], rows_of(change, n)[:, 1:2], peak[:, 0, :, 1], ALU.add, ALU.subtract).then_inc(growth_ready.h, 1)

                    def distances(n, u):
                        v.wait_ge(peak_spread.h, n + 1)
                        v.tensor_reduce(edge_peak[:], ps[2][:, 0:3 * G * HEADS].rearrange("p (j k e) -> p j e k", k=3, e=HEADS), AX.X, ALU.add)
                        v.drain()
                        v.tensor_tensor(below[:], edge_peak[:], logit[:, u % 2, 0:G, :], ALU.subtract).then_inc(below_ready.h, 1)

                    def messages(q, u, half):
                        if half == 0:
                            v.wait_ge(weighed.h, q + 1)
                        m = heads(u)[:, 4 * half:4 * half + 4]
                        v.tensor_tensor(m[:, :, :, 0:HD], m[:, :, :, 0:HD], m[:, :, :, HD:HROW].to_broadcast([P, 4, HEADS, HD]), ALU.mult).then_inc(messages_ready.h, 1)

                    def sums_rows(q):
                        tiles = node_tiles_of(v, q)
                        for d in tiles:
                            v.lower_ap(rows_of(sums, d))
                        return tiles

                    def shrink_sums(q, tiles):
                        row = rows_of(sums, tiles[0]).rearrange("p (e d) -> p e d", d=HROW)
                        v.wait_ge(shrink_ready.h, q + 1)
                        v.tensor_tensor(row, row, shrink[:].rearrange("p (e a) -> p e a", a=1).to_broadcast([P, HEADS, HROW]), ALU.mult)

                    def add_sum(q, tiles, b):
                        row = rows_of(sums, tiles[b])
                        if b % 2 == 0:
                            v.wait_ge(summed.h, 4 * q + b // 2 + 1)
                        op = v.tensor_tensor(row, row, ps[4 + b % 4][:, 0:HCOLS], ALU.add)
                        if b % 2:
                            op.then_inc(sums_added.h, 1)

                    def add_sums(q, tiles, pairs):
                        for b in pairs:
                            v.drain()
                            add_sum(q, tiles, b)

                    v.sem_inc(rows_used.h, 4)
                    v.sem_inc(terms_used.h, 4)
                    v.sem_inc(sums_added.h, 2)
                    v.memset(logit[:, :, G:2 * G, :], 0.0)
                    v.tensor_copy(ident_b[:], ident[:])
                    v.memset(runmax[G * HEADS:P, :], 0.0)
                    v.memset(upto[:], -BIG)
                    v.memset(changes[:], -BIG).then_inc(changes_free.h, 1)
                    v.memset(sums[:], 0.0)
                    rest = node_terms[:]
                    for k in range(3):
                        v.tensor_copy(node_parts[:, :, k, :], rest.bitcast(BF16)[:, :, 1::2]).then_inc(v_step.h, 1)
                        v.wait_ge(v_step.h, v_step.next())
                        if k < 2:
                            v.tensor_tensor(node_rest[:, k], rest, rest.bitcast(BF16)[:, :, 1::2], ALU.subtract).then_inc(v_step.h, 1)
                            v.wait_ge(v_step.h, v_step.next())
                            rest = node_rest[:, k]
                    v.wait_ge(patterns.h, 2)
                    v.tensor_copy(spread_f[:], spread_i[:]).then_inc(v_step.h, 1)
                    v.wait_ge(v_step.h, v_step.next())
                    v.tensor_copy(lane[:], lane_i[:]).then_inc(v_step.h, 1)
                    v.wait_ge(v_step.h, v_step.next())
                    v.tensor_tensor(spread[:], spread_f[:].rearrange("p (g m) -> p g m", g=1).to_broadcast([P, 16, G * HEADS]),
                                    lane[:].rearrange("p (g m) -> p g m", m=1).to_broadcast([P, 16, G * HEADS]), ALU.is_equal).then_inc(patterns_set.h, 1)

                    def nothing():
                        pass

                    def begin():
                        logits(0, 0, 0)
                        run_maxima(0)
                        candidates(0, [nothing] * 3)
                        node_maxima(0, logits_steps(1, 0, 1))
                        v.drain()
                        distances(0, 0)
                        run_maxima(1)

                    def turn_of(q, u, k):
                        return (q + k - (u + k) % 4) // 4

                    def both(q, u):
                        n, un, u2 = q + 1, (u + 1) % 4, (u + 2) % 4
                        messages(q, u, 0)
                        messages(q, u, 1)
                        tiles = sums_rows(q)
                        v.drain()
                        candidates(n, (lambda: shrink_sums(q, tiles), lambda: add_sum(q, tiles, 0), nothing))
                        add_sums(q, tiles, (1, 2, 3))
                        node_maxima(n, logits_steps(n + 1, turn_of(q, u, 2), u2) if there(n + 1) else [nothing] * 4)
                        add_sums(q, tiles, (4, 5))
                        distances(n, un)
                        if there(n + 1):
                            run_maxima(n + 1)
                        add_sums(q, tiles, (6, 7))

                    def last(q, u):
                        messages(q, u, 0)
                        messages(q, u, 1)
                        tiles = sums_rows(q)
                        v.drain()
                        shrink_sums(q, tiles)
                        add_sums(q, tiles, range(8))

                    steps(begin, both, last)(v)

                @block.scalar
                def _(a):
                    def mark(n, u):
                        for b in range(G):
                            op = a.activation(hot[:, u, b, :], iota_f[:], ACT.Abs, bias=pdl[:, bass.ds(n * G + b, 1)], scale=-1.0)
                        op.then_inc(mark_step.h, 1)
                        a.wait_ge(mark_step.h, n + 1)
                        a.activation(hot_b[:, u], hot[:, u], ACT.Relu, bias=ones[:, 0:1], scale=-1.0)
                        a.activation(hot[:, u], hot[:, u], ACT.Relu, bias=ones[:, 0:1], scale=-1.0).then_inc(marked.h, 1)

                    def keep_marks(n, u):
                        a.wait_ge(marks_turned.h, n + 1)
                        a.activation(hot_t[:, u % 2].rearrange("p b n -> p (b n)"), ps[3][:].bitcast(BF16), ACT.Copy).then_inc(marks_kept.h, 1)

                    def keep_starts(n):
                        a.wait_ge(starts_spread.h, n + 1)
                        a.activation(starts[:], ps[0][0:G * HEADS, P:2 * P], ACT.Copy).then_inc(starts_kept.h, 1)

                    def weigh(n, u):
                        a.wait_ge(growth_ready.h, n + 1)
                        a.activation(shrink[:], growth[:], ACT.Exp).then_inc(shrink_ready.h, 1)
                        a.wait_ge(below_ready.h, n + 1)
                        a.activation(below_pos[:], below[:], ACT.Relu).then_inc(weigh_step.h, 1)
                        a.wait_ge(weigh_step.h, n + 1)
                        a.activation(rows[:, u].rearrange("p j (e d) -> p j e d", d=HROW)[:, :, :, HD], below_pos[:], ACT.Exp, scale=-1.0).then_inc(weighed.h, 1)

                    def expand_changes(n):
                        if isinstance(n, int) and n == 0:
                            a.wait_ge(changes_free.h, 1)
                        else:
                            a.wait_ge(peaked.h, n)
                        a.activation(changes[:, 0:HEADS * (G + 1)].rearrange("p (e j) -> p e j", j=G + 1),
                                     change[:, bass.ds(n, 1), :].to_broadcast([P, HEADS, G + 1]), ACT.Copy).then_inc(changes_set.h, 1)

                    def chain(n, u):
                        if there(n + 1):
                            keep_marks(n + 1, (u + 1) % 4)
                            keep_starts(n + 1)
                        if there(n + 2):
                            mark(n + 2, (u + 2) % 4)
                        weigh(n, u)
                        if there(n + 1):
                            expand_changes(n + 1)

                    def begin():
                        expand_changes(0)
                        keep_starts(0)
                        mark(0, 0)
                        mark(1, 1)
                        keep_marks(0, 0)
                        chain(0, 0)

                    steps(begin, lambda q, u: chain(q + 1, (u + 1) % 4), lambda q, u: None)(a)

                @block.tensor
                def _(pe):
                    def spread_starts(n):
                        if not isinstance(n, int) or n > 0:
                            pe.wait_ge(scanned.h, n)
                        pe.matmul(ps[0][0:G * HEADS, P:2 * P], spread[:, bass.ds(n % 16, 1), :].rearrange("p a m -> p (a m)"),
                                  run_start[:, bass.ds(n // 16, 1), :].rearrange("p a m -> p (a m)"), start=True, stop=True).then_inc(starts_spread.h, 1)

                    def turn_logits(n, u):
                        pe.wait_ge(logit_set.h, n + 1)
                        pe.transpose(ps[0][:, 0:P], logit[:, u % 2].rearrange("p j e -> p (j e)"), ident[:]).then_inc(logit_turned.h, 1)

                    turned_marks = ps[3][:].bitcast(BF16)

                    def turn_marks(n, u):
                        pe.wait_ge(marked.h, n + 1)
                        if not isinstance(n, int) or n > 0:
                            pe.wait_ge(marks_kept.h, n)
                        for b in range(G):
                            mm = pe.transpose(turned_marks[:, b * P:(b + 1) * P], hot_b[:, u, b, :], ident_b[:])
                        mm.then_inc(marks_turned.h, 1)

                    def spread_terms(n, u):
                        tiles = node_tiles_of(pe, n)
                        pe.wait_ge(marks_kept.h, n + 1)
                        pe.wait_ge(starts_kept.h, n + 1)
                        for b in range(G):
                            mm = pe.matmul(ps[0][:, 2 * P + 3 * b * HEADS:2 * P + 3 * (b + 1) * HEADS], hot_t[:, u % 2, b, :],
                                           node_parts[:, bass.ds(tiles[b], 1)].rearrange("p a k e -> p (a k e)"), start=True, stop=True)
                        mm.then_inc(terms_spread.h, 1)

                    def turn_runs(n):
                        pe.wait_ge(scanned.h, n + 1)
                        pe.transpose(ps[1][:, 0:P], runmax[:], ident[:]).then_inc(run_turned.h, 1)

                    def meet(n, u):
                        pe.wait_ge(cand_set.h, n + 1)
                        for b in range(G):
                            mm = pe.matmul(ps[1][:, P + 3 * b * (HEADS + 1):P + 3 * (b + 1) * (HEADS + 1)].rearrange("p (k e) -> p k e", k=3),
                                           hot_b[:, u, b, :], upper(cand[:])[:, :, b, :], start=True, stop=True)
                        mm.then_inc(met.h, 1)

                    def spread_peaks(n, u):
                        pe.wait_ge(peaked.h, n + 1)
                        for b in range(G):
                            mm = pe.matmul(ps[2][:, 3 * b * HEADS:3 * (b + 1) * HEADS].rearrange("p (k e) -> p k e", k=3),
                                           hot_t[:, u % 2, b, :], upper(peak[:])[:, :, :, b + 1], start=True, stop=True)
                        mm.then_inc(peak_spread.h, 1)

                    def sum_pairs(q, u, pairs):
                        for b in pairs:
                            if b % 4 == 0:
                                pe.wait_ge(messages_ready.h, 2 * q + b // 4 + 1)
                            if b % 2 == 0:
                                pe.wait_ge(sums_added.h, 4 * q + b // 2 + 1)
                            mm = pe.matmul(ps[4 + b % 4][:, 0:HCOLS], hot[:, u, b, :], rows[:, u, b, :], start=True, stop=True)
                            if b % 2:
                                mm.then_inc(summed.h, 1)

                    def release(q):
                        pe.wait_ge(summed.h, 4 * q + 4)
                        pe.sem_inc(rows_used.h, 1)

                    def begin():
                        pe.wait_ge(patterns_set.h, 1)
                        spread_starts(0)
                        turn_marks(0, 0)
                        spread_terms(0, 0)
                        turn_logits(0, 0)
                        turn_marks(1, 1)
                        turn_runs(0)
                        spread_starts(1)
                        spread_terms(1, 1)
                        meet(0, 0)
                        spread_peaks(0, 0)
                        turn_logits(1, 1)

                    def both(q, u):
                        n, un, u2 = q + 1, (u + 1) % 4, (u + 2) % 4
                        if there(n + 1):
                            turn_marks(n + 1, u2)
                        turn_runs(n)
                        if there(n + 1):
                            spread_starts(n + 1)
                        sum_pairs(q, u, range(4))
                        if there(n + 1):
                            spread_terms(n + 1, u2)
                        meet(n, un)
                        sum_pairs(q, u, (4, 5))
                        spread_peaks(n, un)
                        if there(n + 1):
                            turn_logits(n + 1, u2)
                        sum_pairs(q, u, (6, 7))
                        release(q)

                    def last(q, u):
                        sum_pairs(q, u, range(8))

                    steps(begin, both, last)(pe)
            idx_ready.base += GROUPS

    attend()

    ONE = NT // 7
    BW = ONE * P
    HALF = BW // 2
    TAKE = N // 2 - 1
    assert NT % 7 == 0

    def close_attention():
        with ExitStack() as ctx:
            den = sb("den", [P, NT, HEADS], F32, ctx)
            bias = sb("gat_bias", [P, F], F32, ctx)
            part = sb("part", [P, 2, F], F32, ctx)
            divided, biased, summed = sem("divided"), sem("biased"), sem("summed")
            with nc.Block() as block:
                @block.sync
                def _(sp):
                    sp.dma_start(bias[:], t["L1_gnn_bias"].rearrange("(a h) d -> a (h d)", a=1).to_broadcast([P, F])).then_inc(loaded.h, 16)

                @block.vector
                def _(v):
                    v.tensor_scalar(den[:], sums[:].rearrange("p t (h d) -> p t h d", d=HROW)[:, :, :, HD], 1.0 / BIG, None, ALU.max).then_inc(v_step.h, 1)
                    v.wait_ge(v_step.h, v_step.next())
                    v.reciprocal(den[:], den[:]).then_inc(v_step.h, 1)
                    v.wait_ge(v_step.h, v_step.next())
                    v.wait_ge(loaded.h, loaded.base + 16)
                    for d, k in node_tiles(v):
                        v.tensor_tensor(part[:, k, :].rearrange("p (h d) -> p h d", d=HD), rows_of(sums, d).rearrange("p (h d) -> p h d", d=HROW)[:, :, 0:HD],
                                        den[:, bass.ds(d, 1), :].rearrange("p a (h b) -> p (a h) b", b=1).to_broadcast([P, HEADS, HD]), ALU.mult).then_inc(divided.h, 1)
                        v.tensor_tensor(rows_of(acc, d), rows_of(acc, d), bias[:], ALU.add).then_inc(biased.h, 1)
                        v.wait_ge(divided.h, d + 1)
                        v.wait_ge(biased.h, d + 1)
                        v.tensor_tensor(rows_of(acc, d), rows_of(acc, d), part[:, k, :], ALU.add).then_inc(summed.h, 1)
                    v.wait_ge(summed.h, NT)
            loaded.base += 16

    close_attention()
    lateb.close()

    zt = sb("zt", [P, FC, NPAD], F32, bigs)

    def feed_forward():
        with ExitStack() as ctx:
            norm = NodeNorm(ctx, "ln3")
            stage = sb("stage", [P, 2, F], F32, ctx)
            wr = sb("wr3", [P, FC, 1], F32, ctx)
            br = sb("br3", [P, 1], F32, ctx)
            w1 = sb("w1_3", [P, FC, HID], F32, ctx)
            b1 = sb("b1_3", [P, HC], F32, ctx)
            w2 = sb("w2_3", [P, HC, F], F32, ctx)
            b2 = sb("b2_3", [P, F], F32, ctx)
            hid = sb("hid3", [P, HC, BW], F32, ctx)
            part = sb("part3", [P, 2, F], F32, ctx)
            weight = sb("weight", [P, NT], F32, ctx)
            key = sb("key", [P, NT], I32, ctx)
            sign = sb("sign", [P, NT], I32, ctx)
            half_i = sb("half_i", [P, 2, NT], I32, ctx)
            half = sb("half", [P, 2, NT], F32, ctx)
            node_i = sb("node3_i", [P, NT], I32, ctx)
            valid = sb("valid3", [P, NT], F32, ctx)
            junk = sb("junk3", [P, NT], F32, ctx)
            count = sb("count3", [P, 1], F32, ctx)
            cut = sb("cut", [P, 1], F32, ctx)
            trial = sb("trial", [P, 1], F32, ctx)
            reach = sb("reach", [P, 1], F32, ctx)
            quota = sb("quota", [P, 2], F32, ctx)
            above = sb("above", [P, NT], F32, ctx)
            ties = sb("ties", [P, NT], F32, ctx)
            runs = sb("runs", [P, NT], F32, ctx)
            taken = sb("taken", [P, NT], F32, ctx)
            rows_ready, zt_set, weights_in, numbered = sem("z3_staged"), sem("zt_set"), sem("weights_in"), sem("numbered3")
            routed, counted, summed = sem("routed"), sem("counted3"), sem("count_summed")
            up_done, up_act, down_done, part_set, out_set = sem("up_done"), sem("up_act"), sem("down_done"), sem("part_set"), sem("out_set")
            scaled, freed = sem("scaled"), sem("hid_freed")
            with nc.Block() as block:
                @block.sync
                def _(sp):
                    for c in range(FC):
                        sp.dma_start(wr[:, c, :], t["L1_ffn_wr"][c * P:(c + 1) * P, :]).then_inc(weights_in.h, 16)
                    sp.dma_start(br[:], t["L1_ffn_br"].rearrange("(a e) -> a e", a=1).to_broadcast([P, 1])).then_inc(weights_in.h, 16)
                    sp.dma_start(w1[:], t["L1_ffn_w1"].rearrange("(c p) n -> p c n", p=P)).then_inc(weights_in.h, 16)
                    with nc.allow_non_contiguous_dma("bias of the hidden units onto partitions"):
                        sp.dma_start(b1[:], t["L1_ffn_b1"].rearrange("(c p) -> p c", p=P)).then_inc(weights_in.h, 16)
                    sp.dma_start(w2[:], t["L1_ffn_w2"].rearrange("(c p) n -> p c n", p=P)).then_inc(weights_in.h, 16)
                    sp.dma_start(b2[:], t["L1_ffn_b2"].rearrange("(a n) -> a n", a=1).to_broadcast([P, F])).then_inc(weights_in.h, 16)
                    with sp.Fori(0, NT - 1) as d:
                        sp.wait_ge(out_set.h, d + 2)
                        sp.dma_start(out[bass.ds(d * P, P), :], rows_of(acc, d)).then_inc(stored.h, 16)
                    sp.wait_ge(out_set.h, NT + 1)
                    sp.dma_start(out[(NT - 1) * P:N, :], acc[0:NLAST, NT - 1, :]).then_inc(stored.h, 16)
                    sp.wait_ge(stored.h, stored.base + 16 * NT)

                @block.gpsimd
                def _(g):
                    g.iota(node_i[:], [[P, NT]], base=0, channel_multiplier=1).then_inc(numbered.h, 1)

                @block.vector
                def _(v):
                    v.sem_inc(part_set.h, 2)
                    v.sem_inc(out_set.h, 1)
                    norm.stats_of(v, acc)

                    def stage_rows(d, k):
                        v.wait_ge(turned.h, turned.base + d + 1)
                        norm.rows(v, acc, stage[:, k, :], d, rows_ready)
                        v.wait_ge(rows_ready.h, d + 1)
                        v.tensor_tensor(rows_of(acc, d), rows_of(acc, d), stage[:, k, :], ALU.add).then_inc(scaled.h, 1)

                    for d, k in node_tiles(v):
                        stage_rows(d, k)
                    v.wait_ge(numbered.h, 1)
                    v.tensor_copy(junk[:], node_i[:]).then_inc(v_step.h, 1)
                    v.wait_ge(v_step.h, v_step.next())
                    v.tensor_scalar(valid[:], junk[:], float(N), None, ALU.is_lt).then_inc(v_step.h, 1)
                    v.wait_ge(v_step.h, v_step.next())
                    v.wait_ge(routed.h, 1)
                    v.tensor_scalar(weight[:], ps[2][:, 0:NT], br[:], 0.0, ALU.add, ALU.add).then_inc(v_step.h, 1)
                    v.wait_ge(v_step.h, v_step.next())
                    bits = weight[:].bitcast(I32)
                    v.tensor_scalar(sign[:], bits, 31, None, ALU.arith_shift_right).then_inc(v_step.h, 1)
                    v.wait_ge(v_step.h, v_step.next())
                    v.tensor_scalar(sign[:], sign[:], -(1 << 31), None, ALU.bitwise_or).then_inc(v_step.h, 1)
                    v.wait_ge(v_step.h, v_step.next())
                    v.tensor_tensor(key[:], bits, sign[:], ALU.bitwise_xor).then_inc(v_step.h, 1)
                    v.wait_ge(v_step.h, v_step.next())
                    v.tensor_scalar(half_i[:, 0, :], key[:], 16, 0xFFFF, ALU.arith_shift_right, ALU.bitwise_and).then_inc(v_step.h, 1)
                    v.wait_ge(v_step.h, v_step.next())
                    v.tensor_scalar(half_i[:, 1, :], key[:], 0xFFFF, None, ALU.bitwise_and).then_inc(v_step.h, 1)
                    v.wait_ge(v_step.h, v_step.next())
                    v.tensor_copy(half[:], half_i[:]).then_inc(v_step.h, 1)
                    v.wait_ge(v_step.h, v_step.next())

                    def masked(x, mask):
                        v.scalar_tensor_tensor(x, x, 1.0, mask, ALU.add, ALU.mult).then_inc(v_step.h, 1)
                        v.wait_ge(v_step.h, v_step.next())
                        v.tensor_scalar(x, x, -1.0, None, ALU.add).then_inc(v_step.h, 1)
                        v.wait_ge(v_step.h, v_step.next())

                    calls = [0]

                    def total(x, op, bound):
                        v.tensor_scalar(junk[:], x, bound, 0.0, op, ALU.add, accum_out=count[:]).then_inc(v_step.h, 1)
                        v.wait_ge(v_step.h, v_step.next())
                        v.nop().then_inc(counted.h, 1)
                        calls[0] += 1
                        v.wait_ge(summed.h, calls[0])
                        return ps[3][:, 0:1]

                    def kth(x, goal):
                        v.memset(cut[:], 0.0).then_inc(v_step.h, 1)
                        v.wait_ge(v_step.h, v_step.next())
                        for bit in range(15, -1, -1):
                            v.tensor_scalar(trial[:], cut[:], float(1 << bit), None, ALU.add).then_inc(v_step.h, 1)
                            v.wait_ge(v_step.h, v_step.next())
                            n = total(x, ALU.is_ge, trial[:])
                            v.tensor_tensor(reach[:], n, goal, ALU.is_ge).then_inc(v_step.h, 1)
                            v.wait_ge(v_step.h, v_step.next())
                            v.scalar_tensor_tensor(cut[:], reach[:], float(1 << bit), cut[:], ALU.mult, ALU.add).then_inc(v_step.h, 1)
                            v.wait_ge(v_step.h, v_step.next())

                    masked(half[:, 0, :], valid[:])
                    v.memset(quota[:], float(TAKE)).then_inc(v_step.h, 1)
                    v.wait_ge(v_step.h, v_step.next())
                    kth(half[:, 0, :], quota[:, 0:1])
                    n = total(half[:, 0, :], ALU.is_gt, cut[:])
                    v.tensor_tensor(quota[:, 1:2], quota[:, 0:1], n, ALU.subtract).then_inc(v_step.h, 1)
                    v.wait_ge(v_step.h, v_step.next())
                    v.tensor_scalar(above[:], half[:, 0, :], cut[:], None, ALU.is_gt).then_inc(v_step.h, 1)
                    v.wait_ge(v_step.h, v_step.next())
                    v.tensor_scalar(ties[:], half[:, 0, :], cut[:], None, ALU.is_equal).then_inc(v_step.h, 1)
                    v.wait_ge(v_step.h, v_step.next())
                    masked(half[:, 1, :], ties[:])
                    kth(half[:, 1, :], quota[:, 1:2])
                    n = total(half[:, 1, :], ALU.is_gt, cut[:])
                    v.tensor_tensor(quota[:, 1:2], quota[:, 1:2], n, ALU.subtract).then_inc(v_step.h, 1)
                    v.wait_ge(v_step.h, v_step.next())
                    v.tensor_scalar(junk[:], half[:, 1, :], cut[:], None, ALU.is_gt).then_inc(v_step.h, 1)
                    v.wait_ge(v_step.h, v_step.next())
                    v.tensor_tensor(above[:], above[:], junk[:], ALU.add).then_inc(v_step.h, 1)
                    v.wait_ge(v_step.h, v_step.next())
                    v.tensor_scalar(ties[:], half[:, 1, :], cut[:], None, ALU.is_equal).then_inc(v_step.h, 1)
                    v.wait_ge(v_step.h, v_step.next())
                    v.nop().then_inc(counted.h, 1)
                    calls[0] += 1
                    v.wait_ge(summed.h, calls[0])
                    v.tensor_copy(taken[:], ps[3][:, 64:64 + NT]).then_inc(v_step.h, 1)
                    v.wait_ge(v_step.h, v_step.next())
                    v.tensor_tensor_scan(runs[:], ones[:, 0:NT], taken[:], 0.0, ALU.mult, ALU.add).then_inc(v_step.h, 1)
                    v.wait_ge(v_step.h, v_step.next())
                    v.tensor_tensor(runs[:], runs[:], taken[:], ALU.subtract).then_inc(v_step.h, 1)
                    v.wait_ge(v_step.h, v_step.next())
                    v.tensor_tensor(runs[:], runs[:], ps[3][:, 0:NT], ALU.add).then_inc(v_step.h, 1)
                    v.wait_ge(v_step.h, v_step.next())
                    v.tensor_scalar(runs[:], runs[:], quota[:, 1:2], None, ALU.is_lt).then_inc(v_step.h, 1)
                    v.wait_ge(v_step.h, v_step.next())
                    v.tensor_tensor(ties[:], ties[:], runs[:], ALU.mult).then_inc(v_step.h, 1)
                    v.wait_ge(v_step.h, v_step.next())
                    v.tensor_tensor(taken[:], above[:], ties[:], ALU.add).then_inc(v_step.h, 1)
                    v.wait_ge(v_step.h, v_step.next())
                    v.tensor_tensor(weight[:], weight[:], taken[:], ALU.mult).then_inc(v_step.h, 1)
                    v.wait_ge(v_step.h, v_step.next())
                    v.wait_ge(scaled.h, NT)
                    with v.Fori(0, NT // ONE) as blk:
                        for j in range(ONE):
                            d = blk * ONE + j
                            k = j % 2
                            v.wait_ge(down_done.h, d + 1)
                            if j == 0:
                                v.wait_ge(out_set.h, d + 1)
                            v.tensor_tensor(part[:, k, :], ps[6 + k][:, 0:F], b2[:], ALU.add).then_inc(part_set.h, 1)
                            v.wait_ge(part_set.h, d + 1 + 2)
                            v.scalar_tensor_tensor(rows_of(acc, d), part[:, k, :], weight[:, bass.ds(d, 1)], rows_of(acc, d), ALU.mult, ALU.add).then_inc(out_set.h, 1)

                @block.scalar
                def _(a):
                    norm.root.scalar(a)
                    for d, k in node_tiles(a):
                        a.wait_ge(turned.h, turned.base + d + 1 + 2)
                        a.activation(zt[:, :, bass.ds(d * P, P)], ps[k][:, 0:F].rearrange("p (c n) -> p c n", c=FC), ACT.Copy).then_inc(turned_out.h, 1)
                    a.wait_ge(weights_in.h, 16 * (5 + FC))
                    with a.Fori(0, NT // ONE) as blk:
                        a.wait_ge(freed.h, blk + 1)
                        for c in range(HC):
                            for j in range(2):
                                a.wait_ge(up_done.h, blk * 2 * HC + 2 * c + j + 1)
                                a.activation(hid[:, c, j * HALF:(j + 1) * HALF], ps[4 + j][:, 0:HALF], ACT.Gelu_apprx_tanh, bias=b1[:, c:c + 1]).then_inc(up_act.h, 1)

                @block.tensor
                def _(pe):
                    pe.sem_inc(freed.h, 1)
                    pe.sem_inc(up_act.h, 2)
                    for d, k in node_tiles(pe):
                        turn_staged(pe, stage, d, k, rows_ready)
                    pe.wait_ge(turned_out.h, turned_out.base + NT + 2)
                    pe.wait_ge(weights_in.h, 16 * (5 + FC))
                    for d in range(NT):
                        for c in range(FC):
                            mm = pe.matmul(ps[2][:, d:d + 1], zt[:, c, d * P:(d + 1) * P], wr[:, c, :], start=(c == 0), stop=(c == FC - 1))
                    mm.then_inc(routed.h, 1)
                    for n in range(2 * 17):
                        pe.wait_ge(counted.h, n + 1)
                        pe.matmul(ps[3][:, 0:1], ones[:], count[:], start=True, stop=True).then_inc(summed.h, 1)
                    pe.wait_ge(counted.h, 2 * 17 + 1)
                    pe.matmul(ps[3][:, 0:NT], excl[:], ties[:], start=True, stop=True)
                    pe.matmul(ps[3][:, 64:64 + NT], ones[:], ties[:], start=True, stop=True).then_inc(summed.h, 1)
                    with pe.Fori(0, NT // ONE) as blk:
                        for c in range(HC):
                            for j in range(2):
                                pe.wait_ge(up_act.h, blk * 2 * HC + 2 * c + j + 1)
                                for f in range(FC):
                                    mm = pe.matmul(ps[4 + j][:, 0:HALF], w1[:, f, c * P:(c + 1) * P], zt[:, f, bass.ds(blk * BW + j * HALF, HALF)], start=(f == 0), stop=(f == FC - 1))
                                mm.then_inc(up_done.h, 1)
                        pe.wait_ge(up_act.h, (blk + 1) * 2 * HC + 2)
                        for j in range(ONE):
                            pe.wait_ge(part_set.h, blk * ONE + j + (2 if j == 0 else 1))
                            for c in range(HC):
                                mm = pe.matmul(ps[6 + j % 2][:, 0:F], hid[:, c, j * P:(j + 1) * P], w2[:, c, :], start=(c == 0), stop=(c == HC - 1))
                            mm.then_inc(down_done.h, 1)
                        pe.drain().then_inc(freed.h, 1)
            turned.base += NT
            turned_out.base += NT
            stored.base += 16 * NT

    def turn_staged(pe, stage, d, k, rows_ready):
        pe.wait_ge(rows_ready.h, d + 1)
        pe.wait_ge(turned_out.h, turned_out.base + d + 1)
        for c in range(FC):
            mm = pe.transpose(ps[k][:, c * P:(c + 1) * P], stage[:, k, c * P:(c + 1) * P], ident[:])
        mm.then_inc(turned.h, 1)

    feed_forward()
    bigs.close()


_OUT = ((N, F), "float32")


def kernel(**inputs):
    import numpy as _np
    import concourse.bacc as _bacc
    from concourse import mybir as _mybir
    from concourse.bass_utils import run_bass_kernel_spmd as _run

    nc = _bacc.Bacc("TRN2", target_bir_lowering=False, num_devices=1)
    arrays, tensors = {}, {}
    for name, value in inputs.items():
        a = _np.ascontiguousarray(value)
        arrays[f"in_{name}_dram"] = a
        tensors[name] = nc.dram_tensor(f"in_{name}_dram", a.shape, _mybir.dt.from_np(a.dtype), kind="ExternalInput").ap()
    shape, dtype = _OUT
    out = nc.dram_tensor("out_0_dram", shape, _mybir.dt.from_np(_np.dtype(dtype)), kind="ExternalOutput").ap()
    build(nc, tensors, out)
    r = _run(nc, [arrays], core_ids=[0])
    return r.results[0]["out_0_dram"]
```

```python
from contextlib import ExitStack

import concourse.bass as bass
from concourse import mybir
import numpy as np

F32 = mybir.dt.float32
BF16 = mybir.dt.bfloat16
I32 = mybir.dt.int32
ALU = mybir.AluOpType
ACT = mybir.ActivationFunctionType
AX = mybir.AxisListType

P = 128
N = 6250
E = 100000
F = 256
FC = F // P
NT = -(-N // P)
NPAD = NT * P
NLAST = N - (NT - 1) * P
ET = -(-E // P)
ETB = -(-ET // P)
G = 8
ITERS = -(-(ET + NT - 1) // (2 * G))
NPAIR = ITERS * 2 * G
PCOL = ETB * P
NODST = 1 << 20
BIG = 1.0e30
EPS = 1e-5
HEADS = 8
HD = F // HEADS
EDIM = 64
EXPERTS = 8
HID = 1024
HC = HID // P
SLOPE = 0.2
PART = NT // 4 // 2 * 2
PARTS = [(p * PART, NT if p == 3 else (p + 1) * PART) for p in range(4)]


class Sem:

    def __init__(self, handle):
        self.h, self.base = handle, 0

    def next(self):
        self.base += 1
        return self.base


def node_tiles(eng, lo=0, hi=NT):
    with eng.Fori(lo // 2, hi // 2) as i:
        yield 2 * i, 0
        yield 2 * i + 1, 1
    for d in range(hi // 2 * 2, hi):
        yield d, d % 2


def two_ahead(eng, early, late, before):
    for part, (lo, hi) in enumerate(PARTS):
        before(part)
        first, end = max(lo // 2 - 1, 0), hi // 2 - 1
        if part == 0:
            early(0, 0)
            early(1, 1)
            for k in range(2):
                early(2 + k, k)
                late(k, k)
            first = 1
        with eng.Fori(first, end) as i:
            for k in range(2):
                early(2 * i + 2 + k, k)
                late(2 * i + k, k)
    for d in range(NT // 2 * 2 - 2, NT):
        if d + 2 < NT:
            early(d + 2, d % 2)
        late(d, d % 2)


def node_tiles_apart(eng):
    yield 0, 0
    yield 1, 1
    with eng.Fori(1, NT // 2) as i:
        yield 2 * i, 0
        yield 2 * i + 1, 1
    for d in range(NT // 2 * 2, NT):
        yield d, d % 2


def wait_earlier(eng, sem, d, k, each):
    if not isinstance(d, int):
        eng.wait_ge(sem.h, sem.base + (d - k) * (each // 2))
    elif d >= 2:
        eng.wait_ge(sem.h, sem.base + d // 2 * each)


def build(nc, t, out):
    with ExitStack() as top:
        _build(nc, t, out, top)


def _build(nc, t, out, top):
    uses = {}

    def sb(name, shape, dt=F32, ctx=top):
        uses[name] = uses.get(name, 0) + 1
        return ctx.enter_context(nc.sbuf_tensor(f"{name}_{uses[name]}", shape, dt))

    def sem(name):
        return Sem(top.enter_context(nc.semaphore(name)))

    class PhaseSems:

        def __enter__(self):
            self.used = []
            return self

        def __call__(self, name):
            self.used.append(nc.alloc_semaphore(name=name))
            return Sem(self.used[-1])

        def __exit__(self, *failed):
            if not any(failed):
                nc.clear_and_free_semaphores(self.used)
                nc.all_engine_barrier()

    def dram(name, shape, dt=F32):
        return nc.dram_tensor(name, shape, dt, kind="Internal").ap()

    ps = [top.enter_context(nc.psum_tensor(f"ps{i}", [P, 512], F32)) for i in range(8)]

    ident = sb("ident", [P, P])
    iota_f = sb("iota_f", [P, P])
    ones = sb("ones", [P, P])
    excl = sb("excl", [P, P])
    psrc = sb("psrc", [P, PCOL], I32)
    pdl = sb("pdl", [P, PCOL])
    plast = sb("plast", [P, PCOL])
    run_start = sb("run_start", [P, ETB, P], BF16)
    prow = sb("prow", [2, PCOL], I32)
    dinv = sb("dinv", [P, NT])
    change = sb("change", [P, NPAIR // G, G + 1])
    idx = sb("idx", [P, 4, G], I32)
    carrier = sb("carrier", [P, 1], I32)

    MT = -(-(2 * N) // P) + EXPERTS
    MT += MT % 2
    CAP = MT * P
    slot_rows = dram("slot_rows", [CAP + 2 * P, F])
    slot_out = dram("slot_out", [CAP + 2 * P, F])
    resid = dram("resid", [NPAD, F])
    slots = sb("slots", [P, 2, NT], I32)
    gate = sb("gate", [P, 2, NT], F32)
    tile_expert = sb("tile_expert", [P, MT], F32)
    tile_expert_i = sb("tile_expert_i", [1, MT], I32)

    edge_table = dram("edge_table", [PCOL, 2 * P + 1])
    node_table = dram("node_table", [NPAD, F])
    HROW = HD + 1
    attn_table = dram("attn_table", [NPAD, HEADS * HROW])
    ee_table = dram("ee_table", [P, NPAIR * HEADS])

    v_step = sem("v_step")
    row_sem = [sem(f"row_landed{s}") for s in range(2 * G)]
    idx_ready = sem("idx_ready")
    onehot_ready, aggregated, added = sem("onehot_ready"), sem("aggregated"), sem("added")
    loaded, stored, x_loaded = sem("loaded"), sem("stored"), sem("x_loaded")
    turned, turned_out = sem("turned"), sem("turned_out")
    projected, projected_out = sem("projected"), sem("projected_out")
    credit = {aggregated: 2 * G, added: G, turned: 2, turned_out: 2, projected: 2, projected_out: 2}

    root_ready, root_done = sem("root_ready"), sem("root_done")
    roots = [0]

    class Rsqrt:

        def __init__(self, var, res, tmp):
            self.var, self.res, self.tmp, self.n = var, res, tmp, roots[0] + 1
            roots[0] += 1

        def scalar(self, a):
            a.wait_ge(root_ready.h, self.n)
            a.activation(self.res, self.var, ACT.Sqrt).then_inc(root_done.h, 1)

        def vector(self, v):
            var, res, tmp = self.var, self.res, self.tmp
            v.nop().then_inc(root_ready.h, 1)
            v.wait_ge(root_done.h, self.n)
            v.reciprocal(tmp, res).then_inc(v_step.h, 1)
            v.wait_ge(v_step.h, v_step.next())
            v.tensor_tensor(res, tmp, tmp, ALU.mult).then_inc(v_step.h, 1)
            v.wait_ge(v_step.h, v_step.next())
            v.tensor_tensor(res, res, var, ALU.mult).then_inc(v_step.h, 1)
            v.wait_ge(v_step.h, v_step.next())
            v.tensor_scalar(res, res, -0.5, 1.5, ALU.mult, ALU.add).then_inc(v_step.h, 1)
            v.wait_ge(v_step.h, v_step.next())
            v.tensor_tensor(res, res, tmp, ALU.mult).then_inc(v_step.h, 1)
            v.wait_ge(v_step.h, v_step.next())

    def rows_of(big, d):
        return big[:, bass.ds(d, 1), :].rearrange("p a f -> p (a f)")

    def in_registers(eng, row, most):
        return nc.values_load_multi_w_load_instructions(row, [eng.engine], min_val=0, max_val=most,
                                                        skip_runtime_bounds_check_because="held to that range on the chip")[1]

    def node_tiles_of(eng, q):
        return in_registers(eng, prow[0:1, bass.ds(q * G, G)], NT - 1)

    shares = ExitStack()
    shared = sb("shared", [P, max(EXPERTS * FC * HID, NT * F)], F32, shares)
    acc = shared[:, 0:NT * F].rearrange("p (d f) -> p d f", f=F)
    bigs = ExitStack()
    feat = sb("feat", [P, NT, F], F32, bigs)
    feat_t = feat[:].rearrange("p d f -> p (d f)").rearrange("p (c n) -> p c n", c=FC)
    vecs = sb("vecs", [P, 3, 3, FC], F32, bigs)
    wts = sb("wts", [P, FC, F], F32, bigs)
    stage = sb("stage", [P, 2, F], F32, bigs)
    lhs = sb("lhs", [P, 2, FC, P], F32, bigs)

    def load_rows(sp, big, src, done):
        sp.dma_start(big[:, 0:NT - 1, :], src[0:(NT - 1) * P, :].rearrange("(d p) f -> p d f", p=P)).then_inc(done.h, 16)
        sp.dma_start(big[0:NLAST, NT - 1, :], src[(NT - 1) * P:N, :]).then_inc(done.h, 16)

    def edge_tables():
        with ExitStack() as ctx, PhaseSems() as sem:
            iota_i = sb("iota_i", [P, P], I32, ctx)
            col_i = sb("col_i", [P, 1], I32, ctx)
            pv_i = sb("pv_i", [P, ETB], I32, ctx)
            col_f = sb("col_f", [P, 1], F32, ctx)
            pv = sb("pv", [P, ETB], F32, ctx)
            incl = sb("incl", [P, P], F32, ctx)
            edges_i = sb("edges_i", [P, ETB, 2, P], I32, ctx)
            edges_f = sb("edges_f", [P, ETB, 2 * P + 1], F32, ctx)
            tmp = sb("tmp", [P, ETB, P], F32, ctx)
            mm = sb("mm", [P, 2, ETB], F32, ctx)
            mm_i = sb("mm_i", [P, 2, ETB], I32, ctx)
            small = sb("small", [P, 8, ETB], F32, ctx)
            cumrow = sb("cumrow", [P, PCOL], F32, ctx)
            junk = sb("junk", [P, PCOL], F32, ctx)
            tile_of = sb("tile_of", [P, ETB], F32, ctx)
            tile_i = sb("tile_i", [P, ETB], I32, ctx)
            pair_edges = sb("pair_edges", [P, ETB, 2 * P + 1], F32, ctx)
            pair_dst = sb("pair_dst", [P, ETB, P], F32, ctx)
            lastf = sb("lastf", [P, ETB, P], F32, ctx)
            drow = sb("drow", [P, ETB, 2], F32, ctx)
            consts, padded, edges_in = sem("consts"), sem("padded"), sem("edges_in")
            counted, scanned, spread, spread_done = sem("counted"), sem("scanned"), sem("spread"), sem("spread_done")
            table_ready, tiles_found, pairs_in = sem("table_ready"), sem("tiles_found"), sem("pairs_in")
            pairs_ready, pairs_turned = sem("pairs_ready"), sem("pairs_turned")
            full = (ETB - 1) * P * P
            lastb = ETB - 1
            rows = (E - full) // P
            rest = E - full - rows * P

            block = nc.Block()
            with block as block:
                @block.gpsimd
                def _(g):
                    g.iota(iota_i[:], [[1, P]], base=0, channel_multiplier=0).then_inc(consts.h, 1)
                    g.iota(col_i[:], [[0, 1]], base=0, channel_multiplier=1).then_inc(consts.h, 1)
                    g.iota(pv_i[:], [[P, ETB]], base=0, channel_multiplier=1).then_inc(consts.h, 1)
                    g.memset(edges_i[:, lastb, 0, :], 0).then_inc(padded.h, 1)
                    g.memset(edges_i[:, lastb, 1, :], NODST).then_inc(padded.h, 1)
                    g.memset(ones[:], 1.0).then_inc(consts.h, 1)
                    g.memset(feat[:, NT - 1, :], 0.0).then_inc(padded.h, 1)
                    g.wait_ge(tiles_found.h, 1)
                    g.wait_ge(stored.h, stored.base + 16)
                    for b in range(ETB):
                        g.indirect_dma_start(pair_edges[:, b, :], None, edge_table,
                                             bass.IndirectOffsetOnAxis(ap=tile_i[:, b:b + 1], axis=0)).then_inc(pairs_in.h, 16)

                @block.sync
                def _(sp):
                    sp.wait_ge(padded.h, 2)
                    for k, a in enumerate((t["src"], t["dst"])):
                        sp.dma_start(edges_i[:, 0:lastb, k, :], a[0:full].rearrange("(b p l) -> p b l", p=P, l=P)).then_inc(edges_in.h, 16)
                        sp.dma_start(edges_i[0:rows, lastb, k, :], a[full:full + rows * P].rearrange("(p l) -> p l", l=P)).then_inc(edges_in.h, 16)
                        sp.dma_start(edges_i[rows:rows + 1, lastb, k, P - rest:P], a[E - rest:E].rearrange("(p l) -> p l", p=1)).then_inc(edges_in.h, 16)
                    sp.wait_ge(padded.h, 3)
                    load_rows(sp, feat, t["x"], x_loaded)
                    sp.wait_ge(table_ready.h, 1)
                    sp.dma_start(edge_table.rearrange("(b p) c -> p b c", p=P), edges_f[:]).then_inc(stored.h, 16)

                @block.vector
                def _(v):
                    for s, n in credit.items():
                        v.sem_inc(s.h, n)
                    v.wait_ge(consts.h, 4)
                    v.tensor_copy(iota_f[:], iota_i[:]).then_inc(v_step.h, 1)
                    v.wait_ge(v_step.h, v_step.next())
                    v.tensor_copy(col_f[:], col_i[:]).then_inc(v_step.h, 1)
                    v.wait_ge(v_step.h, v_step.next())
                    v.tensor_copy(pv[:], pv_i[:]).then_inc(v_step.h, 1)
                    v.wait_ge(v_step.h, v_step.next())
                    v.tensor_scalar(ident[:], iota_f[:], col_f[:], None, ALU.is_equal).then_inc(v_step.h, 1)
                    v.wait_ge(v_step.h, v_step.next())
                    v.tensor_scalar(excl[:], iota_f[:], col_f[:], None, ALU.is_gt).then_inc(v_step.h, 1)
                    v.wait_ge(v_step.h, v_step.next())
                    v.tensor_scalar(incl[:], iota_f[:], col_f[:], None, ALU.is_ge).then_inc(v_step.h, 1)
                    v.wait_ge(v_step.h, v_step.next())
                    v.wait_ge(edges_in.h, 6 * 16)
                    v.tensor_copy(edges_f[:, :, 0:2 * P], edges_i[:].rearrange("p b k l -> p b (k l)")).then_inc(v_step.h, 1)
                    v.wait_ge(v_step.h, v_step.next())
                    dst = edges_f[:, :, P:2 * P]
                    v.scalar_tensor_tensor(tmp[:], dst, float(NODST // 2), dst, ALU.is_lt, ALU.mult).then_inc(v_step.h, 1)
                    v.wait_ge(v_step.h, v_step.next())
                    v.tensor_reduce(mm[:, 0, :], dst, AX.X, ALU.min).then_inc(v_step.h, 1)
                    v.wait_ge(v_step.h, v_step.next())
                    v.tensor_reduce(mm[:, 1, :], tmp[:], AX.X, ALU.max).then_inc(v_step.h, 1)
                    v.wait_ge(v_step.h, v_step.next())
                    valid, cnt, tot, cum, off = (small[:, k, :] for k in range(5))
                    v.tensor_scalar(valid, mm[:, 0, :], float(NODST // 2), None, ALU.is_lt).then_inc(v_step.h, 1)
                    v.wait_ge(v_step.h, v_step.next())
                    v.tensor_copy(mm_i[:], mm[:]).then_inc(v_step.h, 1)
                    v.wait_ge(v_step.h, v_step.next())
                    v.tensor_scalar(mm_i[:], mm_i[:], 7, None, ALU.arith_shift_right).then_inc(v_step.h, 1)
                    v.wait_ge(v_step.h, v_step.next())
                    v.tensor_copy(mm[:], mm_i[:]).then_inc(v_step.h, 1)
                    v.wait_ge(v_step.h, v_step.next())
                    v.tensor_tensor(cnt, mm[:, 1, :], mm[:, 0, :], ALU.subtract).then_inc(v_step.h, 1)
                    v.wait_ge(v_step.h, v_step.next())
                    v.scalar_tensor_tensor(cnt, cnt, 1.0, valid, ALU.add, ALU.mult).then_inc(v_step.h, 1)
                    v.wait_ge(v_step.h, v_step.next())
                    v.nop().then_inc(counted.h, 1)
                    v.wait_ge(scanned.h, 1)
                    v.tensor_copy(tot, ps[0][:, 16:16 + ETB]).then_inc(v_step.h, 1)
                    v.wait_ge(v_step.h, v_step.next())
                    v.tensor_tensor_scan(cum, ones[:, 0:ETB], tot, 0.0, ALU.mult, ALU.add).then_inc(v_step.h, 1)
                    v.wait_ge(v_step.h, v_step.next())
                    v.tensor_tensor(cum, cum, ps[0][:, 0:ETB], ALU.add).then_inc(v_step.h, 1)
                    v.wait_ge(v_step.h, v_step.next())
                    v.tensor_tensor(cum, cum, tot, ALU.subtract).then_inc(v_step.h, 1)
                    v.wait_ge(v_step.h, v_step.next())
                    v.tensor_tensor(off, cum, cnt, ALU.subtract).then_inc(v_step.h, 1)
                    v.wait_ge(v_step.h, v_step.next())
                    v.tensor_tensor(off, mm[:, 0, :], off, ALU.subtract).then_inc(v_step.h, 1)
                    v.wait_ge(v_step.h, v_step.next())
                    v.tensor_tensor(edges_f[:, :, 2 * P], off, valid, ALU.mult).then_inc(v_step.h, 1)
                    v.wait_ge(v_step.h, v_step.next())
                    v.nop().then_inc(table_ready.h, 1)
                    v.tensor_tensor(tmp[:], ident[:].rearrange("p (b l) -> p b l", b=1).to_broadcast([P, ETB, P]),
                                    cum.rearrange("p (b l) -> p b l", l=1).to_broadcast([P, ETB, P]), ALU.mult).then_inc(v_step.h, 1)
                    v.wait_ge(v_step.h, v_step.next())
                    v.nop().then_inc(spread.h, 1)
                    v.wait_ge(spread_done.h, 1)
                    v.tensor_copy(cumrow[:, 0:512], ps[1][:]).then_inc(v_step.h, 1)
                    v.wait_ge(v_step.h, v_step.next())
                    v.tensor_copy(cumrow[:, 512:PCOL], ps[2][:, 0:PCOL - 512]).then_inc(v_step.h, 1)
                    v.wait_ge(v_step.h, v_step.next())
                    for b in range(ETB):
                        v.tensor_scalar(junk[:], cumrow[:], pv[:, b:b + 1], 0.0, ALU.is_le, ALU.add, accum_out=tile_of[:, b:b + 1]).then_inc(v_step.h, 1)
                        v.wait_ge(v_step.h, v_step.next())
                    v.tensor_scalar(tile_of[:], tile_of[:], float(PCOL - 1), None, ALU.min).then_inc(v_step.h, 1)
                    v.wait_ge(v_step.h, v_step.next())
                    v.tensor_copy(tile_i[:], tile_of[:]).then_inc(v_step.h, 1)
                    v.wait_ge(v_step.h, v_step.next())
                    v.nop().then_inc(tiles_found.h, 1)
                    v.wait_ge(pairs_in.h, 16 * ETB)
                    dp = drow[:, :, 0]
                    v.tensor_tensor(dp, pv[:], pair_edges[:, :, 2 * P], ALU.add).then_inc(v_step.h, 1)
                    v.wait_ge(v_step.h, v_step.next())
                    v.tensor_scalar(dp, dp, float(NT - 1), 0.0, ALU.min, ALU.max).then_inc(v_step.h, 1)
                    v.wait_ge(v_step.h, v_step.next())
                    v.tensor_scalar(small[:, 5, :], dp, float(P), None, ALU.mult).then_inc(v_step.h, 1)
                    v.wait_ge(v_step.h, v_step.next())
                    v.tensor_scalar(drow[:, :, 1], tile_of[:], float(P), float(E - P), ALU.mult, ALU.min).then_inc(v_step.h, 1)
                    v.wait_ge(v_step.h, v_step.next())
                    v.tensor_tensor(pair_dst[:], pair_edges[:, :, P:2 * P],
                                    small[:, 5, :].rearrange("p (b l) -> p b l", l=1).to_broadcast([P, ETB, P]), ALU.subtract).then_inc(v_step.h, 1)
                    v.wait_ge(v_step.h, v_step.next())
                    v.memset(lastf[:], 1.0).then_inc(v_step.h, 1)
                    v.wait_ge(v_step.h, v_step.next())
                    v.memset(run_start[:], -BIG).then_inc(v_step.h, 1)
                    v.wait_ge(v_step.h, v_step.next())
                    v.tensor_tensor(lastf[:, :, 0:P - 1], pair_dst[:, :, 0:P - 1], pair_dst[:, :, 1:P], ALU.not_equal).then_inc(v_step.h, 1)
                    v.wait_ge(v_step.h, v_step.next())
                    v.tensor_scalar(run_start[:, :, 1:P], lastf[:, :, 0:P - 1], -BIG, None, ALU.mult).then_inc(v_step.h, 1)
                    v.wait_ge(v_step.h, v_step.next())
                    v.nop().then_inc(pairs_ready.h, 1)
                    for b in range(ETB):
                        v.wait_ge(pairs_turned.h, b + 1)
                        c = slice(b * P, (b + 1) * P)
                        v.tensor_copy(psrc[:, c], ps[b][:, 0:P]).then_inc(v_step.h, 1)
                        v.wait_ge(v_step.h, v_step.next())
                        v.tensor_copy(pdl[:, c], ps[b][:, P:2 * P]).then_inc(v_step.h, 1)
                        v.wait_ge(v_step.h, v_step.next())
                        v.tensor_copy(plast[:, c], ps[b][:, 2 * P:3 * P]).then_inc(v_step.h, 1)
                        v.wait_ge(v_step.h, v_step.next())
                        v.tensor_copy(prow[:, c], ps[b][0:2, 3 * P:4 * P]).then_inc(v_step.h, 1)
                        v.wait_ge(v_step.h, v_step.next())

                @block.tensor
                def _(pe):
                    pe.wait_ge(counted.h, 1)
                    pe.matmul(ps[0][:, 0:ETB], incl[:], small[:, 1, :], start=True, stop=True)
                    pe.matmul(ps[0][:, 16:16 + ETB], ones[:], small[:, 1, :], start=True, stop=True).then_inc(scanned.h, 1)
                    pe.wait_ge(spread.h, 1)
                    diag = tmp[:].rearrange("p b l -> p (b l)")
                    pe.matmul(ps[1][:], ones[:], diag[:, 0:512], start=True, stop=True)
                    pe.matmul(ps[2][:, 0:PCOL - 512], ones[:], diag[:, 512:PCOL], start=True, stop=True).then_inc(spread_done.h, 1)
                    pe.wait_ge(pairs_ready.h, 1)
                    for b in range(ETB):
                        pe.transpose(ps[b][:, 0:P], pair_edges[:, b, 0:P], ident[:])
                        pe.transpose(ps[b][:, P:2 * P], pair_dst[:, b, :], ident[:])
                        pe.transpose(ps[b][:, 2 * P:3 * P], lastf[:, b, :], ident[:])
                        pe.matmul(ps[b][0:2, 3 * P:4 * P], drow[:, b, :], ident[:], start=True, stop=True).then_inc(pairs_turned.h, 1)
            stored.base += 16

    edge_tables()

    def degrees():
        with ExitStack() as ctx, PhaseSems() as sem:
            hot = sb("hot", [P, 2, 2 * G, P], BF16, ctx)
            FEW = 4
            away = sb("away", [P, 2, FEW, P], F32, ctx)
            few_step, few_ready = sem("few_step"), sem("few_ready")
            ones_b = sb("ones_b", [P, 1], BF16, ctx)
            cnt = sb("cnt", [P, PCOL], F32, ctx)
            cnt_t = sb("cnt_t", [P, ETB, P], F32, ctx)
            hit = sb("hit", [P, ETB, NT], F32, ctx)
            drow_f = sb("drow_f", [1, PCOL], F32, ctx)
            dcol = sb("dcol", [P, ETB], F32, ctx)
            tile_row = sb("tile_row", [P, PCOL], F32, ctx)
            differs = sb("differs", [P, PCOL], F32, ctx)
            deg = sb("deg", [P, NT], F32, ctx)
            tmp = sb("deg_tmp", [P, NT], F32, ctx)
            hot_ready, hot_used, count_out = sem("hot_ready"), sem("hot_used"), sem("count_out")
            row_ready, col_ready = sem("row_ready"), sem("col_ready")
            cnt_ready, cnt_turned, cnt_back, deg_ready = sem("cnt_ready"), sem("cnt_turned"), sem("cnt_back"), sem("deg_ready")
            root = Rsqrt(deg[:], dinv[:], tmp[:])
            with nc.Block() as block:
                @block.vector
                def _(v):
                    v.memset(ones_b[:], 1.0).then_inc(v_step.h, 1)
                    v.wait_ge(v_step.h, v_step.next())
                    v.memset(cnt[:], 0.0).then_inc(v_step.h, 1)
                    v.wait_ge(v_step.h, v_step.next())
                    v.tensor_copy(drow_f[:], prow[0:1, :]).then_inc(v_step.h, 1)
                    v.wait_ge(v_step.h, v_step.next())
                    v.nop().then_inc(row_ready.h, 1)

                    def mark(i, k):
                        many = 2 * G - FEW
                        v.tensor_tensor(hot[:, k, 0:many], iota_f[:].rearrange("p (j n) -> p j n", j=1).to_broadcast([P, many, P]),
                                        pdl[:, bass.ds(i * 2 * G, many)].rearrange("p (j n) -> p j n", n=1).to_broadcast([P, many, P]),
                                        ALU.is_equal).then_inc(hot_ready.h, 1)

                    def keep(i, k):
                        v.wait_ge(hot_used.h, i + 1)
                        v.tensor_copy(cnt[:, bass.ds(i * 2 * G, 2 * G)], ps[k][:, 0:2 * G]).then_inc(count_out.h, 1)

                    mark(0, 0)
                    with v.Fori(0, ITERS // 2) as j:
                        mark(2 * j + 1, 1)
                        keep(2 * j, 0)
                        mark(2 * j + 2, 0)
                        keep(2 * j + 1, 1)
                    v.wait_ge(count_out.h, ITERS)
                    v.nop().then_inc(cnt_ready.h, 1)
                    v.wait_ge(col_ready.h, 1)
                    v.tensor_copy(dcol[:], ps[7][:, 0:ETB]).then_inc(v_step.h, 1)
                    v.wait_ge(v_step.h, v_step.next())
                    v.tensor_copy(tile_row[:, 0:512], ps[5][:]).then_inc(v_step.h, 1)
                    v.wait_ge(v_step.h, v_step.next())
                    v.tensor_copy(tile_row[:, 512:PCOL], ps[6][:, 0:PCOL - 512]).then_inc(v_step.h, 1)
                    v.wait_ge(v_step.h, v_step.next())
                    v.memset(differs[:, 0:1], 1.0).then_inc(v_step.h, 1)
                    v.wait_ge(v_step.h, v_step.next())
                    v.tensor_tensor(differs[:, 1:PCOL], tile_row[:, 1:PCOL], tile_row[:, 0:PCOL - 1], ALU.not_equal).then_inc(v_step.h, 1)
                    v.wait_ge(v_step.h, v_step.next())
                    v.memset(change[:, :, 0:1], -BIG).then_inc(v_step.h, 1)
                    v.wait_ge(v_step.h, v_step.next())
                    v.tensor_scalar(change[:, :, 1:G + 1], differs[:, 0:NPAIR].rearrange("p (n j) -> p n j", j=G), -BIG, None, ALU.mult).then_inc(v_step.h, 1)
                    v.wait_ge(v_step.h, v_step.next())
                    for b in range(ETB):
                        v.tensor_scalar(hit[:, b, :], iota_f[:, 0:NT], dcol[:, b:b + 1], None, ALU.is_equal).then_inc(v_step.h, 1)
                        v.wait_ge(v_step.h, v_step.next())
                    v.wait_ge(cnt_turned.h, 1)
                    v.tensor_copy(cnt_t[:, 0:4, :], ps[2][:].rearrange("p (b l) -> p b l", l=P)).then_inc(v_step.h, 1)
                    v.wait_ge(v_step.h, v_step.next())
                    v.tensor_copy(cnt_t[:, 4:ETB, :], ps[3][:, 0:(ETB - 4) * P].rearrange("p (b l) -> p b l", l=P)).then_inc(v_step.h, 1)
                    v.wait_ge(v_step.h, v_step.next())
                    v.nop().then_inc(cnt_back.h, 1)
                    v.wait_ge(deg_ready.h, 1)
                    v.tensor_scalar(deg[:], ps[4][:, 0:NT], 1.0, None, ALU.add).then_inc(v_step.h, 1)
                    v.wait_ge(v_step.h, v_step.next())
                    root.vector(v)

                @block.scalar
                def _(a):
                    def mark_few(i, k):
                        if not isinstance(i, int) or i >= 2:
                            a.wait_ge(hot_used.h, i - 1)
                        for b in range(FEW):
                            op = a.activation(away[:, k, b, :], iota_f[:], ACT.Abs, bias=pdl[:, bass.ds((i + 1) * 2 * G - FEW + b, 1)], scale=-1.0)
                        op.then_inc(few_step.h, 1)
                        a.wait_ge(few_step.h, i + 1)
                        a.activation(hot[:, k, 2 * G - FEW:2 * G], away[:, k], ACT.Relu, bias=ones[:, 0:1], scale=-1.0).then_inc(few_ready.h, 1)

                    mark_few(0, 0)
                    mark_few(1, 1)
                    with a.Fori(1, ITERS // 2) as j:
                        for k in range(2):
                            mark_few(2 * j + k, k)
                    root.scalar(a)

                @block.tensor
                def _(pe):
                    pe.wait_ge(row_ready.h, 1)
                    pe.matmul(ps[5][:], ones[0:1, :], drow_f[:, 0:512], start=True, stop=True)
                    pe.matmul(ps[6][:, 0:PCOL - 512], ones[0:1, :], drow_f[:, 512:PCOL], start=True, stop=True)
                    for b in range(ETB):
                        mm = pe.matmul(ps[7][:, b:b + 1], drow_f[0:1, b * P:(b + 1) * P], ones[0:1, 0:1], start=True, stop=True)
                    mm.then_inc(col_ready.h, 1)
                    with pe.Fori(0, ITERS // 2) as j:
                        for k in range(2):
                            pe.wait_ge(hot_ready.h, 2 * j + k + 1)
                            pe.wait_ge(few_ready.h, 2 * j + k + 1)
                            for b in range(2 * G):
                                mm = pe.matmul(ps[k][:, b:b + 1], hot[:, k, b, :], ones_b[:], start=True, stop=True)
                            mm.then_inc(hot_used.h, 1)
                    pe.wait_ge(cnt_ready.h, 1)
                    for b in range(ETB):
                        mm = pe.transpose(ps[2 + b // 4][:, b % 4 * P:(b % 4 + 1) * P], cnt[:, b * P:(b + 1) * P], ident[:])
                    mm.then_inc(cnt_turned.h, 1)
                    pe.wait_ge(cnt_back.h, 1)
                    for b in range(ETB):
                        mm = pe.matmul(ps[4][:, 0:NT], cnt_t[:, b, :], hit[:, b, :], start=(b == 0), stop=(b == ETB - 1))
                    mm.then_inc(deg_ready.h, 1)

    degrees()

    class NodeNorm:

        def __init__(self, ctx, name, parts):
            self.stats = sb(name + "_stats", [P, NT, 6], F32, ctx)
            self.mean = sb(name + "_mean", [P, NT], F32, ctx)
            self.var = sb(name + "_var", [P, NT], F32, ctx)
            self.rstd = sb(name + "_rstd", [P, NT], F32, ctx)
            self.tmp = sb(name + "_tmp", [P, NT], F32, ctx)
            self.parts = parts
            self.roots = [Rsqrt(self.var[:, lo:hi], self.rstd[:, lo:hi], self.tmp[:, lo:hi]) for lo, hi in parts]
            self.seen = sem(name + "_seen")

        def stats_of(self, v, src, part=0):
            lo, hi = self.parts[part]
            with v.Fori(lo, hi) as d:
                v.bn_stats(self.stats[:, bass.ds(d, 1), :], src[:, bass.ds(d, 1), :]).then_inc(self.seen.h, 1)
            v.wait_ge(self.seen.h, hi)
            mean_e, sq_e, mean_o, sq_o = (self.stats[:, lo:hi, j] for j in (1, 2, 4, 5))
            mean, tmp, var = self.mean[:, lo:hi], self.tmp[:, lo:hi], self.var[:, lo:hi]
            v.tensor_tensor(tmp, mean_e, mean_o, ALU.subtract).then_inc(v_step.h, 1)
            v.wait_ge(v_step.h, v_step.next())
            v.tensor_tensor(mean, mean_e, mean_o, ALU.add).then_inc(v_step.h, 1)
            v.wait_ge(v_step.h, v_step.next())
            v.tensor_scalar(mean, mean, 0.5, None, ALU.mult).then_inc(v_step.h, 1)
            v.wait_ge(v_step.h, v_step.next())
            v.tensor_tensor(tmp, tmp, tmp, ALU.mult).then_inc(v_step.h, 1)
            v.wait_ge(v_step.h, v_step.next())
            v.tensor_tensor(var, sq_e, sq_o, ALU.add).then_inc(v_step.h, 1)
            v.wait_ge(v_step.h, v_step.next())
            v.tensor_scalar(var, var, 1.0 / F, EPS, ALU.mult, ALU.add).then_inc(v_step.h, 1)
            v.wait_ge(v_step.h, v_step.next())
            v.scalar_tensor_tensor(var, tmp, 0.25, var, ALU.mult, ALU.add).then_inc(v_step.h, 1)
            v.wait_ge(v_step.h, v_step.next())
            self.roots[part].vector(v)

        def rows(self, v, src, dst, d, ready):
            v.tensor_scalar(dst, src[:, bass.ds(d, 1), :].rearrange("p a f -> p (a f)"), self.mean[:, bass.ds(d, 1)],
                            self.rstd[:, bass.ds(d, 1)], ALU.subtract, ALU.mult).then_inc(ready.h, 1)

    def load_weights(sp, w, dst):
        sp.dma_start(dst, w.rearrange("(c p) n -> p c n", p=P)).then_inc(loaded.h, 16)

    def turn(pe, d, k, rows_ready):
        pe.wait_ge(rows_ready.h, d + 1)
        pe.wait_ge(turned_out.h, turned_out.base + d + 1)
        for c in range(FC):
            mm = pe.transpose(ps[k][:, c * P:(c + 1) * P], stage[:, k, c * P:(c + 1) * P], ident[:])
        mm.then_inc(turned.h, 1)

    def multiply(pe, w, d, k, lhs_ready, lhs_credit, ncols=F, bias=None):
        pe.wait_ge(lhs_ready.h, lhs_ready.base + d + 1 + lhs_credit)
        pe.wait_ge(projected_out.h, projected_out.base + d + 1)
        if bias is not None:
            pe.matmul(ps[2 + k][:, 0:ncols], ones[0:1, :], bias[:, 0:ncols], start=True, stop=False)
        for c in range(FC):
            mm = pe.matmul(ps[2 + k][:, 0:ncols], lhs[:, k, c, :], w[:, c, 0:ncols], start=(c == 0 and bias is None), stop=(c == FC - 1))
        mm.then_inc(projected.h, 1)

    def turn_and_multiply(pe, w, rows_ready, ncols=F, bias=None):
        turn(pe, 0, 0, rows_ready)
        with pe.Fori(0, NT // 2) as i:
            turn(pe, 2 * i + 1, 1, rows_ready)
            multiply(pe, w, 2 * i, 0, turned_out, 2, ncols, bias)
            turn(pe, 2 * i + 2, 0, rows_ready)
            multiply(pe, w, 2 * i + 1, 1, turned_out, 2, ncols, bias)
        multiply(pe, w, NT - 1, 0, turned_out, 2, ncols, bias)

    def turned_to_lhs(a, norm):
        for (lo, hi), root in zip(norm.parts, norm.roots):
            root.scalar(a)
            for d, k in node_tiles(a, lo, hi):
                tile_to_lhs(a, d, k)

    def tile_to_lhs(a, d, k):
        a.wait_ge(turned.h, turned.base + d + 1 + 2)
        a.wait_ge(projected.h, projected.base + d + 1)
        a.activation(lhs[:, k].rearrange("p c n -> p (c n)"), ps[k][:, 0:F], ACT.Copy).then_inc(turned_out.h, 1)

    def scale_to_acc(v, d, k):
        v.wait_ge(projected.h, projected.base + d + 1 + 2)
        v.tensor_scalar(acc[:, bass.ds(d, 1), :].rearrange("p a f -> p (a f)"), ps[2 + k][:, 0:F], dinv[:, bass.ds(d, 1)], None, ALU.mult).then_inc(projected_out.h, 1)

    def store_acc(sp):
        for d, k in node_tiles(sp):
            sp.wait_ge(projected_out.h, projected_out.base + d + 1 + 2)
            sp.dma_start(node_table[bass.ds(d * P, P), :], acc[:, bass.ds(d, 1), :].rearrange("p a f -> p (a f)")).then_inc(stored.h, 16)
        sp.wait_ge(stored.h, stored.base + 16 * NT)

    def project_counted(turned_too=True):
        if turned_too:
            turned.base += NT
            turned_out.base += NT
        projected.base += NT
        projected_out.base += NT
        stored.base += 16 * NT

    def first_projection():
        with ExitStack() as ctx:
            norm = NodeNorm(ctx, "ln0", PARTS)
            rows_ready, vec_in = sem("rows_ready"), sem("vec_in")
            with nc.Block() as block:
                @block.sync
                def _(sp):
                    load_weights(sp, t["L0_gnn_W1"], wts[:])
                    with nc.allow_non_contiguous_dma("vectors of 256 features onto partitions"):
                        for k in range(3):
                            for j, name in enumerate(("b", "g", "be")):
                                sp.dma_start(vecs[:, k, j, :], t[f"L0_gnn_{name}{k + 1}"].rearrange("(c p) -> p c", p=P)).then_inc(vec_in.h, 16)
                    store_acc(sp)
                    sp.wait_ge(vec_in.h, 16 * 9)

                @block.vector
                def _(v):
                    v.wait_ge(x_loaded.h, x_loaded.base + 32)

                    def stage_rows(d, k):
                        v.wait_ge(turned.h, turned.base + d + 1)
                        norm.rows(v, feat, stage[:, k, :], d, rows_ready)

                    two_ahead(v, stage_rows, lambda d, k: scale_to_acc(v, d, k), lambda part: norm.stats_of(v, feat, part))

                @block.scalar
                def _(a):
                    turned_to_lhs(a, norm)

                @block.tensor
                def _(pe):
                    pe.wait_ge(loaded.h, loaded.base + 16)
                    turn_and_multiply(pe, wts, rows_ready)
            x_loaded.base += 32
            loaded.base += 16
            project_counted()

    first_projection()

    def gather_rows(g, rows, table):
        with g.Fori(0, ITERS) as i:
            for h in range(2):
                g.wait_ge(aggregated.h, aggregated.base + (i * 2 + h + 1) * G)
                g.tensor_copy(idx[:, h, :], psrc[:, bass.ds(i * 2 * G + h * G, G)]).then_inc(idx_ready.h, 1)
                g.wait_ge(idx_ready.h, idx_ready.base + 2 * i + h + 1)
                g.tensor_tensor(carrier[:], psrc[:, 0:1], psrc[:, 0:1], ALU.add)
                for b in range(G):
                    s = h * G + b
                    g.indirect_dma_start(rows[:, s, :], None, table,
                                         bass.IndirectOffsetOnAxis(ap=idx[:, h, b:b + 1], axis=0)).then_inc(row_sem[s].h, 16)

    def gather_counted():
        aggregated.base += NPAIR
        added.base += NPAIR
        onehot_ready.base += 2 * ITERS + 1
        idx_ready.base += 2 * ITERS
        for s in row_sem:
            s.base += 16 * ITERS

    def mark_pairs(v, hot, q, h):
        v.tensor_tensor(hot[:, h], iota_f[:].rearrange("p (j n) -> p j n", j=1).to_broadcast([P, G, P]),
                        pdl[:, bass.ds(q * G, G)].rearrange("p (j n) -> p j n", n=1).to_broadcast([P, G, P]),
                        ALU.is_equal).then_inc(onehot_ready.h, 1)

    def pair_bank(b, n=F):
        return ps[4 + b // 2][:, b % 2 * F:b % 2 * F + n]

    def aggregate(pe, hot, rows, i, h):
        pe.wait_ge(onehot_ready.h, onehot_ready.base + 2 * i + h + 1)
        for b in range(G):
            s = h * G + b
            pe.wait_ge(row_sem[s].h, row_sem[s].base + 16 * (i + 1))
            if b % 2 == 0:
                pe.wait_ge(added.h, added.base + (2 * i + h) * G + b + 2)
            pe.matmul(pair_bank(b), hot[:, h, b, :], rows[:, s, :], start=True, stop=True).then_inc(aggregated.h, 1)

    def add_pairs(v, i, h):
        for b in range(G):
            n = (2 * i + h) * G + b
            d = v.value_load(prow[0:1, bass.ds(n, 1)], min_val=0, max_val=NT - 1)
            row = acc[:, bass.ds(d, 1), :].rearrange("p a f -> p (a f)")
            if b % 2 == 0:
                v.wait_ge(aggregated.h, aggregated.base + 2 * G + n + 2)
            v.wait_ge(added.h, added.base + G + n)
            v.tensor_tensor(row, row, pair_bank(b), ALU.add).then_inc(added.h, 1)

    class EdgeTerms:

        def __init__(self, ctx):
            self.terms = sb("edge_terms", [P, NPAIR, HEADS], F32, ctx)
            self.rows = sb("edge_rows", [P, 2, G, EDIM], F32, ctx)
            self.turned_rows = sb("edge_t", [P, 2, G // 2, P], F32, ctx)
            self.weights = sb("edge_w", [P, 2 * HEADS], F32, ctx)
            self.we = sb("we", [P, F], F32, ctx)
            self.attn = sb("attn_e", [P, F], F32, ctx)
            self.weights_in, self.weights_set, self.done = sem("edge_w_in"), sem("edge_w_set"), sem("edge_terms_out")
            self.landed = [sem(f"edge_in{h}") for h in range(2)]
            self.turned, self.kept = sem("edge_turned"), sem("edge_kept")
            self.multiplied, self.stored = sem("edge_multiplied"), sem("edge_terms_kept")

        def sync(self, sp):
            for j in range(2):
                sp.dma_start(self.we[j * EDIM:(j + 1) * EDIM, :], t["L1_gnn_W_e"]).then_inc(self.weights_in.h, 16)
            sp.dma_start(self.attn[:], t["L1_gnn_attn_e"].rearrange("(a h) d -> a (h d)", a=1).to_broadcast([P, F])).then_inc(self.weights_in.h, 16)
            with sp.Fori(0, ITERS) as i:
                for h in range(2):
                    first_edges = in_registers(sp, prow[1:2, bass.ds((2 * i + h) * G, G)], E - P)
                    sp.wait_ge(self.turned.h, 2 * i + h + 1)
                    for b in range(G):
                        sp.dma_start(self.rows[:, h, b, :], t["edge_attr_64"][bass.ds(first_edges[b], P), :]).then_inc(self.landed[h].h, 16)

        def store(self, sp):
            sp.wait_ge(self.stored.h, 2 * ITERS + 2)
            sp.dma_start(ee_table, self.terms[:].rearrange("p n e -> p (n e)")).then_inc(self.done.h, 16)

        def vector(self, v):
            for s in (self.turned, self.kept, self.multiplied, self.stored):
                v.sem_inc(s.h, 2)
            v.wait_ge(self.weights_in.h, 16 * 3)
            v.memset(self.weights[:], 0.0).then_inc(v_step.h, 1)
            v.tensor_tensor(self.we[:], self.we[:], self.attn[:], ALU.mult).then_inc(v_step.h, 1)
            v_step.next()
            v.wait_ge(v_step.h, v_step.next())
            for j in range(2):
                r = slice(j * EDIM, (j + 1) * EDIM)
                v.tensor_reduce(self.weights[r, j * HEADS:(j + 1) * HEADS], self.we[r, :].rearrange("p (h d) -> p h d", d=HD), AX.X, ALU.add).then_inc(self.weights_set.h, 1)

        def scalar(self, a):
            with a.Fori(0, ITERS) as i:
                for h in range(2):
                    a.wait_ge(self.turned.h, 2 * i + h + 1 + 2)
                    a.wait_ge(self.multiplied.h, 2 * i + h + 1)
                    a.activation(self.turned_rows[:, h].rearrange("p j n -> p (j n)"), ps[h][:], ACT.Copy).then_inc(self.kept.h, 1)
                    a.wait_ge(self.multiplied.h, 2 * i + h + 1 + 2)
                    a.activation(self.terms[:, bass.ds((2 * i + h) * G, G), :], ps[2 + h][:, 0:G * HEADS].rearrange("p (j e) -> p j e", e=HEADS), ACT.Copy).then_inc(self.stored.h, 1)

        def turn(self, pe, q, i, h):
            pe.wait_ge(self.landed[h].h, 16 * G * (i + 1))
            pe.wait_ge(self.kept.h, q + 1)
            for j in range(G // 2):
                mm = pe.transpose(ps[h][:, j * P:(j + 1) * P], self.rows[:, h, 2 * j:2 * j + 2, :].rearrange("p a c -> p (a c)"), ident[:])
            mm.then_inc(self.turned.h, 1)

        def multiply(self, pe, q, h):
            pe.wait_ge(self.kept.h, q + 1 + 2)
            pe.wait_ge(self.stored.h, q + 1)
            for j in range(G // 2):
                mm = pe.matmul(ps[2 + h][:, j * 2 * HEADS:(j + 1) * 2 * HEADS], self.turned_rows[:, h, j, :], self.weights[:], start=True, stop=True)
            mm.then_inc(self.multiplied.h, 1)

    def gcn_layer(k):
        last = k == 2
        with ExitStack() as ctx:
            hot = sb("hot", [P, 2, G, P], F32, ctx)
            rows = sb("rows", [P, 2 * G, F], F32, ctx)
            bn = sb("bn", [P, FC, -(-N // (4 * P)), 6], F32, ctx)
            mv = sb("bn_mv", [P, FC, 2], F32, ctx)
            var = sb("bn_var", [P, FC], F32, ctx)
            rstd = sb("bn_rstd", [P, FC], F32, ctx)
            tmp = sb("bn_tmp", [P, FC], F32, ctx)
            gain = sb("gain", [P, FC], F32, ctx)
            shift = sb("shift", [P, FC], F32, ctx)
            y_ready, affine_set, affine_ready, bn_seen = sem(f"y_ready{k}"), sem(f"affine_set{k}"), sem(f"affine_ready{k}"), sem(f"bn_seen{k}")
            last_ready = sem(f"last_ready{k}")
            root = Rsqrt(var[:], rstd[:], tmp[:])
            if k == 0:
                edges = EdgeTerms(ctx)
            if k == 1:
                zeros = sb("zeros", [P, F], F32, ctx)
                zeros_set, zeros_out = sem("zeros_set"), sem("zeros_out")
            with nc.Block() as block:
                @block.gpsimd
                def _(g):
                    gather_rows(g, rows, node_table)

                @block.sync
                def _(sp):
                    if not last:
                        load_weights(sp, t[f"L0_gnn_W{k + 2}"], wts[:])
                    if k == 0:
                        edges.sync(sp)
                        edges.store(sp)
                    if k == 1:
                        sp.wait_ge(zeros_set.h, 1)
                        with sp.Fori(0, MT + 2) as m:
                            sp.dma_start(slot_rows[bass.ds(m * P, P), :], zeros[:]).then_inc(zeros_out.h, 16)
                        for j in range(2):
                            sp.dma_start(slot_out[CAP + j * P:CAP + (j + 1) * P, :], zeros[:]).then_inc(zeros_out.h, 16)
                    if not last:
                        store_acc(sp)
                    else:
                        sp.wait_ge(y_ready.h, NT)
                        load_rows(sp, acc, t["x"], x_loaded)
                    if k == 0:
                        sp.wait_ge(edges.done.h, 16)
                    if k == 1:
                        sp.wait_ge(zeros_out.h, 16 * (MT + 4))

                @block.vector
                def _(v):
                    if k == 0:
                        edges.vector(v)
                    if k == 1:
                        v.memset(zeros[:], 0.0).then_inc(zeros_set.h, 1)
                    mark_pairs(v, hot, 0, 0)
                    with v.Fori(0, ITERS) as i:
                        v.wait_ge(aggregated.h, aggregated.base + (i + 1) * 2 * G)
                        mark_pairs(v, hot, 2 * i + 1, 1)
                        add_pairs(v, i, 0)
                        mark_pairs(v, hot, 2 * i + 2, 0)
                        add_pairs(v, i, 1)
                    v.wait_ge(added.h, added.base + G + NPAIR)

                    def stage_rows(d, par):
                        v.wait_ge(turned.h, turned.base + d + 1)
                        row = acc[:, bass.ds(d, 1), :].rearrange("p a f -> p (a f)")
                        v.tensor_scalar(stage[:, par, :], row, dinv[:, bass.ds(d, 1)], None, ALU.mult).then_inc(y_ready.h, 1)

                    def part_stats(j):
                        n = min(4 * P, N - j * 4 * P) if isinstance(j, int) else 4 * P
                        for c in range(FC):
                            v.bn_stats(bn[:, c, bass.ds(j, 1), :].rearrange("p a s -> p (a s)"), feat_t[:, c, bass.ds(j * 4 * P, n)]).then_inc(bn_seen.h, 1)

                    for m in range(4):
                        stage_rows(m, m % 2)
                    with v.Fori(1, NT // 4) as j:
                        for m in range(4):
                            stage_rows(4 * j + m, m % 2)
                        v.wait_ge(turned_out.h, turned_out.base + 4 * j + 2)
                        part_stats(j - 1)
                    for d in range(NT // 4 * 4, NT):
                        stage_rows(d, d % 2)
                    v.wait_ge(turned_out.h, turned_out.base + NT + 2)
                    for j in range(NT // 4 - 1, -(-N // (4 * P))):
                        part_stats(j)
                    v.wait_ge(bn_seen.h, FC * -(-N // (4 * P)))
                    for c in range(FC):
                        v.bn_aggr(mv[:, c, :], bn[:, c].rearrange("p j s -> p (j s)")).then_inc(v_step.h, 1)
                        v.wait_ge(v_step.h, v_step.next())
                    v.tensor_scalar(var[:], mv[:, :, 1], EPS, None, ALU.add).then_inc(v_step.h, 1)
                    v.wait_ge(v_step.h, v_step.next())
                    root.vector(v)
                    v.tensor_tensor(gain[:], rstd[:], vecs[:, k, 1, :], ALU.mult).then_inc(v_step.h, 1)
                    v.wait_ge(v_step.h, v_step.next())
                    v.tensor_tensor(tmp[:], mv[:, :, 0], gain[:], ALU.mult).then_inc(v_step.h, 1)
                    v.wait_ge(v_step.h, v_step.next())
                    v.tensor_tensor(shift[:], vecs[:, k, 2, :], tmp[:], ALU.subtract).then_inc(v_step.h, 1)
                    v.wait_ge(v_step.h, v_step.next())
                    v.nop().then_inc(affine_set.h, 1)

                    def normalize_last(d, par):
                        v.wait_ge(projected.h, projected.base + d + 1)
                        v.tensor_scalar(lhs[:, par, FC - 1, :], feat_t[:, FC - 1, bass.ds(d * P, P)], gain[:, FC - 1:FC], shift[:, FC - 1:FC], ALU.mult, ALU.add).then_inc(last_ready.h, 1)

                    def add_to_acc(d, par):
                        v.wait_ge(projected.h, projected.base + d + 1 + 2)
                        row = acc[:, bass.ds(d, 1), :].rearrange("p a f -> p (a f)")
                        v.tensor_tensor(row, row, ps[2 + par][:, 0:F], ALU.add).then_inc(projected_out.h, 1)

                    if last:
                        v.wait_ge(x_loaded.h, x_loaded.base + 32)
                    two_ahead(v, normalize_last, add_to_acc if last else lambda d, par: scale_to_acc(v, d, par), lambda part: None)

                @block.scalar
                def _(a):
                    if k == 0:
                        edges.scalar(a)
                    for d, par in node_tiles(a):
                        a.wait_ge(turned.h, turned.base + d + 1 + 2)
                        for c in range(FC):
                            op = a.activation(feat_t[:, c, bass.ds(d * P, P)], ps[par][:, c * P:(c + 1) * P], ACT.Identity, bias=vecs[:, k, 0, c:c + 1])
                        op.then_inc(turned_out.h, 1)
                    root.scalar(a)
                    a.wait_ge(affine_set.h, 1)
                    for d, par in node_tiles(a):
                        a.wait_ge(projected.h, projected.base + d + 1)
                        for c in range(FC - 1):
                            op = a.activation(lhs[:, par, c, :], feat_t[:, c, bass.ds(d * P, P)], ACT.Identity, bias=shift[:, c:c + 1], scale=gain[:, c:c + 1])
                        op.then_inc(affine_ready.h, 1)

                @block.tensor
                def _(pe):
                    if k == 0:
                        pe.wait_ge(edges.weights_set.h, 2)
                    with pe.Fori(0, ITERS) as i:
                        for h in range(2):
                            if k == 0:
                                edges.turn(pe, 2 * i + h, i, h)
                            aggregate(pe, hot, rows, i, h)
                            if k == 0:
                                edges.multiply(pe, 2 * i + h, h)
                    for d, par in node_tiles(pe):
                        turn(pe, d, par, y_ready)
                    if not last:
                        pe.wait_ge(loaded.h, loaded.base + 16)
                        for d, par in node_tiles(pe):
                            pe.wait_ge(last_ready.h, d + 1)
                            multiply(pe, wts, d, par, affine_ready, 0)
                    else:
                        for d, par in node_tiles(pe):
                            pe.wait_ge(affine_ready.h, d + 1)
                            pe.wait_ge(last_ready.h, d + 1)
                            pe.wait_ge(projected_out.h, projected_out.base + d + 1)
                            for c in range(FC):
                                mm = pe.transpose(ps[2 + par][:, c * P:(c + 1) * P], lhs[:, par, c, :], ident[:])
                            mm.then_inc(projected.h, 1)
            gather_counted()
            project_counted()
            if last:
                x_loaded.base += 32
                stored.base -= 16 * NT
            else:
                loaded.base += 16

    for k in range(3):
        gcn_layer(k)
    w1 = shared[:].rearrange("p (e c n) -> p e c n", e=EXPERTS, c=FC)
    w1_in = sem("w1_in")

    def route():
        with ExitStack() as ctx:
            norm = NodeNorm(ctx, "ln1", PARTS)
            inner = NodeNorm(ctx, "ln_moe", [(0, NT)])
            wr = sb("wr", [P, FC, EXPERTS], F32, ctx)
            br = sb("br", [1, EXPERTS], F32, ctx)
            logits = sb("logits", [P, NT, EXPERTS], F32, ctx)
            low = sb("low", [P, NT, EXPERTS], F32, ctx)
            hits = sb("hits", [P, NT, EXPERTS], F32, ctx)
            pick = sb("pick", [P, 2, NT, EXPERTS], F32, ctx)
            both = sb("both", [P, NT, EXPERTS], F32, ctx)
            tot = sb("tot", [P, NT, EXPERTS], F32, ctx)
            run = sb("run", [P, NT, EXPERTS], F32, ctx)
            best = sb("best", [P, 2, NT], F32, ctx)
            top = sb("top", [P, NT], F32, ctx)
            order = sb("order", [P, EXPERTS], F32, ctx)
            node = sb("node", [P, NT], F32, ctx)
            node_i = sb("node_i", [P, NT], I32, ctx)
            valid = sb("valid", [P, NT], F32, ctx)
            spare = sb("spare", [P, NT], F32, ctx)
            slot_f = sb("slot_f", [P, 2, NT], F32, ctx)
            e8 = sb("e8", [P, 4, EXPERTS], F32, ctx)
            e8_i = sb("e8_i", [P, EXPERTS], I32, ctx)
            upto = sb("upto", [P, MT, EXPERTS], F32, ctx)
            z_done, z_ready, rows_ready, xn_ready = sem("z_done"), sem("z_ready"), sem("z_staged"), sem("xn_ready")
            numbered, exp_ready, exp_done = sem("numbered"), sem("exp_ready"), sem("exp_done")
            picked, ranked, slots_set = sem("picked"), sem("ranked"), sem("slots_set")
            slot_idx = sem("slot_idx")
            scattered = [sem(f"scattered{k}") for k in range(2)]
            with nc.Block() as block:
                @block.sync
                def _(sp):
                    sp.dma_start(resid.rearrange("(d p) f -> p d f", p=P), acc[:]).then_inc(stored.h, 16)
                    sp.dma_start(wr[:], t["L0_ffn_Wr"].rearrange("(c p) e -> p c e", p=P)).then_inc(loaded.h, 16)
                    sp.dma_start(br[:], t["L0_ffn_br"].rearrange("(a e) -> a e", a=1)).then_inc(loaded.h, 16)
                    sp.wait_ge(stored.h, stored.base + 16)
                    sp.wait_ge(z_done.h, NT)
                    for e in range(EXPERTS):
                        sp.dma_start(w1[:, e], t["L0_ffn_W1"][e].rearrange("(c p) n -> p c n", p=P)).then_inc(w1_in.h, 16)

                @block.gpsimd
                def _(g):
                    g.iota(node_i[:], [[P, NT]], base=0, channel_multiplier=1).then_inc(numbered.h, 1)
                    for d, k in node_tiles(g):
                        g.wait_ge(z_done.h, d + 1)
                        g.wait_ge(turned.h, turned.base + d + 1)
                        g.tensor_copy(stage[:, k, :], rows_of(feat, d)).then_inc(rows_ready.h, 1)
                    g.wait_ge(slots_set.h, 1)
                    for d, k in node_tiles_apart(g):
                        wait_earlier(g, scattered[k], d, k, 32)
                        g.tensor_copy(idx[:, k, 0:2], slots[:, :, bass.ds(d, 1)].rearrange("p a d -> p (a d)")).then_inc(slot_idx.h, 1)
                        g.wait_ge(xn_ready.h, d + 1)
                        g.wait_ge(slot_idx.h, d + 1)
                        g.tensor_tensor(carrier[:], psrc[:, 0:1], psrc[:, 0:1], ALU.add)
                        for j in range(2):
                            g.indirect_dma_start(slot_rows, bass.IndirectOffsetOnAxis(ap=idx[:, k, j:j + 1], axis=0), stage[:, k, :], None).then_inc(scattered[k].h, 16)
                    g.wait_ge(scattered[0].h, 32 * (NT // 2 + 1))
                    g.wait_ge(scattered[1].h, 32 * (NT // 2))

                @block.vector
                def _(v):
                    for part, (lo, hi) in enumerate(PARTS):
                        norm.stats_of(v, acc, part)
                        for d, _ in node_tiles(v, lo, hi):
                            norm.rows(v, acc, rows_of(feat, d), d, z_done)
                    v.wait_ge(z_done.h, NT)
                    inner.stats_of(v, feat)
                    v.wait_ge(projected_out.h, projected_out.base + NT + 2)

                    def over_e(x):
                        return x.rearrange("p (d a) -> p d a", a=1).to_broadcast([P, NT, EXPERTS])

                    def over_d(x, n=NT):
                        return x.rearrange("p (a e) -> p a e", a=1).to_broadcast([P, n, EXPERTS])

                    v.wait_ge(numbered.h, 1)
                    v.tensor_copy(node[:], node_i[:]).then_inc(v_step.h, 1)
                    v.wait_ge(v_step.h, v_step.next())
                    v.tensor_scalar(valid[:], node[:], float(N), None, ALU.is_lt).then_inc(v_step.h, 1)
                    v.wait_ge(v_step.h, v_step.next())
                    v.tensor_scalar(order[:], iota_f[:, 0:EXPERTS], -1.0, float(EXPERTS), ALU.mult, ALU.add).then_inc(v_step.h, 1)
                    v.wait_ge(v_step.h, v_step.next())
                    src = logits
                    for j in range(2):
                        v.tensor_reduce(best[:, j, :], src[:], AX.X, ALU.max).then_inc(v_step.h, 1)
                        v.wait_ge(v_step.h, v_step.next())
                        v.tensor_tensor(hits[:], src[:], over_e(best[:, j, :]), ALU.is_equal).then_inc(v_step.h, 1)
                        v.wait_ge(v_step.h, v_step.next())
                        v.tensor_tensor(hits[:], hits[:], over_d(order[:]), ALU.mult).then_inc(v_step.h, 1)
                        v.wait_ge(v_step.h, v_step.next())
                        v.tensor_reduce(top[:], hits[:], AX.X, ALU.max).then_inc(v_step.h, 1)
                        v.wait_ge(v_step.h, v_step.next())
                        v.tensor_tensor(pick[:, j], hits[:], over_e(top[:]), ALU.is_equal).then_inc(v_step.h, 1)
                        v.wait_ge(v_step.h, v_step.next())
                        if j == 0:
                            v.scalar_tensor_tensor(low[:], pick[:, 0], -BIG, logits[:], ALU.mult, ALU.add).then_inc(v_step.h, 1)
                            v.wait_ge(v_step.h, v_step.next())
                            src = low
                        v.tensor_tensor(pick[:, j], pick[:, j], over_e(valid[:]), ALU.mult).then_inc(v_step.h, 1)
                        v.wait_ge(v_step.h, v_step.next())
                    v.tensor_tensor(top[:], best[:, 1, :], best[:, 0, :], ALU.subtract).then_inc(v_step.h, 1)
                    v.wait_ge(v_step.h, v_step.next())
                    v.nop().then_inc(exp_ready.h, 1)
                    v.tensor_tensor(both[:], pick[:, 0], pick[:, 1], ALU.add).then_inc(v_step.h, 1)
                    v.wait_ge(v_step.h, v_step.next())
                    v.nop().then_inc(picked.h, 1)
                    v.wait_ge(exp_done.h, 1)
                    v.tensor_scalar(spare[:], best[:, 1, :], 1.0, None, ALU.add).then_inc(v_step.h, 1)
                    v.wait_ge(v_step.h, v_step.next())
                    v.reciprocal(gate[:, 0, :], spare[:]).then_inc(v_step.h, 1)
                    v.wait_ge(v_step.h, v_step.next())
                    v.tensor_tensor(gate[:, 1, :], best[:, 1, :], gate[:, 0, :], ALU.mult).then_inc(v_step.h, 1)
                    v.wait_ge(v_step.h, v_step.next())
                    v.wait_ge(ranked.h, 1)
                    v.tensor_copy(tot[:], ps[1][:, 0:NT * EXPERTS].rearrange("p (d e) -> p d e", e=EXPERTS)).then_inc(v_step.h, 1)
                    v.wait_ge(v_step.h, v_step.next())
                    for e in range(EXPERTS):
                        v.tensor_tensor_scan(run[:, :, e], ones[:, 0:NT], tot[:, :, e], 0.0, ALU.mult, ALU.add).then_inc(v_step.h, 1)
                        v.wait_ge(v_step.h, v_step.next())
                    count, tiles, upto_e, begin = (e8[:, j, :] for j in range(4))
                    v.tensor_scalar(count, run[:, NT - 1, :], float(P - 1), None, ALU.add).then_inc(v_step.h, 1)
                    v.wait_ge(v_step.h, v_step.next())
                    v.tensor_tensor(run[:], run[:], tot[:], ALU.subtract).then_inc(v_step.h, 1)
                    v.wait_ge(v_step.h, v_step.next())
                    v.tensor_tensor(run[:], run[:], ps[0][:, 0:NT * EXPERTS].rearrange("p (d e) -> p d e", e=EXPERTS), ALU.add).then_inc(v_step.h, 1)
                    v.wait_ge(v_step.h, v_step.next())
                    v.tensor_copy(e8_i[:], count).then_inc(v_step.h, 1)
                    v.wait_ge(v_step.h, v_step.next())
                    v.tensor_scalar(e8_i[:], e8_i[:], 7, None, ALU.arith_shift_right).then_inc(v_step.h, 1)
                    v.wait_ge(v_step.h, v_step.next())
                    v.tensor_copy(tiles, e8_i[:]).then_inc(v_step.h, 1)
                    v.wait_ge(v_step.h, v_step.next())
                    v.tensor_tensor_scan(upto_e, ones[:, 0:EXPERTS], tiles, 0.0, ALU.mult, ALU.add).then_inc(v_step.h, 1)
                    v.wait_ge(v_step.h, v_step.next())
                    v.tensor_tensor(begin, upto_e, tiles, ALU.subtract).then_inc(v_step.h, 1)
                    v.wait_ge(v_step.h, v_step.next())
                    v.tensor_scalar(begin, begin, float(P), None, ALU.mult).then_inc(v_step.h, 1)
                    v.wait_ge(v_step.h, v_step.next())
                    v.tensor_tensor(run[:], run[:], over_d(begin), ALU.add).then_inc(v_step.h, 1)
                    v.wait_ge(v_step.h, v_step.next())
                    v.tensor_scalar(spare[:], node[:], float(CAP - (NT - 1) * P), None, ALU.add).then_inc(v_step.h, 1)
                    v.wait_ge(v_step.h, v_step.next())
                    v.tensor_scalar(top[:], valid[:], -1.0, 1.0, ALU.mult, ALU.add).then_inc(v_step.h, 1)
                    v.wait_ge(v_step.h, v_step.next())
                    v.tensor_tensor(spare[:], spare[:], top[:], ALU.mult).then_inc(v_step.h, 1)
                    v.wait_ge(v_step.h, v_step.next())
                    for j in range(2):
                        v.tensor_tensor(hits[:], pick[:, j], run[:], ALU.mult).then_inc(v_step.h, 1)
                        v.wait_ge(v_step.h, v_step.next())
                        v.tensor_reduce(slot_f[:, j, :], hits[:], AX.X, ALU.add).then_inc(v_step.h, 1)
                        v.wait_ge(v_step.h, v_step.next())
                        v.tensor_tensor(slot_f[:, j, :], slot_f[:, j, :], spare[:], ALU.add).then_inc(v_step.h, 1)
                        v.wait_ge(v_step.h, v_step.next())
                        v.scalar_tensor_tensor(spare[:], top[:], float(P), spare[:], ALU.mult, ALU.add).then_inc(v_step.h, 1)
                        v.wait_ge(v_step.h, v_step.next())
                    v.tensor_copy(slots[:], slot_f[:]).then_inc(v_step.h, 1)
                    v.wait_ge(v_step.h, v_step.next())
                    v.nop().then_inc(slots_set.h, 1)
                    v.tensor_tensor(upto[:], over_d(upto_e, MT), iota_f[:, 0:MT].rearrange("p (k a) -> p k a", a=1).to_broadcast([P, MT, EXPERTS]), ALU.is_le).then_inc(v_step.h, 1)
                    v.wait_ge(v_step.h, v_step.next())
                    v.tensor_reduce(tile_expert[:], upto[:], AX.X, ALU.add).then_inc(v_step.h, 1)
                    v.wait_ge(v_step.h, v_step.next())
                    v.tensor_scalar(tile_expert[:], tile_expert[:], float(EXPERTS - 1), None, ALU.min).then_inc(v_step.h, 1)
                    v.wait_ge(v_step.h, v_step.next())
                    v.tensor_copy(tile_expert_i[:], tile_expert[0:1, :]).then_inc(v_step.h, 1)
                    v.wait_ge(v_step.h, v_step.next())
                    for d, k in node_tiles_apart(v):
                        wait_earlier(v, scattered[k], d, k, 32)
                        inner.rows(v, feat, stage[:, k, :], d, xn_ready)

                @block.scalar
                def _(a):
                    def keep_logits(d, k):
                        a.wait_ge(projected.h, projected.base + d + 1 + 2)
                        a.activation(logits[:, bass.ds(d, 1), :].rearrange("p a e -> p (a e)"), ps[2 + k][:, 0:EXPERTS], ACT.Copy).then_inc(projected_out.h, 1)

                    for part, (lo, hi) in enumerate(PARTS):
                        norm.roots[part].scalar(a)
                        if part == 0:
                            tile_to_lhs(a, 0, 0)
                        with a.Fori(max(lo // 2 - 1, 0), NT // 2 if hi == NT else hi // 2 - 1) as i:
                            tile_to_lhs(a, 2 * i + 1, 1)
                            keep_logits(2 * i, 0)
                            tile_to_lhs(a, 2 * i + 2, 0)
                            keep_logits(2 * i + 1, 1)
                    keep_logits(NT - 1, 0)
                    inner.roots[0].scalar(a)
                    a.wait_ge(exp_ready.h, 1)
                    a.activation(best[:, 1, :], top[:], ACT.Exp).then_inc(exp_done.h, 1)

                @block.tensor
                def _(pe):
                    pe.wait_ge(loaded.h, loaded.base + 32)
                    turn_and_multiply(pe, wr, rows_ready, EXPERTS, br)
                    pe.wait_ge(picked.h, 1)
                    flat = both[:].rearrange("p d e -> p (d e)")
                    pe.matmul(ps[0][:, 0:NT * EXPERTS], excl[:], flat, start=True, stop=True)
                    pe.matmul(ps[1][:, 0:NT * EXPERTS], ones[:], flat, start=True, stop=True).then_inc(ranked.h, 1)
            loaded.base += 32
            project_counted()
            stored.base += 16 - 16 * NT

    route()
    bigs.close()

    def experts():
        with ExitStack() as ctx:
            w2 = sb("w2", [P, EXPERTS, HC, F], F32, ctx)
            lng = sb("lng", [P, FC, EXPERTS], F32, ctx)
            lnb = sb("lnb", [P, FC, EXPERTS], F32, ctx)
            bias_f = sb("bias_f", [EXPERTS, F], F32, ctx)
            b1 = sb("b1", [P, HC, EXPERTS], F32, ctx)
            bias = sb("bias", [96, F], BF16, ctx)
            expert_f = sb("expert_f", [96, 1], F32, ctx)
            expert_i = sb("expert_i", [96, 1], I32, ctx)
            sel2 = sb("sel2", [96, 2, P], BF16, ctx)
            xt = sb("xt", [P, 2, F], F32, ctx)
            xe = sb("xe", [P, 2, FC, P], F32, ctx)
            hid_t = sb("hid_t", [P, 2, HC, P], F32, ctx)
            y = sb("y", [P, 2, F], F32, ctx)
            w_in, vec_in, split, lane = sem("w_in"), sem("vec_in_moe"), sem("bias_split"), sem("expert_lane")
            xt_in = [sem(f"xt_in{k}") for k in range(2)]
            y_out = [sem(f"y_out{k}") for k in range(2)]
            x_turned, x_scaled = sem("x_turned"), sem("x_scaled")
            h_done, h_act = sem("h_done"), sem("h_act")
            held = sb("held_w1", [P, 2, FC, HID], F32, ctx)
            held_ready = sem("held_ready")
            y_done, y_kept, sel2_ready = sem("y_done"), sem("y_kept"), sem("sel2_ready")

            def each(eng, lo, hi, body):
                n = (hi - lo) // 2
                if n:
                    with eng.Fori(0, n) as i:
                        body(2 * i + lo, lo % 2)
                        body(2 * i + lo + 1, (lo + 1) % 2)
                if (hi - lo) % 2:
                    body(hi - 1, (hi - 1) % 2)

            with nc.Block() as block:
                @block.sync
                def _(sp):
                    for e in range(EXPERTS):
                        sp.dma_start(w2[:, e], t["L0_ffn_W2"][e].rearrange("(c p) n -> p c n", p=P)).then_inc(w_in.h, 16)

                    def load(k, par):
                        sp.dma_start(xt[:, par, :], slot_rows[bass.ds(k * P, P), :]).then_inc(xt_in[par].h, 16)

                    load(0, 0)
                    load(1, 1)

                    def reload(k, par):
                        sp.wait_ge(x_turned.h, k + 1)
                        load(k + 2, par)

                    def store(k, par):
                        sp.wait_ge(y_kept.h, k + 1)
                        sp.dma_start(slot_out[bass.ds(k * P, P), :], y[:, par, :]).then_inc(y_out[par].h, 16)

                    def body(k, par):
                        reload(k, par)
                        store(k - 3, 1 - par)

                    each(sp, 0, 3, reload)
                    each(sp, 3, MT - 2, body)
                    each(sp, MT - 5, MT, store)
                    for s in y_out:
                        sp.wait_ge(s.h, 16 * (MT // 2))

                @block.gpsimd
                def _(g):
                    for j in range(3):
                        g.iota(expert_i[32 * j:32 * j + 32, :], [[0, 1]], base=0, channel_multiplier=1).then_inc(lane.h, 1)

                @block.vector
                def _(v):
                    v.memset(bias[:], 0.0).then_inc(v_step.h, 1)
                    v.wait_ge(v_step.h, v_step.next())
                    v.wait_ge(lane.h, 3)
                    v.tensor_copy(expert_f[:], expert_i[:]).then_inc(v_step.h, 1)
                    v.wait_ge(v_step.h, v_step.next())
                    v.wait_ge(vec_in.h, 16 * (1 + 3 * EXPERTS))
                    for j in range(3):
                        part = bias[32 * j:32 * j + EXPERTS, :]
                        v.tensor_copy(part, bias_f[:]).then_inc(v_step.h, 1)
                        v.wait_ge(v_step.h, v_step.next())
                        if j < 2:
                            v.tensor_tensor(bias_f[:], bias_f[:], part, ALU.subtract).then_inc(v_step.h, 1)
                            v.wait_ge(v_step.h, v_step.next())
                    v.nop().then_inc(split.h, 1)

                    def select(k, par):
                        v.tensor_scalar(sel2[:, par, :], tile_expert[0:96, bass.ds(k, 1)].to_broadcast([96, P]), expert_f[:], None, ALU.is_equal).then_inc(sel2_ready.h, 1)

                    def keep_y(k, par):
                        v.wait_ge(y_done.h, k + 1)
                        wait_earlier(v, y_out[par], k, par, 16)
                        v.tensor_copy(y[:, par, :], ps[6 + par][:, 0:F]).then_inc(y_kept.h, 1)

                    def hold(k, par):
                        e = v.value_load(tile_expert_i[0:1, bass.ds(k, 1)], min_val=0, max_val=EXPERTS - 1)
                        if not isinstance(k, int) or k >= 2:
                            v.wait_ge(h_done.h, 2 * k - 2)
                            v.nop()
                        v.tensor_copy(held[:, par].rearrange("p c n -> p (c n)"), w1[:, bass.ds(e, 1)].rearrange("p a c n -> p (a c n)")).then_inc(held_ready.h, 1)

                    def body(k, par):
                        hold(k + 2, par)
                        keep_y(k, par)
                        select(k + 2, par)

                    select(0, 0)
                    select(1, 1)
                    v.wait_ge(w1_in.h, 16 * EXPERTS)
                    hold(0, 0)
                    hold(1, 1)
                    body(0, 0)
                    body(1, 1)
                    each(v, 2, MT - 2, body)
                    for k in (MT - 2, MT - 1):
                        keep_y(k, k % 2)

                @block.scalar
                def _(a):
                    with nc.allow_non_contiguous_dma("vectors of 256 features onto partitions"):
                        for e in range(EXPERTS):
                            a.dma_start(lng[:, :, e], t["L0_ffn_ln_g"][e].rearrange("(c p) -> p c", p=P)).then_inc(vec_in.h, 16)
                            a.dma_start(lnb[:, :, e], t["L0_ffn_ln_b"][e].rearrange("(c p) -> p c", p=P)).then_inc(vec_in.h, 16)
                            a.dma_start(b1[:, :, e], t["L0_ffn_b1"][e].rearrange("(c p) -> p c", p=P)).then_inc(vec_in.h, 16)
                    a.dma_start(bias_f[:], t["L0_ffn_b2"]).then_inc(vec_in.h, 16)
                    a.wait_ge(vec_in.h, 16 * (1 + 3 * EXPERTS))

                    def scale_x(k, par):
                        e = a.value_load(tile_expert_i[0:1, bass.ds(k, 1)], min_val=0, max_val=EXPERTS - 1)
                        a.wait_ge(x_turned.h, k + 1)
                        for c in range(FC):
                            op = a.activation(xe[:, par, c, :], ps[par][:, c * P:(c + 1) * P], ACT.Identity,
                                              bias=lnb[:, c, bass.ds(e, 1)], scale=lng[:, c, bass.ds(e, 1)])
                        op.then_inc(x_scaled.h, 1)

                    def act_h(k, par):
                        e = a.value_load(tile_expert_i[0:1, bass.ds(k, 1)], min_val=0, max_val=EXPERTS - 1)
                        for j in range(2):
                            a.wait_ge(h_done.h, 2 * k + j + 1)
                            for c in range(4):
                                op = a.activation(hid_t[:, par, 4 * j + c, :], ps[2 + 2 * par + j][:, c * P:(c + 1) * P], ACT.Gelu, bias=b1[:, 4 * j + c, bass.ds(e, 1)])
                            op.then_inc(h_act.h, 1)

                    def body(k, par):
                        act_h(k, par)
                        scale_x(k + 2, par)

                    scale_x(0, 0)
                    scale_x(1, 1)
                    each(a, 0, MT - 2, body)
                    for k in (MT - 2, MT - 1):
                        act_h(k, k % 2)

                @block.tensor
                def _(pe):
                    def turn_x(k, par):
                        pe.wait_ge(xt_in[par].h, (k - par) * 8 + 16)
                        for c in range(FC):
                            mm = pe.transpose(ps[par][:, c * P:(c + 1) * P], xt[:, par, c * P:(c + 1) * P], ident[:])
                        mm.then_inc(x_turned.h, 1)

                    def up(k, par):
                        pe.wait_ge(held_ready.h, k + 1)
                        pe.wait_ge(x_scaled.h, k + 1)
                        if not isinstance(k, int) or k >= 2:
                            pe.wait_ge(h_act.h, 2 * k - 2)
                        for j in range(2):
                            for c in range(4):
                                for f in range(FC):
                                    mm = pe.matmul(ps[2 + 2 * par + j][:, c * P:(c + 1) * P], held[:, par, f, (4 * j + c) * P:(4 * j + c + 1) * P],
                                                   xe[:, par, f, :], start=(f == 0), stop=(f == FC - 1))
                            mm.then_inc(h_done.h, 1)

                    def down(k, par):
                        e = pe.value_load(tile_expert_i[0:1, bass.ds(k, 1)], min_val=0, max_val=EXPERTS - 1)
                        pe.wait_ge(sel2_ready.h, k + 1)
                        pe.matmul(ps[6 + par][:, 0:F], sel2[:, par, :], bias[:], start=True, stop=False)
                        pe.wait_ge(h_act.h, 2 * k + 2)
                        for c in range(HC):
                            mm = pe.matmul(ps[6 + par][:, 0:F], hid_t[:, par, c, :], w2[:, bass.ds(e, 1), c, :].rearrange("p a n -> p (a n)"),
                                           start=False, stop=(c == HC - 1))
                        mm.then_inc(y_done.h, 1)

                    def body(k, par):
                        up(k + 1, 1 - par)
                        pe.wait_ge(x_scaled.h, k + 1)
                        turn_x(k + 2, par)
                        down(k, par)

                    turn_x(0, 0)
                    turn_x(1, 1)
                    up(0, 0)
                    pe.wait_ge(w_in.h, 16 * EXPERTS)
                    pe.wait_ge(split.h, 1)
                    body(0, 0)
                    body(1, 1)
                    each(pe, 2, MT - 2, body)
                    up(MT - 1, (MT - 1) % 2)
                    for k in (MT - 2, MT - 1):
                        down(k, k % 2)

    experts()
    shares.close()

    bigs = ExitStack()
    acc = sb("acc", [P, NT, F], F32, bigs)
    node_terms = sb("node_terms", [P, NT, HEADS], F32, bigs)
    HCOLS = HEADS * HROW
    WCOLS = HCOLS + HEADS

    def combine():
        with ExitStack() as ctx:
            norm = NodeNorm(ctx, "ln2", PARTS)
            expert_rows = sb("y_rows", [P, 2, 2, F], F32, ctx)
            y_in = [sem(f"y_in{k}") for k in range(2)]
            y_used, slot_idx, y_first = sem("y_used"), sem("slot_idx_back"), sem("y_first")
            stage2 = sb("stage2", [P, 2, HCOLS], F32, ctx)
            wcat = sb("wcat", [P, FC, WCOLS], F32, ctx)
            attn = sb("attn", [P, 2, F], F32, ctx)
            prod = sb("prod", [P, F], F32, ctx)
            rows_ready, attn_in, wcat_ready = sem("z2_staged"), sem("attn_in"), sem("wcat_ready")
            ft_out = [sem(f"ft_out{k}") for k in range(2)]
            ft_ready = sem("ft_ready")
            with nc.Block() as block:
                @block.sync
                def _(sp):
                    sp.dma_start(acc[:], resid.rearrange("(d p) f -> p d f", p=P)).then_inc(x_loaded.h, 16)
                    for c in range(FC):
                        sp.dma_start(wcat[:, c, 0:HCOLS].rearrange("p (h d) -> p h d", d=HROW)[:, :, 0:HD],
                                     t["L1_gnn_W_fc"][c * P:(c + 1) * P, :].rearrange("p (h d) -> p h d", d=HD)).then_inc(attn_in.h, 16)
                    for j, name in enumerate(("attn_h", "attn_t")):
                        sp.dma_start(attn[:, j, :], t[f"L1_gnn_{name}"].rearrange("(a h) d -> a (h d)", a=1).to_broadcast([P, F])).then_inc(attn_in.h, 16)
                    for d, k in node_tiles(sp):
                        sp.wait_ge(ft_ready.h, d + 1)
                        sp.dma_start(attn_table[bass.ds(d * P, P), :], stage2[:, k, :]).then_inc(ft_out[k].h, 16)
                    sp.wait_ge(ft_out[0].h, 16 * (NT // 2 + 1))
                    sp.wait_ge(ft_out[1].h, 16 * (NT // 2))

                @block.gpsimd
                def _(g):
                    for d, k in node_tiles(g):
                        g.wait_ge(y_used.h, d + 1)
                        g.tensor_copy(idx[:, k, 0:2], slots[:, :, bass.ds(d, 1)].rearrange("p a d -> p (a d)")).then_inc(slot_idx.h, 1)
                        g.wait_ge(slot_idx.h, d + 1)
                        g.tensor_tensor(carrier[:], psrc[:, 0:1], psrc[:, 0:1], ALU.add)
                        for j in range(2):
                            g.indirect_dma_start(expert_rows[:, k, j, :], None, slot_out,
                                                 bass.IndirectOffsetOnAxis(ap=idx[:, k, j:j + 1], axis=0)).then_inc(y_in[k].h, 16)

                @block.vector
                def _(v):
                    v.sem_inc(y_used.h, 2)
                    v.wait_ge(attn_in.h, 16 * (FC + 2))
                    for c in range(FC):
                        heads = wcat[:, c, 0:HCOLS].rearrange("p (h d) -> p h d", d=HROW)
                        for j, dst in enumerate((heads[:, :, HD], wcat[:, c, HCOLS:WCOLS])):
                            v.tensor_tensor(prod[:].rearrange("p (h d) -> p h d", d=HD), heads[:, :, 0:HD], attn[:, j, :].rearrange("p (h d) -> p h d", d=HD), ALU.mult).then_inc(v_step.h, 1)
                            v.wait_ge(v_step.h, v_step.next())
                            v.tensor_reduce(dst, prod[:].rearrange("p (h d) -> p h d", d=HD), AX.X, ALU.add).then_inc(v_step.h, 1)
                            v.wait_ge(v_step.h, v_step.next())
                    v.nop().then_inc(wcat_ready.h, 1)
                    v.wait_ge(x_loaded.h, x_loaded.base + 16)
                    part_now = [0]

                    def add_experts(d, k):
                        v.wait_ge(y_in[k].h, 32 * (d // 2 + 1) if isinstance(d, int) else (d - k) * 16 + 32)
                        row = rows_of(acc, d)
                        v.scalar_tensor_tensor(row, expert_rows[:, k, 0, :], gate[:, 0, bass.ds(d, 1)], row, ALU.mult, ALU.add).then_inc(y_first.h, 1)
                        v.wait_ge(y_first.h, d + 1)
                        v.scalar_tensor_tensor(row, expert_rows[:, k, 1, :], gate[:, 1, bass.ds(d, 1)], row, ALU.mult, ALU.add).then_inc(y_used.h, 1)

                    def close_part(part):
                        lo, hi = PARTS[part]
                        part_now[0] = part
                        if part == 0:
                            for d, k in node_tiles(v, lo, hi):
                                add_experts(d, k)
                        for d in range(lo + PART, hi):
                            add_experts(d, d % 2)
                        v.wait_ge(y_used.h, hi + 2)
                        norm.stats_of(v, acc, part)

                    def stage_rows(d, k):
                        v.wait_ge(turned.h, turned.base + d + 1)
                        norm.rows(v, acc, stage[:, k, :], d, rows_ready)
                        if part_now[0] < len(PARTS) - 1:
                            add_experts(d + PART, k)

                    def keep(d, k):
                        v.wait_ge(projected.h, projected.base + d + 1 + 2)
                        wait_earlier(v, ft_out[k], d, k, 16)
                        v.tensor_copy(rows_of(node_terms, d), ps[2 + k][:, HCOLS:WCOLS])
                        v.tensor_copy(stage2[:, k, :], ps[2 + k][:, 0:HCOLS]).then_inc(projected_out.h, 1)
                        v.wait_ge(projected_out.h, projected_out.base + d + 1 + 2)
                        v.nop().then_inc(ft_ready.h, 1)

                    two_ahead(v, stage_rows, keep, close_part)

                @block.scalar
                def _(a):
                    turned_to_lhs(a, norm)

                @block.tensor
                def _(pe):
                    pe.wait_ge(wcat_ready.h, 1)
                    turn_and_multiply(pe, wcat, rows_ready, WCOLS)
            x_loaded.base += 16
            project_counted()
            stored.base -= 16 * NT

    with ExitStack() as proj:
        stage = sb("stage", [P, 2, F], F32, proj)
        lhs = sb("lhs", [P, 2, FC, P], F32, proj)
        combine()

    QUADS = NPAIR // (4 * G)
    GROUPS = 4 * QUADS
    assert GROUPS * G == NPAIR
    lateb = ExitStack()
    sums = sb("sums", [P, NT, HCOLS], F32, lateb)

    def attend():
        with ExitStack() as ctx:
            rows = sb("rows", [P, 4, G, HCOLS], F32, ctx)
            hot = sb("hot", [P, 4, G, P], F32, ctx)
            hot_b = sb("hot_b", [P, 4, G, P], BF16, ctx)
            hot_t = sb("hot_t", [P, 2, G, P], BF16, ctx)
            spread = sb("spread", [P, 16, G * HEADS], BF16, ctx)
            spread_i = sb("spread_i", [P, G * HEADS], I32, ctx)
            spread_f = sb("spread_f", [P, G * HEADS], F32, ctx)
            lane_i = sb("lane_i", [P, 16], I32, ctx)
            lane = sb("lane", [P, 16], F32, ctx)
            edge_terms = sb("edge_terms", [P, 4, G, HEADS], F32, ctx)
            terms = sb("terms", [P, G, HEADS], F32, ctx)
            total = sb("total", [P, G, HEADS], F32, ctx)
            logit = sb("logit", [P, 2, 2 * G, HEADS], F32, ctx)
            ident_b = sb("ident_b", [P, P], BF16, ctx)
            starts = sb("starts", [G * HEADS, P], F32, ctx)
            runmax = sb("runmax", [P, P], F32, ctx)
            cand = sb("cand", [P, 3, G, HEADS + 1], F32, ctx)
            node_rest = sb("node_rest", [P, 2, NT, HEADS], F32, ctx)
            node_parts = sb("node_parts", [P, NT, 3, HEADS], BF16, ctx)
            dst_terms = sb("dst_terms", [P, G, HEADS], F32, ctx)
            run_best = sb("run_best", [P, G, HEADS], F32, ctx)
            edge_peak = sb("edge_peak", [P, G, HEADS], F32, ctx)
            unmet = sb("unmet", [P, G], F32, ctx)
            best = sb("best", [P, HEADS, G + 1], F32, ctx)
            upto = sb("upto", [P, HEADS, G + 1], F32, ctx)
            peak = sb("peak", [P, 3, HEADS, G + 1], F32, ctx)
            changes = sb("changes", [P, HEADS * (G + 1) + 1], F32, ctx)
            below = sb("below", [P, G, HEADS], F32, ctx)
            below_pos = sb("below_pos", [P, G, HEADS], F32, ctx)
            growth = sb("growth", [P, HEADS], F32, ctx)
            shrink = sb("shrink", [P, HEADS], F32, ctx)
            edge_terms_in = [sem(f"edge_terms_in{u}") for u in range(4)]
            terms_used = sem("terms_used")
            changes_free, changes_set = sem("changes_free"), sem("changes_set")
            rows_in = [sem(f"rows_in{u}") for u in range(4)]
            rows_used, patterns, patterns_set = sem("rows_used"), sem("patterns"), sem("patterns_set")
            marked, mark_step, marks_turned, marks_kept = sem("marked"), sem("mark_step"), sem("marks_turned"), sem("marks_kept")
            starts_spread, starts_kept, terms_spread = sem("starts_spread"), sem("starts_kept"), sem("terms_spread")
            logit_set, logit_turned, scanned, run_turned = sem("logit_set"), sem("logit_turned"), sem("run_scanned"), sem("run_turned")
            cand_set, met, peaked, peak_spread = sem("cand_set"), sem("met"), sem("peaked"), sem("peak_spread")
            below_ready, weighed, weigh_step = sem("below_ready"), sem("weighed"), sem("weigh_step")
            growth_ready, shrink_ready = sem("growth_ready"), sem("shrink_ready")
            messages_ready, summed, sums_added = sem("messages_ready"), sem("pair_summed"), sem("sums_added")

            def steps(begin, both, last):

                def run(eng):
                    begin()
                    with eng.Fori(0, QUADS - 1) as i:
                        for u in range(4):
                            both(4 * i + u, u)
                    for q in range(GROUPS - 4, GROUPS - 1):
                        both(q, q % 4)
                    last(GROUPS - 1, (GROUPS - 1) % 4)

                return run

            def upper(a):
                return a.bitcast(BF16)[:, :, :, 1::2]

            def there(n):
                return not isinstance(n, int) or n < GROUPS

            with nc.Block() as block:
                @block.sync
                def _(sp):
                    with sp.Fori(0, QUADS) as i:
                        for u in range(4):
                            sp.wait_ge(terms_used.h, 4 * i + u + 1)
                            sp.dma_start(edge_terms[:, u].rearrange("p j e -> p (j e)"), ee_table[:, bass.ds((4 * i + u) * G * HEADS, G * HEADS)]).then_inc(edge_terms_in[u].h, 16)

                @block.gpsimd
                def _(g):
                    g.iota(spread_i[:], [[1, G], [0, HEADS]], base=0, channel_multiplier=0).then_inc(patterns.h, 1)
                    g.iota(lane_i[:], [[-G, 16]], base=0, channel_multiplier=1).then_inc(patterns.h, 1)
                    with g.Fori(0, QUADS) as i:
                        for u in range(4):
                            q = 4 * i + u
                            g.wait_ge(rows_used.h, q + 1)
                            g.tensor_copy(idx[:, u, :], psrc[:, bass.ds(q * G, G)]).then_inc(idx_ready.h, 1)
                            g.wait_ge(idx_ready.h, idx_ready.base + q + 1)
                            g.tensor_tensor(carrier[:], psrc[:, 0:1], psrc[:, 0:1], ALU.add)
                            for b in range(G):
                                g.indirect_dma_start(rows[:, u, b, :], None, attn_table,
                                                     bass.IndirectOffsetOnAxis(ap=idx[:, u, b:b + 1], axis=0)).then_inc(rows_in[u].h, 16)

                @block.vector
                def _(v):
                    def heads(u):
                        return rows[:, u].rearrange("p j (e d) -> p j e d", d=HROW)

                    def logits_steps(n, turn, u):

                        def spread_sum():
                            v.wait_ge(terms_spread.h, n + 1)
                            v.tensor_reduce(dst_terms[:], ps[0][:, 2 * P:2 * P + 3 * G * HEADS].rearrange("p (j k e) -> p j e k", k=3, e=HEADS), AX.X, ALU.add)

                        def known_terms():
                            v.wait_ge(edge_terms_in[u].h, 16 * (turn + 1))
                            v.tensor_tensor(terms[:], edge_terms[:, u], dst_terms[:], ALU.add).then_inc(terms_used.h, 1)

                        def all_terms():
                            v.wait_ge(rows_in[u].h, 16 * G * (turn + 1))
                            v.tensor_tensor(total[:], heads(u)[:, :, :, HD], terms[:], ALU.add)

                        def leaky():
                            v.scalar_tensor_tensor(logit[:, u % 2, 0:G, :], total[:], SLOPE, total[:], ALU.mult, ALU.max).then_inc(logit_set.h, 1)

                        return spread_sum, known_terms, all_terms, leaky

                    def logits(n, turn, u):
                        for step in logits_steps(n, turn, u):
                            step()
                            v.drain()

                    def run_maxima(n):
                        v.wait_ge(logit_turned.h, n + 1)
                        v.tensor_tensor_scan(runmax[0:G * HEADS, :], starts[:], ps[0][0:G * HEADS, 0:P], -BIG, ALU.add, ALU.max).then_inc(scanned.h, 1)

                    def candidates(n, beside):
                        last = plast[:, bass.ds(n * G, G)].rearrange("p (j a) -> p j a", a=1)
                        v.tensor_copy(cand[:, 0, :, HEADS:HEADS + 1], last)
                        v.wait_ge(run_turned.h, n + 1)
                        v.tensor_tensor(cand[:, 0, :, 0:HEADS], ps[1][:, 0:G * HEADS].rearrange("p (j e) -> p j e", e=HEADS),
                                        last.to_broadcast([P, G, HEADS]), ALU.mult)
                        beside[0]()
                        v.drain()
                        v.tensor_tensor(cand[:, 1], cand[:, 0], upper(cand[:])[:, 0], ALU.subtract)
                        beside[1]()
                        v.drain()
                        v.tensor_tensor(cand[:, 2], cand[:, 1], upper(cand[:])[:, 1], ALU.subtract).then_inc(cand_set.h, 1)
                        beside[2]()

                    def node_maxima(n, beside):
                        v.drain()
                        v.tensor_copy(best[:, :, 0:1], upto[:, :, G:G + 1])
                        v.wait_ge(met.h, n + 1)
                        got = ps[1][:, P:P + 3 * G * (HEADS + 1)].rearrange("p (j k e) -> p j e k", k=3, e=HEADS + 1)
                        v.tensor_reduce(run_best[:], got[:, :, 0:HEADS, :], AX.X, ALU.add)
                        v.tensor_scalar(unmet[:].rearrange("p (j a) -> p j a", a=1), got[:, :, HEADS:HEADS + 1, 0], BIG, -BIG, ALU.mult, ALU.add)
                        beside[0]()
                        v.drain()
                        v.tensor_tensor(best[:, :, 1:G + 1].rearrange("p e j -> p j e"), run_best[:],
                                        unmet[:].rearrange("p (j a) -> p j a", a=1).to_broadcast([P, G, HEADS]), ALU.add)
                        beside[1]()
                        v.drain()
                        v.wait_ge(changes_set.h, n + 1)
                        flat = HEADS * (G + 1)
                        up = upto[:].rearrange("p e j -> p (e j)")
                        v.tensor_tensor_scan(up, changes[:, 0:flat], best[:].rearrange("p e j -> p (e j)"), -BIG, ALU.add, ALU.max)
                        beside[2]()
                        v.drain()
                        v.tensor_tensor_scan(peak[:, 0].rearrange("p e j -> p (e j)")[:, ::-1], changes[:, flat:0:-1], up[:, ::-1], -BIG, ALU.add, ALU.max)
                        beside[3]()
                        for k in range(2):
                            v.drain()
                            op = v.tensor_tensor(peak[:, k + 1], peak[:, k], upper(peak[:])[:, k], ALU.subtract)
                        op.then_inc(peaked.h, 1)
                        v.scalar_tensor_tensor(growth[:], best[:, :, 0], rows_of(change, n)[:, 1:2], peak[:, 0, :, 1], ALU.add, ALU.subtract).then_inc(growth_ready.h, 1)

                    def distances(n, u):
                        v.wait_ge(peak_spread.h, n + 1)
                        v.tensor_reduce(edge_peak[:], ps[2][:, 0:3 * G * HEADS].rearrange("p (j k e) -> p j e k", k=3, e=HEADS), AX.X, ALU.add)
                        v.drain()
                        v.tensor_tensor(below[:], edge_peak[:], logit[:, u % 2, 0:G, :], ALU.subtract).then_inc(below_ready.h, 1)

                    def messages(q, u, half):
                        if half == 0:
                            v.wait_ge(weighed.h, q + 1)
                        m = heads(u)[:, 4 * half:4 * half + 4]
                        v.tensor_tensor(m[:, :, :, 0:HD], m[:, :, :, 0:HD], m[:, :, :, HD:HROW].to_broadcast([P, 4, HEADS, HD]), ALU.mult).then_inc(messages_ready.h, 1)

                    def sums_rows(q):
                        tiles = node_tiles_of(v, q)
                        for d in tiles:
                            v.lower_ap(rows_of(sums, d))
                        return tiles

                    def shrink_sums(q, tiles):
                        row = rows_of(sums, tiles[0]).rearrange("p (e d) -> p e d", d=HROW)
                        v.wait_ge(shrink_ready.h, q + 1)
                        v.tensor_tensor(row, row, shrink[:].rearrange("p (e a) -> p e a", a=1).to_broadcast([P, HEADS, HROW]), ALU.mult)

                    def add_sum(q, tiles, b):
                        row = rows_of(sums, tiles[b])
                        if b % 2 == 0:
                            v.wait_ge(summed.h, 4 * q + b // 2 + 1)
                        op = v.tensor_tensor(row, row, ps[4 + b % 4][:, 0:HCOLS], ALU.add)
                        if b % 2:
                            op.then_inc(sums_added.h, 1)

                    def add_sums(q, tiles, pairs):
                        for b in pairs:
                            v.drain()
                            add_sum(q, tiles, b)

                    v.sem_inc(rows_used.h, 4)
                    v.sem_inc(terms_used.h, 4)
                    v.sem_inc(sums_added.h, 2)
                    v.memset(logit[:, :, G:2 * G, :], 0.0)
                    v.tensor_copy(ident_b[:], ident[:])
                    v.memset(runmax[G * HEADS:P, :], 0.0)
                    v.memset(upto[:], -BIG)
                    v.memset(changes[:], -BIG).then_inc(changes_free.h, 1)
                    v.memset(sums[:], 0.0)
                    rest = node_terms[:]
                    for k in range(3):
                        v.tensor_copy(node_parts[:, :, k, :], rest.bitcast(BF16)[:, :, 1::2]).then_inc(v_step.h, 1)
                        v.wait_ge(v_step.h, v_step.next())
                        if k < 2:
                            v.tensor_tensor(node_rest[:, k], rest, rest.bitcast(BF16)[:, :, 1::2], ALU.subtract).then_inc(v_step.h, 1)
                            v.wait_ge(v_step.h, v_step.next())
                            rest = node_rest[:, k]
                    v.wait_ge(patterns.h, 2)
                    v.tensor_copy(spread_f[:], spread_i[:]).then_inc(v_step.h, 1)
                    v.wait_ge(v_step.h, v_step.next())
                    v.tensor_copy(lane[:], lane_i[:]).then_inc(v_step.h, 1)
                    v.wait_ge(v_step.h, v_step.next())
                    v.tensor_tensor(spread[:], spread_f[:].rearrange("p (g m) -> p g m", g=1).to_broadcast([P, 16, G * HEADS]),
                                    lane[:].rearrange("p (g m) -> p g m", m=1).to_broadcast([P, 16, G * HEADS]), ALU.is_equal).then_inc(patterns_set.h, 1)

                    def nothing():
                        pass

                    def begin():
                        logits(0, 0, 0)
                        run_maxima(0)
                        candidates(0, [nothing] * 3)
                        node_maxima(0, logits_steps(1, 0, 1))
                        v.drain()
                        distances(0, 0)
                        run_maxima(1)

                    def turn_of(q, u, k):
                        return (q + k - (u + k) % 4) // 4

                    def both(q, u):
                        n, un, u2 = q + 1, (u + 1) % 4, (u + 2) % 4
                        messages(q, u, 0)
                        messages(q, u, 1)
                        tiles = sums_rows(q)
                        v.drain()
                        candidates(n, (lambda: shrink_sums(q, tiles), lambda: add_sum(q, tiles, 0), nothing))
                        add_sums(q, tiles, (1, 2, 3))
                        node_maxima(n, logits_steps(n + 1, turn_of(q, u, 2), u2) if there(n + 1) else [nothing] * 4)
                        add_sums(q, tiles, (4, 5))
                        distances(n, un)
                        if there(n + 1):
                            run_maxima(n + 1)
                        add_sums(q, tiles, (6, 7))

                    def last(q, u):
                        messages(q, u, 0)
                        messages(q, u, 1)
                        tiles = sums_rows(q)
                        v.drain()
                        shrink_sums(q, tiles)
                        add_sums(q, tiles, range(8))

                    steps(begin, both, last)(v)

                @block.scalar
                def _(a):
                    def mark(n, u):
                        for b in range(G):
                            op = a.activation(hot[:, u, b, :], iota_f[:], ACT.Abs, bias=pdl[:, bass.ds(n * G + b, 1)], scale=-1.0)
                        op.then_inc(mark_step.h, 1)
                        a.wait_ge(mark_step.h, n + 1)
                        a.activation(hot_b[:, u], hot[:, u], ACT.Relu, bias=ones[:, 0:1], scale=-1.0)
                        a.activation(hot[:, u], hot[:, u], ACT.Relu, bias=ones[:, 0:1], scale=-1.0).then_inc(marked.h, 1)

                    def keep_marks(n, u):
                        a.wait_ge(marks_turned.h, n + 1)
                        a.activation(hot_t[:, u % 2].rearrange("p b n -> p (b n)"), ps[3][:].bitcast(BF16), ACT.Copy).then_inc(marks_kept.h, 1)

                    def keep_starts(n):
                        a.wait_ge(starts_spread.h, n + 1)
                        a.activation(starts[:], ps[0][0:G * HEADS, P:2 * P], ACT.Copy).then_inc(starts_kept.h, 1)

                    def weigh(n, u):
                        a.wait_ge(growth_ready.h, n + 1)
                        a.activation(shrink[:], growth[:], ACT.Exp).then_inc(shrink_ready.h, 1)
                        a.wait_ge(below_ready.h, n + 1)
                        a.activation(below_pos[:], below[:], ACT.Relu).then_inc(weigh_step.h, 1)
                        a.wait_ge(weigh_step.h, n + 1)
                        a.activation(rows[:, u].rearrange("p j (e d) -> p j e d", d=HROW)[:, :, :, HD], below_pos[:], ACT.Exp, scale=-1.0).then_inc(weighed.h, 1)

                    def expand_changes(n):
                        if isinstance(n, int) and n == 0:
                            a.wait_ge(changes_free.h, 1)
                        else:
                            a.wait_ge(peaked.h, n)
                        a.activation(changes[:, 0:HEADS * (G + 1)].rearrange("p (e j) -> p e j", j=G + 1),
                                     change[:, bass.ds(n, 1), :].to_broadcast([P, HEADS, G + 1]), ACT.Copy).then_inc(changes_set.h, 1)

                    def chain(n, u):
                        if there(n + 1):
                            keep_marks(n + 1, (u + 1) % 4)
                            keep_starts(n + 1)
                        if there(n + 2):
                            mark(n + 2, (u + 2) % 4)
                        weigh(n, u)
                        if there(n + 1):
                            expand_changes(n + 1)

                    def begin():
                        expand_changes(0)
                        keep_starts(0)
                        mark(0, 0)
                        mark(1, 1)
                        keep_marks(0, 0)
                        chain(0, 0)

                    steps(begin, lambda q, u: chain(q + 1, (u + 1) % 4), lambda q, u: None)(a)

                @block.tensor
                def _(pe):
                    def spread_starts(n):
                        if not isinstance(n, int) or n > 0:
                            pe.wait_ge(scanned.h, n)
                        pe.matmul(ps[0][0:G * HEADS, P:2 * P], spread[:, bass.ds(n % 16, 1), :].rearrange("p a m -> p (a m)"),
                                  run_start[:, bass.ds(n // 16, 1), :].rearrange("p a m -> p (a m)"), start=True, stop=True).then_inc(starts_spread.h, 1)

                    def turn_logits(n, u):
                        pe.wait_ge(logit_set.h, n + 1)
                        pe.transpose(ps[0][:, 0:P], logit[:, u % 2].rearrange("p j e -> p (j e)"), ident[:]).then_inc(logit_turned.h, 1)

                    turned_marks = ps[3][:].bitcast(BF16)

                    def turn_marks(n, u):
                        pe.wait_ge(marked.h, n + 1)
                        if not isinstance(n, int) or n > 0:
                            pe.wait_ge(marks_kept.h, n)
                        for b in range(G):
                            mm = pe.transpose(turned_marks[:, b * P:(b + 1) * P], hot_b[:, u, b, :], ident_b[:])
                        mm.then_inc(marks_turned.h, 1)

                    def spread_terms(n, u):
                        tiles = node_tiles_of(pe, n)
                        pe.wait_ge(marks_kept.h, n + 1)
                        pe.wait_ge(starts_kept.h, n + 1)
                        for b in range(G):
                            mm = pe.matmul(ps[0][:, 2 * P + 3 * b * HEADS:2 * P + 3 * (b + 1) * HEADS], hot_t[:, u % 2, b, :],
                                           node_parts[:, bass.ds(tiles[b], 1)].rearrange("p a k e -> p (a k e)"), start=True, stop=True)
                        mm.then_inc(terms_spread.h, 1)

                    def turn_runs(n):
                        pe.wait_ge(scanned.h, n + 1)
                        pe.transpose(ps[1][:, 0:P], runmax[:], ident[:]).then_inc(run_turned.h, 1)

                    def meet(n, u):
                        pe.wait_ge(cand_set.h, n + 1)
                        for b in range(G):
                            mm = pe.matmul(ps[1][:, P + 3 * b * (HEADS + 1):P + 3 * (b + 1) * (HEADS + 1)].rearrange("p (k e) -> p k e", k=3),
                                           hot_b[:, u, b, :], upper(cand[:])[:, :, b, :], start=True, stop=True)
                        mm.then_inc(met.h, 1)

                    def spread_peaks(n, u):
                        pe.wait_ge(peaked.h, n + 1)
                        for b in range(G):
                            mm = pe.matmul(ps[2][:, 3 * b * HEADS:3 * (b + 1) * HEADS].rearrange("p (k e) -> p k e", k=3),
                                           hot_t[:, u % 2, b, :], upper(peak[:])[:, :, :, b + 1], start=True, stop=True)
                        mm.then_inc(peak_spread.h, 1)

                    def sum_pairs(q, u, pairs):
                        for b in pairs:
                            if b % 4 == 0:
                                pe.wait_ge(messages_ready.h, 2 * q + b // 4 + 1)
                            if b % 2 == 0:
                                pe.wait_ge(sums_added.h, 4 * q + b // 2 + 1)
                            mm = pe.matmul(ps[4 + b % 4][:, 0:HCOLS], hot[:, u, b, :], rows[:, u, b, :], start=True, stop=True)
                            if b % 2:
                                mm.then_inc(summed.h, 1)

                    def release(q):
                        pe.wait_ge(summed.h, 4 * q + 4)
                        pe.sem_inc(rows_used.h, 1)

                    def begin():
                        pe.wait_ge(patterns_set.h, 1)
                        spread_starts(0)
                        turn_marks(0, 0)
                        spread_terms(0, 0)
                        turn_logits(0, 0)
                        turn_marks(1, 1)
                        turn_runs(0)
                        spread_starts(1)
                        spread_terms(1, 1)
                        meet(0, 0)
                        spread_peaks(0, 0)
                        turn_logits(1, 1)

                    def both(q, u):
                        n, un, u2 = q + 1, (u + 1) % 4, (u + 2) % 4
                        if there(n + 1):
                            turn_marks(n + 1, u2)
                        turn_runs(n)
                        if there(n + 1):
                            spread_starts(n + 1)
                        sum_pairs(q, u, range(4))
                        if there(n + 1):
                            spread_terms(n + 1, u2)
                        meet(n, un)
                        sum_pairs(q, u, (4, 5))
                        spread_peaks(n, un)
                        if there(n + 1):
                            turn_logits(n + 1, u2)
                        sum_pairs(q, u, (6, 7))
                        release(q)

                    def last(q, u):
                        sum_pairs(q, u, range(8))

                    steps(begin, both, last)(pe)
            idx_ready.base += GROUPS

    attend()

    ONE = NT // 7
    BW = ONE * P
    HALF = BW // 2
    TAKE = N // 2 - 1
    assert NT % 7 == 0

    def close_attention():
        with ExitStack() as ctx:
            den = sb("den", [P, NT, HEADS], F32, ctx)
            bias = sb("gat_bias", [P, F], F32, ctx)
            with nc.Block() as block:
                @block.sync
                def _(sp):
                    sp.dma_start(bias[:], t["L1_gnn_bias"].rearrange("(a h) d -> a (h d)", a=1).to_broadcast([P, F])).then_inc(loaded.h, 16)

                @block.vector
                def _(v):
                    v.tensor_scalar(den[:], sums[:].rearrange("p t (h d) -> p t h d", d=HROW)[:, :, :, HD], 1.0 / BIG, None, ALU.max).then_inc(v_step.h, 1)
                    v.wait_ge(v_step.h, v_step.next())
                    v.reciprocal(den[:], den[:]).then_inc(v_step.h, 1)
                    v.wait_ge(v_step.h, v_step.next())
                    v.wait_ge(loaded.h, loaded.base + 16)
                    features = sums[:].rearrange("p t (h d) -> p t h d", d=HROW)[:, :, :, 0:HD]
                    rows = acc[:].rearrange("p t (h d) -> p t h d", d=HD)
                    v.tensor_tensor(features, features, den[:].rearrange("p t (h b) -> p t h b", b=1).to_broadcast([P, NT, HEADS, HD]), ALU.mult).then_inc(v_step.h, 1)
                    v.wait_ge(v_step.h, v_step.next())
                    v.tensor_tensor(rows, rows, features, ALU.add).then_inc(v_step.h, 1)
                    v.wait_ge(v_step.h, v_step.next())
                    v.tensor_tensor(acc[:], acc[:], bias[:].rearrange("p (t f) -> p t f", t=1).to_broadcast([P, NT, F]), ALU.add).then_inc(v_step.h, 1)
                    v.wait_ge(v_step.h, v_step.next())
            loaded.base += 16

    close_attention()
    lateb.close()

    zt = sb("zt", [P, FC, NPAD], F32, bigs)

    KTH_BITS = (12, 8, 4, 0)
    TRIALS = 15

    def feed_forward():
        with ExitStack() as ctx:
            norm = NodeNorm(ctx, "ln3", PARTS)
            stage = sb("stage", [P, 2, F], F32, ctx)
            wr = sb("wr3", [P, FC, 1], F32, ctx)
            br = sb("br3", [P, 1], F32, ctx)
            w1 = sb("w1_3", [P, FC, HID], F32, ctx)
            b1 = sb("b1_3", [P, HC], F32, ctx)
            w2 = sb("w2_3", [P, HC, F], F32, ctx)
            b2 = sb("b2_3", [P, F], F32, ctx)
            hid = sb("hid3", [P, HC, BW], F32, ctx)
            part = sb("part3", [P, 2, F], F32, ctx)
            weight = sb("weight", [P, NT], F32, ctx)
            key = sb("key", [P, NT], I32, ctx)
            sign = sb("sign", [P, NT], I32, ctx)
            half_i = sb("half_i", [P, 2, NT], I32, ctx)
            half = sb("half", [P, 2, NT], F32, ctx)
            node_i = sb("node3_i", [P, NT], I32, ctx)
            valid = sb("valid3", [P, NT], F32, ctx)
            junk = sb("junk3", [P, NT], F32, ctx)
            count = sb("count3", [P, 1], F32, ctx)
            cut = sb("cut", [P, 1], F32, ctx)
            trials = sb("trials", [P, TRIALS], F32, ctx)
            reached = sb("reached", [P, TRIALS, NT], F32, ctx)
            counts = sb("counts", [P, TRIALS], F32, ctx)
            reach = sb("reach", [P, 1], F32, ctx)
            quota = sb("quota", [P, 2], F32, ctx)
            above = sb("above", [P, NT], F32, ctx)
            ties = sb("ties", [P, NT], F32, ctx)
            runs = sb("runs", [P, NT], F32, ctx)
            taken = sb("taken", [P, NT], F32, ctx)
            rows_ready, zt_set, weights_in, numbered = sem("z3_staged"), sem("zt_set"), sem("weights_in"), sem("numbered3")
            routed, counted, summed = sem("routed"), sem("counted3"), sem("count_summed")
            up_done, up_act, down_done, part_set, out_set = sem("up_done"), sem("up_act"), sem("down_done"), sem("part_set"), sem("out_set")
            scaled, freed = sem("scaled"), sem("hid_freed")
            with nc.Block() as block:
                @block.sync
                def _(sp):
                    for c in range(FC):
                        sp.dma_start(wr[:, c, :], t["L1_ffn_wr"][c * P:(c + 1) * P, :]).then_inc(weights_in.h, 16)
                    sp.dma_start(br[:], t["L1_ffn_br"].rearrange("(a e) -> a e", a=1).to_broadcast([P, 1])).then_inc(weights_in.h, 16)
                    sp.dma_start(w1[:], t["L1_ffn_w1"].rearrange("(c p) n -> p c n", p=P)).then_inc(weights_in.h, 16)
                    with nc.allow_non_contiguous_dma("bias of the hidden units onto partitions"):
                        sp.dma_start(b1[:], t["L1_ffn_b1"].rearrange("(c p) -> p c", p=P)).then_inc(weights_in.h, 16)
                    sp.dma_start(w2[:], t["L1_ffn_w2"].rearrange("(c p) n -> p c n", p=P)).then_inc(weights_in.h, 16)
                    sp.dma_start(b2[:], t["L1_ffn_b2"].rearrange("(a n) -> a n", a=1).to_broadcast([P, F])).then_inc(weights_in.h, 16)
                    with sp.Fori(0, NT - 1) as d:
                        sp.wait_ge(out_set.h, d + 2)
                        sp.dma_start(out[bass.ds(d * P, P), :], rows_of(acc, d)).then_inc(stored.h, 16)
                    sp.wait_ge(out_set.h, NT + 1)
                    sp.dma_start(out[(NT - 1) * P:N, :], acc[0:NLAST, NT - 1, :]).then_inc(stored.h, 16)
                    sp.wait_ge(stored.h, stored.base + 16 * NT)

                @block.gpsimd
                def _(g):
                    g.iota(node_i[:], [[P, NT]], base=0, channel_multiplier=1).then_inc(numbered.h, 1)

                @block.vector
                def _(v):
                    v.sem_inc(part_set.h, 2)
                    v.sem_inc(out_set.h, 1)

                    def stage_rows(d, k):
                        v.wait_ge(turned.h, turned.base + d + 1)
                        norm.rows(v, acc, stage[:, k, :], d, rows_ready)
                        v.wait_ge(rows_ready.h, d + 1)
                        v.tensor_tensor(rows_of(acc, d), rows_of(acc, d), stage[:, k, :], ALU.add).then_inc(scaled.h, 1)

                    for n, (lo, hi) in enumerate(PARTS):
                        norm.stats_of(v, acc, n)
                        for d, k in node_tiles(v, lo, hi):
                            stage_rows(d, k)
                    v.wait_ge(numbered.h, 1)
                    v.tensor_copy(junk[:], node_i[:]).then_inc(v_step.h, 1)
                    v.wait_ge(v_step.h, v_step.next())
                    v.tensor_scalar(valid[:], junk[:], float(N), None, ALU.is_lt).then_inc(v_step.h, 1)
                    v.wait_ge(v_step.h, v_step.next())
                    v.wait_ge(routed.h, 1)
                    v.tensor_scalar(weight[:], ps[2][:, 0:NT], br[:], 0.0, ALU.add, ALU.add).then_inc(v_step.h, 1)
                    v.wait_ge(v_step.h, v_step.next())
                    bits = weight[:].bitcast(I32)
                    v.tensor_scalar(sign[:], bits, 31, None, ALU.arith_shift_right).then_inc(v_step.h, 1)
                    v.wait_ge(v_step.h, v_step.next())
                    v.tensor_scalar(sign[:], sign[:], -(1 << 31), None, ALU.bitwise_or).then_inc(v_step.h, 1)
                    v.wait_ge(v_step.h, v_step.next())
                    v.tensor_tensor(key[:], bits, sign[:], ALU.bitwise_xor).then_inc(v_step.h, 1)
                    v.wait_ge(v_step.h, v_step.next())
                    v.tensor_scalar(half_i[:, 0, :], key[:], 16, 0xFFFF, ALU.arith_shift_right, ALU.bitwise_and).then_inc(v_step.h, 1)
                    v.wait_ge(v_step.h, v_step.next())
                    v.tensor_scalar(half_i[:, 1, :], key[:], 0xFFFF, None, ALU.bitwise_and).then_inc(v_step.h, 1)
                    v.wait_ge(v_step.h, v_step.next())
                    v.tensor_copy(half[:], half_i[:]).then_inc(v_step.h, 1)
                    v.wait_ge(v_step.h, v_step.next())

                    def masked(x, mask):
                        v.scalar_tensor_tensor(x, x, 1.0, mask, ALU.add, ALU.mult).then_inc(v_step.h, 1)
                        v.wait_ge(v_step.h, v_step.next())
                        v.tensor_scalar(x, x, -1.0, None, ALU.add).then_inc(v_step.h, 1)
                        v.wait_ge(v_step.h, v_step.next())

                    calls = [0]

                    def total(x, op, bound):
                        v.tensor_scalar(junk[:], x, bound, 0.0, op, ALU.add, accum_out=count[:]).then_inc(v_step.h, 1)
                        v.wait_ge(v_step.h, v_step.next())
                        v.nop().then_inc(counted.h, 1)
                        calls[0] += 1
                        v.wait_ge(summed.h, calls[0])
                        return ps[3][:, 0:1]

                    def kth(x, goal):
                        v.memset(cut[:], 0.0).then_inc(v_step.h, 1)
                        v.wait_ge(v_step.h, v_step.next())
                        for low_bit in KTH_BITS:
                            unit = float(1 << low_bit)
                            v.tensor_scalar(trials[:], iota_f[:, 1:TRIALS + 1], unit, cut[:], ALU.mult, ALU.add).then_inc(v_step.h, 1)
                            v.wait_ge(v_step.h, v_step.next())
                            v.tensor_tensor(reached[:], x.rearrange("p (a d) -> p a d", a=1).to_broadcast([P, TRIALS, NT]),
                                            trials[:].rearrange("p (a d) -> p a d", d=1).to_broadcast([P, TRIALS, NT]), ALU.is_ge).then_inc(v_step.h, 1)
                            v.wait_ge(v_step.h, v_step.next())
                            v.tensor_reduce(counts[:], reached[:], AX.X, ALU.add).then_inc(counted.h, 1)
                            calls[0] += 1
                            v.wait_ge(summed.h, calls[0])
                            v.tensor_scalar(trials[:], ps[3][:, 0:TRIALS], goal, 0.0, ALU.is_ge, ALU.add, accum_out=reach[:]).then_inc(v_step.h, 1)
                            v.wait_ge(v_step.h, v_step.next())
                            v.scalar_tensor_tensor(cut[:], reach[:], unit, cut[:], ALU.mult, ALU.add).then_inc(v_step.h, 1)
                            v.wait_ge(v_step.h, v_step.next())

                    masked(half[:, 0, :], valid[:])
                    v.memset(quota[:], float(TAKE)).then_inc(v_step.h, 1)
                    v.wait_ge(v_step.h, v_step.next())
                    kth(half[:, 0, :], quota[:, 0:1])
                    n = total(half[:, 0, :], ALU.is_gt, cut[:])
                    v.tensor_tensor(quota[:, 1:2], quota[:, 0:1], n, ALU.subtract).then_inc(v_step.h, 1)
                    v.wait_ge(v_step.h, v_step.next())
                    v.tensor_scalar(above[:], half[:, 0, :], cut[:], None, ALU.is_gt).then_inc(v_step.h, 1)
                    v.wait_ge(v_step.h, v_step.next())
                    v.tensor_scalar(ties[:], half[:, 0, :], cut[:], None, ALU.is_equal).then_inc(v_step.h, 1)
                    v.wait_ge(v_step.h, v_step.next())
                    masked(half[:, 1, :], ties[:])
                    kth(half[:, 1, :], quota[:, 1:2])
                    n = total(half[:, 1, :], ALU.is_gt, cut[:])
                    v.tensor_tensor(quota[:, 1:2], quota[:, 1:2], n, ALU.subtract).then_inc(v_step.h, 1)
                    v.wait_ge(v_step.h, v_step.next())
                    v.tensor_scalar(junk[:], half[:, 1, :], cut[:], None, ALU.is_gt).then_inc(v_step.h, 1)
                    v.wait_ge(v_step.h, v_step.next())
                    v.tensor_tensor(above[:], above[:], junk[:], ALU.add).then_inc(v_step.h, 1)
                    v.wait_ge(v_step.h, v_step.next())
                    v.tensor_scalar(ties[:], half[:, 1, :], cut[:], None, ALU.is_equal).then_inc(v_step.h, 1)
                    v.wait_ge(v_step.h, v_step.next())
                    v.nop().then_inc(counted.h, 1)
                    calls[0] += 1
                    v.wait_ge(summed.h, calls[0])
                    v.tensor_copy(taken[:], ps[3][:, 64:64 + NT]).then_inc(v_step.h, 1)
                    v.wait_ge(v_step.h, v_step.next())
                    v.tensor_tensor_scan(runs[:], ones[:, 0:NT], taken[:], 0.0, ALU.mult, ALU.add).then_inc(v_step.h, 1)
                    v.wait_ge(v_step.h, v_step.next())
                    v.tensor_tensor(runs[:], runs[:], taken[:], ALU.subtract).then_inc(v_step.h, 1)
                    v.wait_ge(v_step.h, v_step.next())
                    v.tensor_tensor(runs[:], runs[:], ps[3][:, 0:NT], ALU.add).then_inc(v_step.h, 1)
                    v.wait_ge(v_step.h, v_step.next())
                    v.tensor_scalar(runs[:], runs[:], quota[:, 1:2], None, ALU.is_lt).then_inc(v_step.h, 1)
                    v.wait_ge(v_step.h, v_step.next())
                    v.tensor_tensor(ties[:], ties[:], runs[:], ALU.mult).then_inc(v_step.h, 1)
                    v.wait_ge(v_step.h, v_step.next())
                    v.tensor_tensor(taken[:], above[:], ties[:], ALU.add).then_inc(v_step.h, 1)
                    v.wait_ge(v_step.h, v_step.next())
                    v.tensor_tensor(weight[:], weight[:], taken[:], ALU.mult).then_inc(v_step.h, 1)
                    v.wait_ge(v_step.h, v_step.next())
                    v.wait_ge(scaled.h, NT)
                    with v.Fori(0, NT // ONE) as blk:
                        for j in range(ONE):
                            d = blk * ONE + j
                            k = j % 2
                            v.wait_ge(down_done.h, d + 1)
                            if j == 0:
                                v.wait_ge(out_set.h, d + 1)
                            v.tensor_tensor(part[:, k, :], ps[6 + k][:, 0:F], b2[:], ALU.add).then_inc(part_set.h, 1)
                            v.wait_ge(part_set.h, d + 1 + 2)
                            v.scalar_tensor_tensor(rows_of(acc, d), part[:, k, :], weight[:, bass.ds(d, 1)], rows_of(acc, d), ALU.mult, ALU.add).then_inc(out_set.h, 1)

                @block.scalar
                def _(a):
                    for (lo, hi), root in zip(norm.parts, norm.roots):
                        root.scalar(a)
                        for d, k in node_tiles(a, lo, hi):
                            a.wait_ge(turned.h, turned.base + d + 1 + 2)
                            a.activation(zt[:, :, bass.ds(d * P, P)], ps[k][:, 0:F].rearrange("p (c n) -> p c n", c=FC), ACT.Copy).then_inc(turned_out.h, 1)
                    a.wait_ge(weights_in.h, 16 * (5 + FC))
                    with a.Fori(0, NT // ONE) as blk:
                        a.wait_ge(freed.h, blk + 1)
                        for c in range(HC):
                            for j in range(2):
                                a.wait_ge(up_done.h, blk * 2 * HC + 2 * c + j + 1)
                                a.activation(hid[:, c, j * HALF:(j + 1) * HALF], ps[4 + j][:, 0:HALF], ACT.Gelu_apprx_tanh, bias=b1[:, c:c + 1]).then_inc(up_act.h, 1)

                @block.tensor
                def _(pe):
                    pe.sem_inc(freed.h, 1)
                    pe.sem_inc(up_act.h, 2)
                    pe.wait_ge(weights_in.h, 16 * (5 + FC))
                    for d in range(NT + 1):
                        if d < NT:
                            turn_staged(pe, stage, d, d % 2, rows_ready)
                        if d > 0:
                            pe.wait_ge(turned_out.h, turned_out.base + d + 2)
                            for c in range(FC):
                                mm = pe.matmul(ps[2][:, d - 1:d], zt[:, c, (d - 1) * P:d * P], wr[:, c, :], start=(c == 0), stop=(c == FC - 1))
                    mm.then_inc(routed.h, 1)
                    def up(blk, c, j):
                        pe.wait_ge(up_act.h, blk * 2 * HC + 2 * c + j + 1)
                        for f in range(FC):
                            mm = pe.matmul(ps[4 + j][:, 0:HALF], w1[:, f, c * P:(c + 1) * P], zt[:, f, bass.ds(blk * BW + j * HALF, HALF)], start=(f == 0), stop=(f == FC - 1))
                        mm.then_inc(up_done.h, 1)

                    def down(blk):
                        pe.wait_ge(up_act.h, (blk + 1) * 2 * HC + 2)
                        for j in range(ONE):
                            pe.wait_ge(part_set.h, blk * ONE + j + (2 if j == 0 else 1))
                            for c in range(HC):
                                mm = pe.matmul(ps[6 + j % 2][:, 0:F], hid[:, c, j * P:(j + 1) * P], w2[:, c, :], start=(c == 0), stop=(c == HC - 1))
                            mm.then_inc(down_done.h, 1)
                        pe.drain().then_inc(freed.h, 1)

                    def count_all(n):
                        rounds = len(KTH_BITS) + 1
                        pe.wait_ge(counted.h, n + 1)
                        if n == 2 * rounds:
                            pe.matmul(ps[3][:, 0:NT], excl[:], ties[:], start=True, stop=True)
                            pe.matmul(ps[3][:, 64:64 + NT], ones[:], ties[:], start=True, stop=True).then_inc(summed.h, 1)
                        elif n % rounds < rounds - 1:
                            pe.matmul(ps[3][:, 0:TRIALS], ones[:], counts[:], start=True, stop=True).then_inc(summed.h, 1)
                        else:
                            pe.matmul(ps[3][:, 0:1], ones[:], count[:], start=True, stop=True).then_inc(summed.h, 1)

                    calls = 2 * (len(KTH_BITS) + 1) + 1
                    for n in range(2 * HC):
                        up(0, n // 2, n % 2)
                        if n < calls:
                            count_all(n)
                    down(0)
                    with pe.Fori(1, NT // ONE) as blk:
                        for c in range(HC):
                            for j in range(2):
                                up(blk, c, j)
                        down(blk)
            turned.base += NT
            turned_out.base += NT
            stored.base += 16 * NT

    def turn_staged(pe, stage, d, k, rows_ready):
        pe.wait_ge(rows_ready.h, d + 1)
        pe.wait_ge(turned_out.h, turned_out.base + d + 1)
        for c in range(FC):
            mm = pe.transpose(ps[k][:, c * P:(c + 1) * P], stage[:, k, c * P:(c + 1) * P], ident[:])
        mm.then_inc(turned.h, 1)

    feed_forward()
    bigs.close()


_OUT = ((N, F), "float32")


def kernel(**inputs):
    import numpy as _np
    import concourse.bacc as _bacc
    from concourse import mybir as _mybir
    from concourse.bass_utils import run_bass_kernel_spmd as _run

    nc = _bacc.Bacc("TRN2", target_bir_lowering=False, num_devices=1)
    arrays, tensors = {}, {}
    for name, value in inputs.items():
        a = _np.ascontiguousarray(value)
        arrays[f"in_{name}_dram"] = a
        tensors[name] = nc.dram_tensor(f"in_{name}_dram", a.shape, _mybir.dt.from_np(a.dtype), kind="ExternalInput").ap()
    shape, dtype = _OUT
    out = nc.dram_tensor("out_0_dram", shape, _mybir.dt.from_np(_np.dtype(dtype)), kind="ExternalOutput").ap()
    build(nc, tensors, out)
    r = _run(nc, [arrays], core_ids=[0])
    return r.results[0]["out_0_dram"]
```
